# Optimizing a Trainium2 kernel written in Bass

```python
import numpy as np
import jax
import jax.numpy as jnp

def _softmax(x, axis=-1):
    return jax.nn.softmax(x, axis=axis)

def _gelu(x):
    return jax.nn.gelu(x, approximate=True)

def _silu(x):
    return jax.nn.silu(x)

def _sigmoid(x):
    return jax.nn.sigmoid(x)

def _layernorm(x, axis=-1, eps=1e-05):
    m = jnp.mean(x, axis=axis, keepdims=True)
    v = jnp.var(x, axis=axis, keepdims=True)
    return (x - m) / jnp.sqrt(v + eps)

def _scatter_add(tgt, idx, src, axis=0):
    return tgt.at[idx].add(src)

def _segment_sum(src, seg, n):
    return jax.ops.segment_sum(src, seg, n)
kernel_name = 'mk_xattn_seq_d2_seqx_r4_23e115'

def setup_inputs(seed: int=0):
    np.random.seed(seed)
    _w = jnp.asarray

    def _rec_inputs():
        import jax
        import jax.numpy as jnp
        _rk = jax.random.key(seed)
        x = -0.000125 + 0.9999 * jax.random.normal(jax.random.fold_in(_rk, 1), (4, 512, 512), jnp.float32)
        _lenS = 512 - jax.random.randint(jax.random.fold_in(_rk, 7), (4,), 0, max(1, 512 // 4) + 1, jnp.int32)
        _lenS2 = 1024 - jax.random.randint(jax.random.fold_in(_rk, 8), (4,), 0, max(1, 1024 // 4) + 1, jnp.int32)
        _ctx_1024P = jax.random.normal(jax.random.fold_in(_rk, 11), (4, 16, 256), jnp.float32)
        _ctx_1024c = jax.random.dirichlet(jax.random.fold_in(_rk, 511), 0.3 * jnp.ones((16,), jnp.float32), (4, 1024))
        _ctx_1024t = jnp.einsum('bsk,bkd->bsd', _ctx_1024c, _ctx_1024P)
        _ctx_1024t = _ctx_1024t * jax.lax.rsqrt(jnp.mean(jnp.square(_ctx_1024t)) + 1e-12) * 0.953939
        ctx_1024 = 4.13588e-05 + 0.999923 * (_ctx_1024t + 0.3 * jax.random.normal(jax.random.fold_in(_rk, 611), (4, 1024, 256), jnp.float32))
        pos_1xS = jnp.broadcast_to(jnp.arange(512, dtype=jnp.int32), (1, 512))
        _validS = jnp.arange(512)[None, :] < _lenS[:, None]
        _validS2 = jnp.arange(1024)[None, :] < _lenS2[:, None]
        _causal = jnp.tril(jnp.ones((512, 512), dtype=bool))
        mask_BxS_ik0 = jnp.where(jnp.broadcast_to(_validS[:, :], (4, 512)), 0, 1).astype(jnp.int32)
        return (x, ctx_1024, pos_1xS, mask_BxS_ik0)
    x, ctx_1024, pos_1xS, mask_BxS_ik0 = _rec_inputs()

    def _L0_xattn_setup():
        import jax, jax.numpy as jnp
        import numpy as np
        EPS = 1e-06

        def _rmsnorm(x, w):
            var = jnp.mean(jnp.square(x), axis=-1, keepdims=True)
            return x * jax.lax.rsqrt(var + EPS) * w
        key = jax.random.key(seed)
        ks = jax.random.split(key, 6)
        B, N, M = (4, 1024, 512)
        d_model, memory_dim = (512, 256)
        hidden_states = jax.random.normal(ks[0], (B, N, d_model), dtype=jnp.float32)
        memory = jax.random.normal(ks[1], (B, M, memory_dim), dtype=jnp.float32)
        W_mem = jax.random.normal(ks[2], (d_model, memory_dim), dtype=jnp.float32) / np.sqrt(memory_dim)
        W_gate = jax.random.normal(ks[3], (d_model, 2 * d_model), dtype=jnp.float32) / np.sqrt(2 * d_model)
        b_gate = jax.random.normal(ks[4], (d_model,), dtype=jnp.float32) * 0.01
        norm_w = jnp.ones((d_model,), dtype=jnp.float32)
        return {'hidden_states': hidden_states, 'memory': memory, 'W_mem': W_mem, 'W_gate': W_gate, 'b_gate': b_gate, 'norm_w': norm_w}
    _L0_xattn_all = _L0_xattn_setup()
    _L0_xattn_in = {k: v for k, v in _L0_xattn_all.items() if k in ('W_mem', 'W_gate', 'b_gate', 'norm_w')}
    del _L0_xattn_all

    def _L1_xattn_setup():
        import jax, jax.numpy as jnp
        import numpy as np
        H = 512
        NH = 16
        HD = H // NH
        CH = 256
        CC = 256
        CHD = CC // NH
        I = 1376
        B = 2
        L = 512
        LE = 256
        EPS = 1e-06

        def rms_norm(x, w):
            xf = x.astype(jnp.float32)
            var = jnp.mean(xf * xf, axis=-1, keepdims=True)
            return (w * (xf * jax.lax.rsqrt(var + EPS))).astype(x.dtype)

        def expert_mask(tt):
            vm = jnp.zeros(tt.shape, dtype=bool)
            vm = vm.at[:, :-1].set((tt[:, :-1] == 1) & (tt[:, 1:] == 1))
            return vm

        def rotate_half(x):
            d = x.shape[-1] // 2
            return jnp.concatenate([-x[..., d:], x[..., :d]], axis=-1)

        def apply_rotary(q, k, position_ids, seq_len):
            inv = 1.0 / 10000.0 ** (jnp.arange(0, HD, 2, dtype=jnp.float32) / HD)
            t = jnp.arange(seq_len, dtype=jnp.float32)
            freqs = jnp.outer(t, inv)
            emb = jnp.concatenate([freqs, freqs], axis=-1)
            cos = jnp.cos(emb)[position_ids][:, None].astype(q.dtype)
            sin = jnp.sin(emb)[position_ids][:, None].astype(q.dtype)
            return (q * cos + rotate_half(q) * sin, k * cos + rotate_half(k) * sin)

        def sdpa(q, k, v, causal):
            scale = 1.0 / np.sqrt(q.shape[-1])
            scores = jnp.einsum('bhqd,bhkd->bhqk', q * scale, k)
            if causal:
                mask = jnp.tril(jnp.ones((q.shape[-2], k.shape[-2]), dtype=bool))
                scores = jnp.where(mask, scores, jnp.finfo(jnp.float32).min)
            p = jax.nn.softmax(scores.astype(jnp.float32), axis=-1).astype(q.dtype)
            return jnp.einsum('bhqk,bhkd->bhqd', p, v)

        def heads(x, nh, hd):
            b, l, _ = x.shape
            return x.reshape(b, l, nh, hd).transpose(0, 2, 1, 3)
        key = jax.random.key(seed)
        ks = jax.random.split(key, 20)
        s = 0.02
        f32 = jnp.float32
        return {'hidden_states': jax.random.normal(ks[0], (B, L, H), f32), 'encoder_outputs': jax.random.normal(ks[1], (B, LE, CH), f32), 'token_type_ids': jax.random.randint(ks[2], (B, L), 0, 2, jnp.int32), 'position_ids': jnp.arange(L, dtype=jnp.int32)[None, :], 'ln_in_w': jnp.ones((H,), f32), 'ln_post_attn_w': jnp.ones((H,), f32), 'ln_post_cross_w': jnp.ones((H,), f32), 'v_qkv': jax.random.normal(ks[3], (H, 3 * H), f32) * s, 'l_qkv': jax.random.normal(ks[4], (H, 3 * H), f32) * s, 'v_dense': jax.random.normal(ks[5], (H, H), f32) * s, 'l_dense': jax.random.normal(ks[6], (H, H), f32) * s, 'cq_w': jax.random.normal(ks[7], (H, CC), f32) * s, 'ckv_w': jax.random.normal(ks[8], (CH, 2 * CC), f32) * s, 'cdense_w': jax.random.normal(ks[9], (CC, H), f32) * s, 'v_gate': jax.random.normal(ks[10], (H, I), f32) * s, 'v_up': jax.random.normal(ks[11], (H, I), f32) * s, 'v_down': jax.random.normal(ks[12], (I, H), f32) * s, 'l_gate': jax.random.normal(ks[13], (H, I), f32) * s, 'l_up': jax.random.normal(ks[14], (H, I), f32) * s, 'l_down': jax.random.normal(ks[15], (I, H), f32) * s}
    _L1_xattn_all = _L1_xattn_setup()
    _L1_xattn_in = {k: v for k, v in _L1_xattn_all.items() if k in ('ln_in_w', 'ln_post_attn_w', 'ln_post_cross_w', 'v_qkv', 'l_qkv', 'v_dense', 'l_dense', 'cq_w', 'ckv_w', 'cdense_w', 'v_gate', 'v_up', 'v_down', 'l_gate', 'l_up', 'l_down')}
    del _L1_xattn_all
    return {'x': x, 'ctx_1024': ctx_1024, 'pos_1xS': pos_1xS, 'mask_BxS_ik0': mask_BxS_ik0, 'L0_xattn_W_mem': _L0_xattn_in['W_mem'], 'L0_xattn_W_gate': _L0_xattn_in['W_gate'], 'L0_xattn_b_gate': _L0_xattn_in['b_gate'], 'L0_xattn_norm_w': _L0_xattn_in['norm_w'], 'L1_xattn_ln_in_w': _L1_xattn_in['ln_in_w'], 'L1_xattn_ln_post_attn_w': _L1_xattn_in['ln_post_attn_w'], 'L1_xattn_ln_post_cross_w': _L1_xattn_in['ln_post_cross_w'], 'L1_xattn_v_qkv': _L1_xattn_in['v_qkv'], 'L1_xattn_l_qkv': _L1_xattn_in['l_qkv'], 'L1_xattn_v_dense': _L1_xattn_in['v_dense'], 'L1_xattn_l_dense': _L1_xattn_in['l_dense'], 'L1_xattn_cq_w': _L1_xattn_in['cq_w'], 'L1_xattn_ckv_w': _L1_xattn_in['ckv_w'], 'L1_xattn_cdense_w': _L1_xattn_in['cdense_w'], 'L1_xattn_v_gate': _L1_xattn_in['v_gate'], 'L1_xattn_v_up': _L1_xattn_in['v_up'], 'L1_xattn_v_down': _L1_xattn_in['v_down'], 'L1_xattn_l_gate': _L1_xattn_in['l_gate'], 'L1_xattn_l_up': _L1_xattn_in['l_up'], 'L1_xattn_l_down': _L1_xattn_in['l_down']}

def reference(x, ctx_1024, pos_1xS, mask_BxS_ik0, L0_xattn_W_mem, L0_xattn_W_gate, L0_xattn_b_gate, L0_xattn_norm_w, L1_xattn_ln_in_w, L1_xattn_ln_post_attn_w, L1_xattn_ln_post_cross_w, L1_xattn_v_qkv, L1_xattn_l_qkv, L1_xattn_v_dense, L1_xattn_l_dense, L1_xattn_cq_w, L1_xattn_ckv_w, L1_xattn_cdense_w, L1_xattn_v_gate, L1_xattn_v_up, L1_xattn_v_down, L1_xattn_l_gate, L1_xattn_l_up, L1_xattn_l_down):
    import jax
    import jax.numpy as jnp

    def _L0_xattn_ref(hidden_states, memory, W_mem, W_gate, b_gate, norm_w):
        import jax, jax.numpy as jnp
        import numpy as np
        EPS = 1e-06

        def _rmsnorm(x, w):
            var = jnp.mean(jnp.square(x), axis=-1, keepdims=True)
            return x * jax.lax.rsqrt(var + EPS) * w
        D = hidden_states.shape[-1]
        memory_proj = jnp.einsum('bme,de->bmd', memory, W_mem)
        scores = jnp.einsum('bnd,bmd->bnm', hidden_states, memory_proj) / jnp.sqrt(jnp.float32(D))
        attn = jax.nn.softmax(scores, axis=-1)
        memory_context = jnp.einsum('bnm,bmd->bnd', attn, memory_proj)
        gate_input = jnp.concatenate([hidden_states, memory_context], axis=-1)
        gate = jax.nn.sigmoid(jnp.einsum('bnf,df->bnd', gate_input, W_gate) + b_gate)
        fused = hidden_states + gate * memory_context
        return _rmsnorm(fused, norm_w)

    def _L1_xattn_ref(hidden_states, encoder_outputs, token_type_ids, position_ids, ln_in_w, ln_post_attn_w, ln_post_cross_w, v_qkv, l_qkv, v_dense, l_dense, cq_w, ckv_w, cdense_w, v_gate, v_up, v_down, l_gate, l_up, l_down):
        import jax, jax.numpy as jnp
        import numpy as np
        H = 512
        NH = 16
        HD = H // NH
        CH = 256
        CC = 256
        CHD = CC // NH
        I = 1376
        B = 2
        L = 512
        LE = 256
        EPS = 1e-06

        def rms_norm(x, w):
            xf = x.astype(jnp.float32)
            var = jnp.mean(xf * xf, axis=-1, keepdims=True)
            return (w * (xf * jax.lax.rsqrt(var + EPS))).astype(x.dtype)

        def expert_mask(tt):
            vm = jnp.zeros(tt.shape, dtype=bool)
            vm = vm.at[:, :-1].set((tt[:, :-1] == 1) & (tt[:, 1:] == 1))
            return vm

        def rotate_half(x):
            d = x.shape[-1] // 2
            return jnp.concatenate([-x[..., d:], x[..., :d]], axis=-1)

        def apply_rotary(q, k, position_ids, seq_len):
            inv = 1.0 / 10000.0 ** (jnp.arange(0, HD, 2, dtype=jnp.float32) / HD)
            t = jnp.arange(seq_len, dtype=jnp.float32)
            freqs = jnp.outer(t, inv)
            emb = jnp.concatenate([freqs, freqs], axis=-1)
            cos = jnp.cos(emb)[position_ids][:, None].astype(q.dtype)
            sin = jnp.sin(emb)[position_ids][:, None].astype(q.dtype)
            return (q * cos + rotate_half(q) * sin, k * cos + rotate_half(k) * sin)

        def sdpa(q, k, v, causal):
            scale = 1.0 / np.sqrt(q.shape[-1])
            scores = jnp.einsum('bhqd,bhkd->bhqk', q * scale, k)
            if causal:
                mask = jnp.tril(jnp.ones((q.shape[-2], k.shape[-2]), dtype=bool))
                scores = jnp.where(mask, scores, jnp.finfo(jnp.float32).min)
            p = jax.nn.softmax(scores.astype(jnp.float32), axis=-1).astype(q.dtype)
            return jnp.einsum('bhqk,bhkd->bhqd', p, v)

        def heads(x, nh, hd):
            b, l, _ = x.shape
            return x.reshape(b, l, nh, hd).transpose(0, 2, 1, 3)
        b, l, _ = hidden_states.shape
        vm = expert_mask(token_type_ids)[..., None]
        residual = hidden_states
        x = rms_norm(hidden_states, ln_in_w)
        mixed = jnp.where(vm, x @ v_qkv, x @ l_qkv)
        q, k, v = jnp.split(mixed, 3, axis=-1)
        q, k, v = (heads(q, NH, HD), heads(k, NH, HD), heads(v, NH, HD))
        q, k = apply_rotary(q, k, position_ids, l)
        ctx = sdpa(q, k, v, causal=True)
        ctx = ctx.transpose(0, 2, 1, 3).reshape(b, l, H)
        attn_out = jnp.where(vm, ctx @ v_dense, ctx @ l_dense)
        hidden_states = residual + attn_out
        ci = rms_norm(hidden_states, ln_post_cross_w)
        cq = heads(ci @ cq_w, NH, CHD)
        ckv = encoder_outputs @ ckv_w
        ck, cv = jnp.split(ckv, 2, axis=-1)
        ck, cv = (heads(ck, NH, CHD), heads(cv, NH, CHD))
        cctx = sdpa(cq, ck, cv, causal=False)
        cctx = cctx.transpose(0, 2, 1, 3).reshape(b, l, CC)
        hidden_states = hidden_states + cctx @ cdense_w
        mi = rms_norm(hidden_states, ln_post_attn_w)
        v_out = jax.nn.silu(mi @ v_gate) * (mi @ v_up) @ v_down
        l_out = jax.nn.silu(mi @ l_gate) * (mi @ l_up) @ l_down
        hidden_states = hidden_states + jnp.where(vm, v_out, l_out)
        return hidden_states
    x = _L0_xattn_ref(x, ctx_1024, L0_xattn_W_mem, L0_xattn_W_gate, L0_xattn_b_gate, L0_xattn_norm_w)
    x = _L1_xattn_ref(x, ctx_1024, mask_BxS_ik0, pos_1xS, L1_xattn_ln_in_w, L1_xattn_ln_post_attn_w, L1_xattn_ln_post_cross_w, L1_xattn_v_qkv, L1_xattn_l_qkv, L1_xattn_v_dense, L1_xattn_l_dense, L1_xattn_cq_w, L1_xattn_ckv_w, L1_xattn_cdense_w, L1_xattn_v_gate, L1_xattn_v_up, L1_xattn_v_down, L1_xattn_l_gate, L1_xattn_l_up, L1_xattn_l_down)
    return x

_drawn_inputs = setup_inputs


def setup_inputs(seed=0):
    import zlib

    import numpy as np

    out = dict(_drawn_inputs(seed))
    spreads = {'L0_xattn_norm_w': (1.0, 0.2),
     'L1_xattn_ln_in_w': (1.0, 0.6),
     'L1_xattn_ln_post_attn_w': (1.0, 0.6),
     'L1_xattn_ln_post_cross_w': (1.0, 0.6)}
    factors = {'L0_xattn_b_gate': 8.0,
     'L1_xattn_v_qkv': 8.0,
     'L1_xattn_v_dense': 3.292,
     'L1_xattn_cq_w': 38.312,
     'L1_xattn_ckv_w': 2.752,
     'L1_xattn_cdense_w': 2.834,
     'L1_xattn_v_gate': 2.926,
     'L1_xattn_v_up': 2.824,
     'L1_xattn_v_down': 2.83}
    for name, (base, spread) in spreads.items():
        noise = np.random.default_rng([zlib.crc32(name.encode()), seed]).standard_normal(out[name].shape)
        drawn = base * np.exp(spread * noise) if base else spread * noise
        out[name] = jnp.asarray(drawn.astype(out[name].dtype))
    for name, factor in factors.items():
        out[name] = (out[name] * factor).astype(out[name].dtype)
    return out
```

```python
from contextlib import ExitStack

import concourse.bass as bass
from concourse import mybir

F32 = mybir.dt.float32
F32R = mybir.dt.float32r
BF16 = mybir.dt.bfloat16
I32 = mybir.dt.int32
ALU = mybir.AluOpType
ACT = mybir.ActivationFunctionType
AX = mybir.AxisListType

P = 128
BANK = 512
EPS = 1e-6


class Lane:

    def __init__(self, engine, sem):
        self.engine, self.sem, self.count, self.passed = engine, sem, 0, {}

    def wait(self, *after):
        for sem, value in marks(after):
            if self.passed.get(id(sem), 0) < value:
                self.passed[id(sem)] = value
                self.engine.wait_ge(sem, value)

    def do(self, emit, *after):
        self.wait(*after)
        self.count += 1
        emit(self.engine).then_inc(self.sem, 1)
        return (self.sem, self.count)

    def dma(self, port, out, in_, *after):
        self.wait(*after)
        port.count += 16
        self.engine.dma_start(out, in_).then_inc(port.sem, 16)
        return (port.sem, port.count)


class Port:

    def __init__(self, sem):
        self.sem, self.count = sem, 0


def marks(after):
    for a in after:
        if a is None:
            continue
        if isinstance(a, tuple) and len(a) == 2 and isinstance(a[1], int):
            yield a
        else:
            yield from marks(a)


class Slot:

    def __init__(self, view, port=None):
        self.view, self.port, self.freed = view, port, []


class Ring:
    def __init__(self, slots):
        self.slots, self.next = slots, 0

    def take(self):
        slot = self.slots[self.next % len(self.slots)]
        self.next += 1
        return slot

    def skip_to_multiple(self, n):
        self.next = -(-self.next // n) * n


def f32(ap):
    return ap.bitcast(F32)


def products(pairs):
    out = []
    for (ah, al), (bh, bl) in pairs:
        out += [(al, bh), (ah, bl), (ah, bh)]
    return out


def gemm(out, passes):
    def emit(e):
        for i, (lhsT, rhs) in enumerate(passes):
            last = e.matmul(out, lhsT, rhs, start=(i == 0), stop=(i == len(passes) - 1))
        return last
    return emit


def xattn_block(nc, dims, ins, const, out):
    B, T, D, E, M, NH, I = (dims[k] for k in ("B", "T", "D", "E", "M", "NH", "I"))
    HD, CC = D // NH, E
    CHD = CC // NH
    DT, TT, ET, MT = D // P, T // P, E // P, M // P
    assert T == BANK and D == BANK and M == 2 * BANK and HD == 32 and CHD == 16
    GH = P // HD
    L0_SCALE, SELF_SCALE, CROSS_SCALE = D ** -0.5, HD ** -0.5, CHD ** -0.5

    top = ExitStack()

    def sem(name):
        return top.enter_context(nc.semaphore(name))

    pe = Lane(nc.tensor, sem("pe_done"))
    act = Lane(nc.scalar, sem("act_done"))
    dve = Lane(nc.vector, sem("dve_done"))
    pool = Lane(nc.gpsimd, sem("pool_done"))
    sp = Lane(nc.sync, sem("sp_done"))

    all_ports = []

    def on_pool(emit, *after):
        return pool.do(emit, *after, (pool.sem, pool.count) if pool.count else None)

    def port(name):
        all_ports.append(Port(sem(name)))
        return all_ports[-1]

    def alloc(ctx, name, shape, dt=F32):
        return ctx.enter_context(nc.sbuf_tensor(name, shape, dt))

    def ring(ctx, name, n, shape, dt=F32, dma=False):
        return Ring([Slot(alloc(ctx, f"{name}{i}", shape, dt), port(f"{name}{i}_dma") if dma else None)
                     for i in range(n)])

    def pair(ctx, name, shape):
        return alloc(ctx, name + "_hi", shape, F32R), alloc(ctx, name + "_lo", shape, F32R)

    lanes = (pe, act, dve, pool, sp)
    stores = []

    def barrier():
        ends = [(x.sem, x.count) for x in lanes if x.count]
        ports = [(p.sem, p.count) for p in all_ports if p.count]
        for x in lanes:
            x.wait(ends, ports)

    psum = top.enter_context(nc.psum_tensor("psum", [P, 8, BANK], F32))

    def split(src, hi, lo, *after, copier=None):
        copier = copier or act
        if copier is act:
            m_hi = act.do(lambda e: e.activation(hi, src, ACT.Copy), *after)
        else:
            m_hi = copier.do(lambda e: e.tensor_copy(hi, src), *after)
        m_lo = dve.do(lambda e: e.tensor_tensor(lo, src, f32(hi), ALU.subtract), *after, m_hi)
        return [m_hi, m_lo]

    hT = alloc(top, "hT", [P, B, DT, T])
    h_ready = [None] * B
    ident = alloc(top, "ident", [P, P])
    ident16 = alloc(top, "ident16", [P, P], BF16)
    mean_w = alloc(top, "mean_w", [P, P])
    eps_col = alloc(top, "eps_col", [P, 1])
    causal = alloc(top, "causal", [P, 2, P], BF16)
    norm_ws = alloc(top, "norm_ws", [P, 4, DT])
    gate_b = alloc(top, "gate_b", [P, DT])
    picked = alloc(top, "picked", [P, 2, B, T], BF16)
    VEXP, LEXP = 0, 1

    c_port = port("const_dma")
    for dst, src in ((ident[:, :], const["ident"]), (mean_w[:, :], const["mean_w"]),
                     (gate_b[:, :], ins["b_gate"]),
                     (norm_ws[:, 0, :], ins["norm_w"]),
                     (norm_ws[:, 1, :], ins["ln_in_w"]),
                     (norm_ws[:, 2, :], ins["ln_post_cross_w"]),
                     (norm_ws[:, 3, :], ins["ln_post_attn_w"])):
        consts = sp.dma(c_port, dst, src)
    eps_set = dve.do(lambda e: e.memset(eps_col[:, :], EPS))

    self_qk = nc.dram_tensor("self_qk", [B, 2, DT, 2, P, T], F32, kind="Internal").ap()
    self_v = nc.dram_tensor("self_v", [B, TT, P, D], F32, kind="Internal").ap()
    cross_k = nc.dram_tensor("cross_k", [B, ET, 2, P, M], F32, kind="Internal").ap()
    cross_v = nc.dram_tensor("cross_v", [B, MT, P, CC], F32, kind="Internal").ap()
    cross_q = nc.dram_tensor("cross_q", [B, ET, 2, P, T], F32, kind="Internal").ap()

    def norm_buffers(ctx, name, n=2):
        return {"sq": ring(ctx, name + "_sq", 2, [P, T]), "rstd": ring(ctx, name + "_rstd", n, [P, T])}

    def rstd_of(src, buf, banks, *after):
        total = buf["rstd"].take()
        prev = None
        for t in range(DT):
            sq = buf["sq"].take()
            m = act.do(lambda e, t=t, sq=sq: e.activation(sq.view[:, :], src[:, t, :], ACT.Square),
                       *after, sq.freed)
            if t == 0:
                prev = dve.do(lambda e, sq=sq: e.tensor_copy(total.view[:, :], sq.view[:, :]), m, total.freed)
            else:
                prev = dve.do(lambda e, sq=sq: e.tensor_tensor(total.view[:, :], total.view[:, :], sq.view[:, :],
                                                               ALU.add), m, prev)
            sq.freed = [prev]
        bank = banks.take()
        m = pe.do(gemm(bank.view, [(mean_w[:, :], total.view[:, :])]), prev, bank.freed, consts)
        r = total
        m = act.do(lambda e: e.activation(r.view[:, :], bank.view, ACT.Sqrt, bias=eps_col[:, 0:1]), m, eps_set)
        bank.freed = [m]
        m = dve.do(lambda e: e.reciprocal(r.view[:, :], r.view[:, :]), m)
        return r, m

    def scaled(dst, src, norm, t, r, *after):
        return dve.do(lambda e: e.scalar_tensor_tensor(out=dst, in0=src, scalar=norm_ws[:, norm, t:t + 1],
                                                       in1=r.view[:, :], op0=ALU.mult, op1=ALU.mult),
                      *after, consts)

    def load_split(w, n, source, staging, width):
        out = []
        for i in range(n):
            s = staging.take()
            rows, src = source(i)
            m = sp.dma(s.port, s.view[0:rows, 0:width], src, s.freed)
            raw = s.view[0:rows, 0:width]
            ms = split(raw, w[0][0:rows, i, 0:width], w[1][0:rows, i, 0:width], m)
            s.freed = ms
            out.append(ms)
        return out

    def bank_ring(first, n, width=1):
        return Ring([Slot(psum[:, first + i * width:first + (i + 1) * width, :] if width > 1 else psum[:, first + i, :])
                     for i in range(n)])

    def T_(ap_pair, *idx):
        return ap_pair[0][idx], ap_pair[1][idx]

    with ExitStack() as ph:
        wm = pair(ph, "wm", [P, DT, E])
        wmT = pair(ph, "wmT", [P, ET, D])
        wgT = pair(ph, "wgT", [P, DT, D])
        wc = pair(ph, "wc", [P, ET, D])
        ckv = pair(ph, "ckv", [P, ET, 2 * CC])
        banks = bank_ring(0, 8)
        all_cols = slice(None)

        with ExitStack() as setup:
            staging = ring(setup, "wstage", 3, [P, D], dma=True)
            wg2T = pair(setup, "wg2T", [P, DT, D])
            wm_raw = alloc(setup, "wm_raw", [P, DT, E])
            wg_raw = alloc(setup, "wg_raw", [P, DT, 2 * D])
            raw_port, g_port = port("wm_raw_dma"), port("wg_raw_dma")
            wm_in = sp.dma(raw_port, wm_raw[:, :, :], ins["W_mem"].rearrange("(t p) e -> p t e", p=P))
            wg_in = sp.dma(g_port, wg_raw[:, :, :], ins["W_gate"].rearrange("(t p) f -> p t f", p=P))
            wm_ready = split(wm_raw[:, :, :], wm[0][:, :, :], wm[1][:, :, :], wm_in)
            ckv_ready = load_split(ckv, ET, lambda i: (P, ins["ckv_w"][i * P:(i + 1) * P, :]), staging, 2 * CC)

            def turn(raw, col, dst, i, landed):
                bank = banks.take()

                def emit(e):
                    for t in range(DT):
                        last = e.transpose(bank.view[:, t * P:(t + 1) * P], raw[:, t, col:col + P], ident[:, :])
                    return last
                m = pe.do(emit, landed, consts, bank.freed)
                bank.freed = split(bank.view, dst[0][:, i, :], dst[1][:, i, :], m)
                return bank.freed

            wmT_ready = [turn(wm_raw, i * P, wmT, i, wm_in) for i in range(ET)]
            wgT_ready = [turn(wg_raw, i * P, wgT, i, wg_in) for i in range(DT)]
            wg2T_ready = [turn(wg_raw, D + i * P, wg2T, i, wg_in) for i in range(DT)]
            wc_ready = []
            for i in range(ET):
                bank = banks.take()
                m = pe.do(gemm(bank.view, products([(T_(wm, all_cols, t, slice(i * P, i * P + P)),
                                                     T_(wg2T, all_cols, t, all_cols)) for t in range(DT)])),
                          wm_ready, wg2T_ready, bank.freed)
                bank.freed = split(bank.view, wc[0][:, i, :], wc[1][:, i, :], m)
                wc_ready.append(bank.freed)
            causal_in = alloc(setup, "causal_in", [P, 2, P])
            m = sp.dma(port("causal_dma"), causal_in[:, :, :], const["causal"])
            dve.do(lambda e: e.tensor_copy(causal[:, :, :], causal_in[:, :, :]), m)
            dve.do(lambda e: e.tensor_copy(ident16[:, :], ident[:, :]), consts)
            types = alloc(setup, "types", [P, B, T], I32)
            types_f = alloc(setup, "types_f", [P, B, T])
            t_port = port("types_dma")
            m = sp.dma(t_port, types[:, :, :].rearrange("p b t -> p (b t)"),
                       ins["mask"].rearrange("b t -> (b t)").partition_broadcast(P))
            m = dve.do(lambda e: e.tensor_scalar(types_f[:, :, :], types[:, :, :], 1.0, None, ALU.is_equal), m)
            m1 = dve.do(lambda e: e.memset(picked[:, VEXP, :, T - 1:T], 0.0))
            m2 = dve.do(lambda e: e.tensor_tensor(picked[:, VEXP, :, 0:T - 1], types_f[:, :, 0:T - 1],
                                                  types_f[:, :, 1:T], ALU.mult), m)
            picked_ready = dve.do(lambda e: e.tensor_scalar(picked[:, LEXP, :, :], picked[:, VEXP, :, :], -1.0, 1.0,
                                                            ALU.mult, ALU.add), m1, m2)
        barrier()

        x_rows = ring(ph, "x_rows", 2, [P, D], dma=True)
        m_rows = ring(ph, "m_rows", 4, [P, E], dma=True)
        xT = pair(ph, "xT", [P, DT, T])
        mem = pair(ph, "mem", [P, MT, E])
        memT = pair(ph, "memT", [P, ET, M])
        k_out = Ring([Slot((alloc(ph, "k_hi", [P, BANK], F32R), alloc(ph, "k_lo", [P, BANK], F32R)), port("k_dma"))])
        v_out = ring(ph, "v_out", 2, [P, CC], dma=True)
        qT = pair(ph, "qT", [P, ET, T])
        probs = alloc(ph, "probs", [P, M])
        probsT = pair(ph, "probsT", [P, MT, T])
        gates = ring(ph, "gate", 2, [P, T])
        stat = alloc(ph, "stat", [P, 4])
        nb = norm_buffers(ph, "n0", 1)
        xT_free = mem_free = memT_free = probs_free = probsT_free = qT_free = stat_free = []

        for b in range(B):
            x_banks = [banks.take() for _ in range(DT)]
            for t in range(TT):
                s = x_rows.take()
                m = sp.dma(s.port, s.view[:, :], ins["x"][b, t * P:(t + 1) * P, :], s.freed)

                def emit(e, s=s, t=t):
                    for f in range(DT):
                        last = e.transpose(x_banks[f].view[:, t * P:(t + 1) * P], s.view[:, f * P:(f + 1) * P],
                                           ident[:, :])
                    return last
                turned = pe.do(emit, m, [k.freed for k in x_banks])
                s.freed = [turned]
            xT_ready = []
            for f, k in enumerate(x_banks):
                keep = act.do(lambda e, f=f, k=k: e.activation(hT[:, b, f, :], k.view, ACT.Copy), turned)
                ms = split(k.view, xT[0][:, f, :], xT[1][:, f, :], turned, xT_free)
                k.freed = [keep, ms]
                xT_ready += [ms]
                h_ready[b] = keep
            mem_ready, memT_ready = [], []
            for half in range(2):
                t_banks = [banks.take() for _ in range(ET)]
                for j in range(MT // 2):
                    mt = half * (MT // 2) + j
                    s = m_rows.take()
                    m = sp.dma(s.port, s.view[:, :], ins["ctx"][b, mt * P:(mt + 1) * P, :], s.freed)

                    def emit(e, s=s, j=j, t_banks=t_banks):
                        for f in range(ET):
                            last = e.transpose(t_banks[f].view[:, j * P:(j + 1) * P], s.view[:, f * P:(f + 1) * P],
                                               ident[:, :])
                        return last
                    turned = pe.do(emit, m, [k.freed for k in t_banks])
                    ms = split(s.view[:, :], mem[0][:, mt, :], mem[1][:, mt, :], m, mem_free)
                    mem_ready += [ms]
                    s.freed = [turned, ms]
                for f, k in enumerate(t_banks):
                    cols = slice(half * BANK, (half + 1) * BANK)
                    k.freed = split(k.view, memT[0][:, f, cols], memT[1][:, f, cols], turned, memT_free)
                    memT_ready += [k.freed]
            q_ready = []
            for i in range(ET):
                k = banks.take()
                m = pe.do(gemm(k.view, products([(T_(wm, all_cols, t, slice(i * P, i * P + P)),
                                                  T_(xT, all_cols, t, all_cols)) for t in range(DT)])),
                          xT_ready, k.freed)
                k.freed = split(k.view, qT[0][:, i, :], qT[1][:, i, :], m, qT_free)
                q_ready += [k.freed]
            for i in range(ET):
                for half in range(2):
                    cols = slice(half * BANK, (half + 1) * BANK)
                    k = banks.take()
                    m = pe.do(gemm(k.view, products([(T_(ckv, all_cols, t, slice(i * P, i * P + P)),
                                                      T_(memT, all_cols, t, cols)) for t in range(ET)])),
                              memT_ready, k.freed)
                    s = k_out.take()
                    k.freed = split(k.view, s.view[0][:, :], s.view[1][:, :], m, s.freed)
                    sp.dma(s.port, cross_k[b, i, 0, :, cols], f32(s.view[0][:, :]), k.freed)
                    s.freed = [sp.dma(s.port, cross_k[b, i, 1, :, cols], f32(s.view[1][:, :]))]
            for mt in range(MT):
                k = banks.take()
                m = pe.do(gemm(k.view[:, 0:CC], products([(T_(memT, all_cols, t, slice(mt * P, mt * P + P)),
                                                           T_(ckv, all_cols, t, slice(CC, 2 * CC)))
                                                          for t in range(ET)])),
                          memT_ready, k.freed)
                s = v_out.take()
                k.freed = [act.do(lambda e, k=k, s=s: e.activation(s.view[:, :], k.view[:, 0:CC], ACT.Copy),
                                  m, s.freed)]
                s.freed = [sp.dma(s.port, cross_v[b, mt, :, :], s.view[:, :], k.freed)]
            probsT_ready = []
            for qt in range(TT):
                banks.skip_to_multiple(2)
                b0 = banks.next % 8
                s_banks = [banks.take(), banks.take()]
                scores = psum[:, b0:b0 + 2, :]
                qcols = slice(qt * P, (qt + 1) * P)
                for half, k in enumerate(s_banks):
                    cols = slice(half * BANK, (half + 1) * BANK)
                    scored = pe.do(gemm(k.view, products([(T_(qT, all_cols, t, qcols), T_(memT, all_cols, t, cols))
                                                          for t in range(ET)])),
                                   q_ready, memT_ready, k.freed)
                m = dve.do(lambda e, scores=scores: e.tensor_reduce(stat[:, 0:1], scores, AX.XY, ALU.max),
                           scored, stat_free)
                m = dve.do(lambda e: e.tensor_scalar(stat[:, 1:2], stat[:, 0:1], -L0_SCALE, None, ALU.mult), m)
                m = act.do(lambda e, scores=scores: e.activation(
                    probs[:, :].rearrange("p (a n) -> p a n", a=2), scores, ACT.Exp, bias=stat[:, 1:2],
                    scale=L0_SCALE, accum_out=stat[:, 2:3]), m, probs_free)
                for k in s_banks:
                    k.freed = [m]
                m = dve.do(lambda e: e.reciprocal(stat[:, 3:4], stat[:, 2:3]), m)
                m = dve.do(lambda e: e.tensor_scalar(probs[:, :], probs[:, :], stat[:, 3:4], None, ALU.mult), m)
                stat_free = [m]
                for half in range(2):
                    k = banks.take()

                    def emit(e, k=k, half=half):
                        for j in range(4):
                            at = (4 * half + j) * P
                            last = e.transpose(k.view[:, j * P:(j + 1) * P], probs[:, at:at + P], ident[:, :])
                        return last
                    turned = pe.do(emit, m, k.freed)
                    src = k.view.rearrange("p (j n) -> p j n", j=4)
                    k.freed = split(src, probsT[0][:, 4 * half:4 * half + 4, qcols],
                                    probsT[1][:, 4 * half:4 * half + 4, qcols], turned, probsT_free)
                    probsT_ready += [k.freed]
                probs_free = [turned]
            a_ready = []
            for i in range(ET):
                k = banks.take()
                m = pe.do(gemm(k.view, products([(T_(mem, all_cols, t, slice(i * P, i * P + P)),
                                                  T_(probsT, all_cols, t, all_cols)) for t in range(MT)])),
                          mem_ready, probsT_ready, k.freed)
                k.freed = split(k.view, qT[0][:, i, :], qT[1][:, i, :], m, scored)
                a_ready += [k.freed]
            probsT_free = mem_free = [m]
            memT_free = [m]
            for f in range(DT):
                fcols = slice(f * P, (f + 1) * P)
                kz, kc = banks.take(), banks.take()
                mz = pe.do(gemm(kz.view, products(
                    [(T_(wgT, all_cols, t, fcols), T_(xT, all_cols, t, all_cols)) for t in range(DT)]
                    + [(T_(wc, all_cols, t, fcols), T_(qT, all_cols, t, all_cols)) for t in range(ET)])),
                    a_ready, xT_ready, kz.freed)
                mc = pe.do(gemm(kc.view, products([(T_(wmT, all_cols, t, fcols), T_(qT, all_cols, t, all_cols))
                                                   for t in range(ET)])), a_ready, kc.freed)
                g = gates.take()
                m = act.do(lambda e, g=g, kz=kz, f=f: e.activation(g.view[:, :], kz.view, ACT.Sigmoid,
                                                                   bias=gate_b[:, f:f + 1]), mz, g.freed)
                kz.freed = [m]
                m = dve.do(lambda e, g=g, kc=kc: e.tensor_tensor(g.view[:, :], kc.view, g.view[:, :], ALU.mult),
                           m, mc)
                kc.freed = [m]
                h_ready[b] = dve.do(lambda e, g=g, f=f: e.tensor_tensor(hT[:, b, f, :], hT[:, b, f, :], g.view[:, :],
                                                                        ALU.add), m, h_ready[b])
                g.freed = [h_ready[b]]
            xT_free = qT_free = [mc]
            r, rm = rstd_of(hT[:, b, :, :], nb, banks, h_ready[b])
            for f in range(DT):
                h_ready[b] = scaled(hT[:, b, f, :], hT[:, b, f, :], 0, f, r, rm)
            r.freed = [h_ready[b]]
        barrier()

    with ExitStack() as ph:
        W3 = 3 * D
        wv = pair(ph, "wv_qkv", [P, DT, W3])
        wl = pair(ph, "wl_qkv", [P, DT, W3])
        staging = ring(ph, "qkv_stage", 3, [P, D], dma=True)
        cos = alloc(ph, "cos", [P, T])
        sin = alloc(ph, "sin", [P, T])
        banks = bank_ring(0, 8)
        turn_r = alloc(ph, "turn_r", [P, P], F32R)
        with ExitStack() as setup:
            turn_raw = alloc(setup, "turn_raw", [P, P])
            table = alloc(setup, "table", [P, 2, TT, P])
            pos_i = alloc(setup, "pos_i", [P, T], I32)
            pos_f = alloc(setup, "pos_f", [P, T])
            onehot = alloc(setup, "onehot", [P, TT, T])
            row_no = alloc(setup, "row_no", [P, TT])
            r_port, tab_port = port("turn_dma"), port("table_dma")
            pos_port, row_port = port("pos_dma"), port("row_dma")
            m = sp.dma(r_port, turn_raw[:, :], const["turn"])
            turn_ready = dve.do(lambda e: e.tensor_copy(turn_r[:, :], turn_raw[:, :]), m)
            tab_in = sp.dma(tab_port, table[:, :, :, :], const["rope"].rearrange("a (t p) d -> p a t d", p=P))
            row_in = sp.dma(row_port, row_no[:, :], const["row_no"])
            m = sp.dma(pos_port, pos_i[:, :], ins["pos"].rearrange("a t -> (a t)").partition_broadcast(P))
            m = dve.do(lambda e: e.tensor_scalar(pos_f[:, :], pos_i[:, :], 0.0, float(T - 1), ALU.max, ALU.min), m)
            for t in range(TT):
                hot = dve.do(lambda e, t=t: e.tensor_scalar(onehot[:, t, :], pos_f[:, :], row_no[:, t:t + 1], None,
                                                            ALU.is_equal), m, row_in)
            for a, dst in enumerate((cos, sin)):
                k = banks.take()
                m = pe.do(gemm(k.view, [(table[:, a, t, :], onehot[:, t, :]) for t in range(TT)]), hot, tab_in)
                rope_ready = act.do(lambda e, dst=dst, k=k: e.activation(dst[:, :], k.view, ACT.Copy), m)
                k.freed = [rope_ready]
        barrier()
        xs = {(x, p): alloc(ph, f"xn_{'vl'[x]}_{p}", [P, DT, T], F32R) for x in (VEXP, LEXP) for p in ("hi", "lo")}
        xn = ring(ph, "xn", 1, [P, T])
        xe = ring(ph, "xe", 2, [P, T])
        nb = norm_buffers(ph, "n1", 1)
        raw = Ring([Slot(pair(ph, f"raw{i}", [P, T])) for i in range(1)])
        prod = ring(ph, "prod", 2, [P, T])
        qk_out = Ring([Slot(pair(ph, f"qk{i}", [P, T]), port(f"qk{i}_dma")) for i in range(1)])
        v_out = ring(ph, "sv_out", 1, [P, D], dma=True)

        w_ready = {}
        for part in range(3):
            for x, w, name in ((VEXP, wv, "v_qkv"), (LEXP, wl, "l_qkv")):
                cols = slice(part * D, (part + 1) * D)
                w_ready[x, part] = []
                for t in range(DT):
                    s = staging.take()
                    m = sp.dma(s.port, s.view[:, :], ins[name][t * P:(t + 1) * P, cols], s.freed)
                    s.freed = split(s.view[:, :], w[0][:, t, cols], w[1][:, t, cols], m)
                    w_ready[x, part] += [s.freed]
        xs_free = []

        def expert_split(b, src, dsts, t, xe, *after):
            out = []
            for x in (VEXP, LEXP):
                s = xe.take()
                m = dve.do(lambda e, s=s, x=x: e.tensor_tensor(s.view[:, :], src, picked[:, x, b, :], ALU.mult),
                           *after, s.freed, picked_ready)
                s.freed = split(s.view[:, :], dsts[x, "hi"][:, t, :], dsts[x, "lo"][:, t, :], m, xs_free)
                out += [m, s.freed]
            return out

        def expert_pairs(ws, xs, wcols, xcols, x_is_lhs=False):
            out = []
            for x, w in ((VEXP, ws[0]), (LEXP, ws[1])):
                for t in range(DT):
                    a = T_(w, all_cols, t, wcols)
                    c = (xs[x, "hi"][:, t, xcols], xs[x, "lo"][:, t, xcols])
                    out.append((c, a) if x_is_lhs else (a, c))
            return out

        for b in range(B):
            r, rm = rstd_of(hT[:, b, :, :], nb, banks, h_ready[b])
            xs_ready = []
            for t in range(DT):
                s = xn.take()
                m = scaled(s.view[:, :], hT[:, b, t, :], 1, t, r, rm, s.freed)
                ms = expert_split(b, s.view[:, :], xs, t, xe, m)
                s.freed = ms
                xs_ready += ms
                r.freed = [m]
            for part in range(2):
                for f in range(DT):
                    k = banks.take()
                    wcols = slice(part * D + f * P, part * D + (f + 1) * P)
                    m = pe.do(gemm(k.view, products(expert_pairs((wv, wl), xs, wcols, all_cols))),
                              xs_ready, w_ready[VEXP, part], w_ready[LEXP, part], k.freed)
                    rw = raw.take()
                    ms = split(k.view, rw.view[0][:, :], rw.view[1][:, :], m, rw.freed)
                    kr = banks.take()
                    mr = pe.do(gemm(kr.view, [(turn_r[:, :], rw.view[1][:, :]), (turn_r[:, :], rw.view[0][:, :])]),
                               ms, turn_ready, kr.freed)
                    rw.freed = [mr]
                    p1, p2 = prod.take(), prod.take()
                    m1 = dve.do(lambda e, p1=p1, k=k: e.tensor_tensor(p1.view[:, :], k.view, cos[:, :], ALU.mult),
                                m, rope_ready, p1.freed)
                    m2 = dve.do(lambda e, p2=p2, kr=kr: e.tensor_tensor(p2.view[:, :], kr.view, sin[:, :], ALU.mult),
                                mr, p2.freed)
                    k.freed, kr.freed = [ms, m1], [m2]
                    m = dve.do(lambda e, p1=p1, p2=p2: e.tensor_tensor(p1.view[:, :], p1.view[:, :], p2.view[:, :],
                                                                       ALU.add), m1, m2)
                    p2.freed = [m]
                    s = qk_out.take()
                    ms = split(p1.view[:, :], s.view[0][:, :], s.view[1][:, :], m, s.freed)
                    p1.freed = ms
                    sp.dma(s.port, self_qk[b, part, f, 0, :, :], f32(s.view[0][:, :]), ms)
                    s.freed = [sp.dma(s.port, self_qk[b, part, f, 1, :, :], f32(s.view[1][:, :]))]
            for t in range(TT):
                k = banks.take()
                m = pe.do(gemm(k.view, products(expert_pairs((wv, wl), xs, slice(2 * D, W3),
                                                             slice(t * P, (t + 1) * P), True))),
                          xs_ready, w_ready[VEXP, 2], w_ready[LEXP, 2], k.freed)
                s = v_out.take()
                k.freed = [act.do(lambda e, k=k, s=s: e.activation(s.view[:, :], k.view, ACT.Copy), m, s.freed)]
                s.freed = [sp.dma(s.port, self_v[b, t, :, :], s.view[:, :], k.freed)]
            xs_free = [m]
        barrier()

    def attention(groups, G, score_sets, out_banks, bufs, load_group, load_values, row_blocks, col_blocks, scale,
                  set_views, neg_rows, pv_blocks, heads_per_out, finish, lag, early):
        stage = {}

        chunks = len(col_blocks)
        units = G * chunks

        def rows_of(g, unit):
            st = stage[g]
            h, c = divmod(unit, chunks)
            s = score_sets.take()
            m = pe.do(set_views["row"](s, st, h, row_blocks[c]), st["loaded"], s.freed)
            s.freed = [dve.do(lambda e: e.tensor_reduce(
                st["max"].view[:, h * TT + col:h * TT + col + 1], view, AX.X, ALU.max), m, st["max"].freed)
                for col, view in set_views["maxima"](s, row_blocks[c])]
            st["maxed"] += s.freed

        def maxima_to_rows(g):
            st = stage[g]
            k = out_banks.take()
            n = G * TT
            m = pe.do(lambda e: e.transpose(k.view[0:n, 0:P], st["max"].view[:, 0:n], ident[:, :]),
                      st["maxed"], k.freed)
            st["max"].freed = [m]
            neg = bufs["neg"].take()
            m1 = dve.do(lambda e: e.tensor_scalar(neg.view[0][0:n, :], k.view[0:n, 0:P], -1.0, None, ALU.mult),
                        m, neg.freed)
            m2 = dve.do(lambda e: e.scalar_tensor_tensor(out=neg.view[1][0:n, :], in0=k.view[0:n, 0:P], scalar=-1.0,
                                                         in1=f32(neg.view[0][0:n, :]), op0=ALU.mult,
                                                         op1=ALU.subtract), m1)
            k.freed = [m1, m2]
            for part in range(2):
                row = f32(st["q"].view[neg_rows + part:neg_rows + part + 1, :, :]).rearrange(
                    "o h (t n) -> o (h t) n", n=P)
                st["neg_in"] = sp.dma(neg.port, row, f32(neg.view[part][0:n, :]), m1, m2)
            neg.freed = [st["neg_in"]]

        def exps(g, unit):
            st = stage[g]
            h, c = divmod(unit, chunks)
            s = score_sets.take()
            m = pe.do(set_views["col"](s, st, h, col_blocks[c]), st["neg_in"], s.freed)
            p = bufs["probs"].take()
            s.freed = [act.do(lambda e: e.activation(p.view[:, :], set_views["used"](s), ACT.Exp, scale=scale),
                              m, p.freed)]
            if unit == units - 1:
                st["q"].freed = st["k"].freed = [m]
            return p, s.freed

        def values(g, unit, p, ready):
            st = stage[g]
            h, c = divmod(unit, chunks)
            first = h % heads_per_out == 0 and c == 0
            last = h % heads_per_out == heads_per_out - 1 and c == chunks - 1
            if first:
                st["acc"] = out_banks.take()
            acc = st["acc"]
            parts = list(pv_blocks(col_blocks[c]))

            def emit(e):
                for n, (block, cols, pcols) in enumerate(parts):
                    x = e.matmul(acc.view[:, cols], st["v_lhs"](h, block), p.view[:, pcols],
                                 start=first and n == 0, stop=last and n == len(parts) - 1, skip_group_check=True)
                return x
            m = pe.do(emit, ready, st["v_ready"](), acc.freed if first else None)
            p.freed = [m]
            if last:
                rs = bufs["recip"].take()
                m1 = dve.do(lambda e: e.reciprocal(rs.view[:, :], acc.view[32:64, :]), m, rs.freed)
                m2 = finish(g, h // heads_per_out, acc, rs, m1)
                acc.freed = [m1, m2]
                rs.freed = [m2]
            return m

        def start(g):
            stage[g] = load_group(g)
            stage[g]["max"] = bufs["max"].take()
            stage[g]["maxed"] = []

        start(0)
        load_values(0)
        for unit in range(units):
            rows_of(0, unit)
        maxima_to_rows(0)
        if groups > 1:
            start(1)
        waiting = []
        for g in range(groups):
            row_at = 0
            for unit in range(units):
                while g + 1 < groups and row_at < min(units, -(-(unit + 1) * units // (units - early))):
                    rows_of(g + 1, row_at)
                    row_at += 1
                    if row_at == units:
                        turn_at = unit + 1
                if g + 1 < groups and row_at == units and unit == turn_at:
                    maxima_to_rows(g + 1)
                waiting.append((g, unit, *exps(g, unit)))
                while len(waiting) > lag or (waiting and g == groups - 1 and unit == units - 1):
                    done, at, *operands = waiting.pop(0)
                    m = values(done, at, *operands)
                    if at == units - 1:
                        stage[done]["v_done"](m)
                        if done + 1 < groups:
                            load_values(done + 1)
                        yield done
            if g + 2 < groups:
                start(g + 2)

    def stack(ctx, name, width, n_rows):
        return alloc(ctx, name, [n_rows, 4, width], F32R)

    with ExitStack() as ph:
        NEG = 3 * HD
        wdv, wdl = pair(ph, "wdv", [P, DT, D]), pair(ph, "wdl", [P, DT, D])
        wcq = pair(ph, "wcq", [P, DT, CC])
        q_ring = Ring([Slot(stack(ph, f"sq{i}", T, P)) for i in range(2)])
        k_ring = Ring([Slot(stack(ph, f"sk{i}", T, P)) for i in range(2)])
        for r_, n_ in ((q_ring, "sq"), (k_ring, "sk")):
            for i, s in enumerate(r_.slots):
                s.ports = [port(f"{n_}{i}_{j}_dma") for j in range(3)]
        VW = 2 * HD
        VEND = TT * NH * VW
        v_ring = ring(ph, "sv", 1, [P, VEND + VW])
        v_rows = ring(ph, "sv_rows", 1, [P, D], dma=True)
        bufs = {"max": ring(ph, "smax", 2, [P, 4 * TT]),
                "neg": Ring([Slot(pair(ph, f"sneg{i}", [4 * TT, P]), port(f"sneg{i}_dma")) for i in range(2)]),
                "probs": ring(ph, "sprobs", 3, [P, 1280]),
                "recip": ring(ph, "srecip", 1, [32, T])}
        ctxT = alloc(ph, "ctxT", [P, DT, T])
        xs = {(x, p): alloc(ph, f"cx_{'vl'[x]}_{p}", [P, DT, T], F32R) for x in (VEXP, LEXP) for p in ("hi", "lo")}
        staging = ring(ph, "d_stage", 2, [P, D], dma=True)
        xe = ring(ph, "cxe", 1, [P, T])
        nb = norm_buffers(ph, "n2", 1)
        cn = xs
        q_out = Ring([Slot(pair(ph, "cq_out", [P, T]), port("cq_dma"))])
        for s in k_ring.slots:
            s.freed = [on_pool(lambda e, s=s: e.memset(f32(s.view[NEG:P, :, :]), 1.0))]
        for s in q_ring.slots:
            s.freed = [on_pool(lambda e, s=s: e.memset(f32(s.view[NEG:P, :, :]), 0.0))]
        vs = v_ring.slots[0]
        vs.freed = [on_pool(lambda e: e.memset(vs.view[:, :], 1.0))]
        wdv_ready = load_split(wdv, DT, lambda i: (P, ins["v_dense"][i * P:(i + 1) * P, :]), staging, D)
        wdl_ready = load_split(wdl, DT, lambda i: (P, ins["l_dense"][i * P:(i + 1) * P, :]), staging, D)
        wcq_ready = load_split(wcq, DT, lambda i: (P, ins["cq_w"][i * P:(i + 1) * P, :]), staging, CC)
        sets = Ring([Slot(psum[:, 0:3, :]), Slot(psum[:, 3:6, :])])
        outs = bank_ring(6, 2)
        at_of = {512: 0, 384: 512, 128: 896, 256: 1024}
        state = {"v_free": []}

        def load_group(g):
            b, f = divmod(g, DT)
            q, k = q_ring.take(), k_ring.take()
            ms = []
            for s, part, order in ((q, 0, (0, 1, 0)), (k, 1, (0, 0, 1))):
                for j, hl in enumerate(order):
                    src = self_qk[b, part, f, hl, :, :].rearrange("(h r) t -> r h t", h=GH)
                    ms.append(sp.dma(s.ports[j], f32(s.view[j * HD:(j + 1) * HD, :, :]), src, s.freed))
            def v_lhs(h, t):
                head = f * GH + h
                at = (t * NH + head) * VW
                return state["v"].view[:, at:at + P]

            def v_done(m):
                if f == DT - 1:
                    state["v"].freed = [m]
            return {"q": q, "k": k, "loaded": ms, "v_lhs": v_lhs, "v_ready": lambda: state["v_ready"], "v_done": v_done}

        def load_values(g):
            b, f = divmod(g, DT)
            if f == 0:
                vs = v_ring.take()
                vms = []
                for t in range(TT):
                    r_ = v_rows.take()
                    m = sp.dma(r_.port, r_.view[:, :], self_v[b, t, :, :], r_.freed)
                    dst = vs.view[:, t * NH * VW:(t + 1) * NH * VW].rearrange("p (h w) -> p h w", w=VW)[:, :, 0:HD]
                    src = r_.view[:, :].rearrange("p (h w) -> p h w", w=HD)
                    vms.append(on_pool(lambda e, dst=dst, src=src: e.tensor_copy(dst, src), m, vs.freed))
                    r_.freed = vms[-1:]
                state["v"], state["v_ready"] = vs, vms

        def flat(s):
            return s.view.rearrange("p a n -> p (a n)")

        def row_scores(s, st, h, blocks):
            def emit(e):
                for i in blocks:
                    n = P * (i + 1)
                    at = at_of[n]
                    o = flat(s)
                    e.matmul(o[:, at:at + n], st["q"].view[0:NEG, h, i * P:(i + 1) * P], st["k"].view[0:NEG, h, 0:n],
                             start=True, stop=False, skip_group_check=True)
                    last = e.matmul(o[:, at + n - P:at + n], ident16[:, :], causal[:, 0, :], start=False, stop=True,
                                    skip_group_check=True)
                return last
            return emit

        def col_scores(s, st, h, blocks):
            def emit(e):
                for j in blocks:
                    n = T - P * j
                    at = at_of[n]
                    o = flat(s)
                    e.matmul(o[:, at:at + n], st["k"].view[0:NEG + 2, h, j * P:(j + 1) * P],
                             st["q"].view[0:NEG + 2, h, j * P:T], start=True, stop=False, skip_group_check=True)
                    last = e.matmul(o[:, at:at + P], ident16[:, :], causal[:, 1, :], start=False, stop=True,
                                    skip_group_check=True)
                return last
            return emit

        views = {"row": row_scores, "col": col_scores,
                 "maxima": lambda s, blocks: [(i, flat(s)[:, at_of[P * (i + 1)]:at_of[P * (i + 1)] + P * (i + 1)])
                                              for i in blocks],
                 "used": lambda s: flat(s)[:, 0:1280]}

        def pv_blocks(blocks):
            return [(j, slice(j * P, T), slice(at_of[T - j * P], at_of[T - j * P] + T - j * P)) for j in blocks]

        ctx_ready, ctx_free = {}, []

        def finish(g, i, acc, rs, m):
            b, f = divmod(g, DT)
            m = dve.do(lambda e: e.tensor_tensor(ctxT[HD * i:HD * (i + 1), f, :], acc.view[0:HD, :], rs.view[:, :],
                                                 ALU.mult), m, ctx_free)
            ctx_ready.setdefault(b, []).append(m)
            return m

        xs_free = []
        for g in attention(B * DT, GH, sets, outs, bufs, load_group, load_values, [range(TT)], [range(TT)], SELF_SCALE, views,
                           NEG, pv_blocks, 1, finish, lag=2, early=2):
            b, f = divmod(g, DT)
            if f != DT - 1:
                continue
            xs_ready = []
            for t in range(DT):
                xs_ready += expert_split(b, ctxT[:, t, :], xs, t, xe, ctx_ready[b])
            ctx_free = xs_ready
            for f in range(DT):
                k = outs.take()
                m = pe.do(gemm(k.view, products(expert_pairs((wdv, wdl), xs, slice(f * P, f * P + P), all_cols))),
                          xs_ready, wdv_ready, wdl_ready, k.freed)
                h_ready[b] = dve.do(lambda e, f=f, k=k: e.tensor_tensor(hT[:, b, f, :], hT[:, b, f, :], k.view,
                                                                        ALU.add), m, h_ready[b])
                k.freed = [h_ready[b]]
            dense_done = m
            r, rm = rstd_of(hT[:, b, :, :], nb, outs, h_ready[b])
            cn_ready = []
            for t in range(DT):
                s = xe.take()
                m = scaled(s.view[:, :], hT[:, b, t, :], 2, t, r, rm, s.freed)
                s.freed = split(s.view[:, :], cn[VEXP, "hi"][:, t, :], cn[VEXP, "lo"][:, t, :], m, dense_done)
                cn_ready += [s.freed]
            r.freed = [m]
            for i in range(ET):
                k = outs.take()
                m = pe.do(gemm(k.view, products([(T_(wcq, all_cols, t, slice(i * P, i * P + P)),
                                                  (cn[VEXP, "hi"][:, t, :], cn[VEXP, "lo"][:, t, :]))
                                                 for t in range(DT)])), cn_ready, wcq_ready, k.freed)
                s = q_out.take()
                k.freed = split(k.view, s.view[0][:, :], s.view[1][:, :], m, s.freed)
                sp.dma(s.port, cross_q[b, i, 0, :, :], f32(s.view[0][:, :]), k.freed)
                s.freed = [sp.dma(s.port, cross_q[b, i, 1, :, :], f32(s.view[1][:, :]))]
            xs_free = [m]
        barrier()

    with ExitStack() as ph:
        NEG = 4 * CHD + 32
        wcd = pair(ph, "wcd", [P, ET, D])
        q_ring = Ring([Slot(stack(ph, f"xq{i}", T, P)) for i in range(2)])
        k_ring = Ring([Slot(stack(ph, f"xk{i}", M, P)) for i in range(2)])
        for r_, n_ in ((q_ring, "xq"), (k_ring, "xk")):
            for i, s in enumerate(r_.slots):
                s.ports = [port(f"{n_}{i}_{j}_dma") for j in range(4)]
        VW = 4 * CHD
        VEND = MT * NH * VW
        v_ring = ring(ph, "xv", 1, [P, VEND + VW])
        v_rows = ring(ph, "xv_rows", 2, [P, CC], dma=True)
        bufs = {"max": ring(ph, "xmax", 2, [P, 4 * TT]),
                "neg": Ring([Slot(pair(ph, f"xneg{i}", [4 * TT, P]), port(f"xneg{i}_dma")) for i in range(2)]),
                "probs": ring(ph, "xprobs", 6, [P, 1024]),
                "recip": ring(ph, "xrecip", 1, [32, T])}
        cctx = alloc(ph, "cctx", [P, ET, T])
        cs = pair(ph, "cctx", [P, ET, T])
        staging = ring(ph, "cd_stage", 2, [P, D], dma=True)
        for s in k_ring.slots:
            z = on_pool(lambda e, s=s: e.memset(f32(s.view[64:96, :, :]), 0.0))
            s.freed = [z, on_pool(lambda e, s=s: e.memset(f32(s.view[96:P, :, :]), 1.0))]
        for s in q_ring.slots:
            s.freed = [on_pool(lambda e, s=s: e.memset(f32(s.view[64:P, :, :]), 0.0))]
        vs = v_ring.slots[0]
        z = on_pool(lambda e: e.memset(vs.view[:, :], 0.0))
        pairs = vs.view[:, 0:VEND].rearrange("p (h o w) -> p h o w", o=2, w=VW)
        vs.freed = [on_pool(lambda e, o=o: e.memset(pairs[:, :, o, (2 + o) * CHD:(3 + o) * CHD], 1.0), z)
                    for o in range(2)]
        wcd_ready = load_split(wcd, ET, lambda i: (P, ins["cdense_w"][i * P:(i + 1) * P, :]), staging, D)
        sets = bank_ring(0, 3, 2)
        outs = bank_ring(6, 2)
        GPT = P // (4 * CHD)
        state = {}

        def load_group(g):
            b, i = divmod(g, NH // 4)
            f, part0 = i // GPT, (i % GPT) * 4 * CHD
            q, k = q_ring.take(), k_ring.take()
            ms = []
            for s, dram, order in ((q, cross_q, (0, 1, 0, 1)), (k, cross_k, (0, 0, 1, 1))):
                for j, hl in enumerate(order):
                    src = dram[b, f, hl, part0:part0 + 4 * CHD, :].rearrange("(h r) t -> r h t", h=4)
                    ms.append(sp.dma(s.ports[j], f32(s.view[j * CHD:(j + 1) * CHD, :, :]), src, s.freed))
            def v_lhs(h, t):
                at = (t * NH + i * 4 + h) * VW
                return state["v"].view[:, at:at + P]

            def v_done(m):
                if i == NH // 4 - 1:
                    state["v"].freed = [m]
            return {"q": q, "k": k, "loaded": ms, "v_lhs": v_lhs, "v_ready": lambda: state["v_ready"], "v_done": v_done}

        def load_values(g):
            b, i = divmod(g, NH // 4)
            if i == 0:
                vs = v_ring.take()
                vms = []
                for t in range(MT):
                    r_ = v_rows.take()
                    m = sp.dma(r_.port, r_.view[:, :], cross_v[b, t, :, :], r_.freed)
                    for o in range(2):
                        dst = vs.view[:, t * NH * VW:(t + 1) * NH * VW].rearrange("p (h o w) -> p h o w", o=2, w=VW)[
                            :, :, o, o * CHD:(o + 1) * CHD]
                        src = r_.view[:, :].rearrange("p (h o w) -> p h o w", o=2, w=CHD)[:, :, o, :]
                        vms.append(on_pool(lambda e, dst=dst, src=src: e.tensor_copy(dst, src), m, vs.freed))
                    r_.freed = vms[-2:]
                state["v"], state["v_ready"] = vs, vms

        def row_scores(s, st, h, blocks):
            (i,) = blocks

            def emit(e):
                for half in range(2):
                    last = e.matmul(s.view[:, half, :], st["q"].view[0:NEG, h, i * P:(i + 1) * P],
                                    st["k"].view[0:NEG, h, half * BANK:(half + 1) * BANK], start=True, stop=True)
                return last
            return emit

        def col_scores(s, st, h, blocks):
            def emit(e):
                for n, j in enumerate(blocks):
                    last = e.matmul(s.view[:, n, :], st["k"].view[0:NEG + 2, h, j * P:(j + 1) * P],
                                    st["q"].view[0:NEG + 2, h, :], start=True, stop=True)
                return last
            return emit

        views = {"row": row_scores, "col": col_scores,
                 "maxima": lambda s, blocks: [(blocks[0], s.view.rearrange("p a n -> p (a n)"))],
                 "used": lambda s: s.view.rearrange("p a n -> p (a n)")}

        def pv_blocks(blocks):
            return [(j, slice(0, T), slice(n * BANK, (n + 1) * BANK)) for n, j in enumerate(blocks)]

        ctx_ready, ctx_free, cs_free = {}, [], []

        def finish(g, two, acc, rs, m):
            b, i = divmod(g, NH // 4)
            at = 4 * CHD * (i % GPT) + 2 * CHD * two
            rows = slice(at, at + 2 * CHD)
            m = dve.do(lambda e: e.tensor_tensor(cctx[rows, i // GPT, :], acc.view[0:2 * CHD, :], rs.view[:, :],
                                                 ALU.mult), m, ctx_free)
            ctx_ready.setdefault(b, []).append(m)
            return m

        for g in attention(B * NH // 4, 4, sets, outs, bufs, load_group, load_values, [(i,) for i in range(TT)],
                           [(2 * j, 2 * j + 1) for j in range(MT // 2)], CROSS_SCALE, views,
                           NEG, pv_blocks, 2, finish, lag=4, early=2):
            b, i = divmod(g, NH // 4)
            if i != NH // 4 - 1:
                continue
            ms = split(cctx[:, :, :], cs[0][:, :, :], cs[1][:, :, :], ctx_ready[b], cs_free)
            ctx_free = ms
            for f in range(DT):
                k = outs.take()
                m = pe.do(gemm(k.view, products([(T_(wcd, all_cols, t, slice(f * P, f * P + P)),
                                                  T_(cs, all_cols, t, all_cols)) for t in range(ET)])),
                          ms, wcd_ready, k.freed)
                h_ready[b] = dve.do(lambda e, f=f, k=k, b=b: e.tensor_tensor(hT[:, b, f, :], hT[:, b, f, :], k.view,
                                                                             ALU.add), m, h_ready[b])
                k.freed = [h_ready[b]]
            cs_free = [m]
        barrier()

    with ExitStack() as ph:
        IT = -(-I // P)
        xn = pair(ph, "mn", [P, B * DT, T])
        tmp = ring(ph, "mtmp", 2, [P, T])
        nb = norm_buffers(ph, "n3", 1)
        up_w = Ring([Slot(pair(ph, f"up_w{i}", [P, 4 * DT, P])) for i in range(2)])
        down_w = Ring([Slot(pair(ph, f"down_w{i}", [P, 2, D])) for i in range(2)])
        up_stage = ring(ph, "up_stage", 2, [P, DT, P], dma=True)
        down_stage = ring(ph, "down_stage", 1, [P, D], dma=True)
        act_buf = ring(ph, "silu", 2, [P, T])
        hid = Ring([Slot([pair(ph, f"hid{i}_{x}", [P, T]) for x in "vl"]) for i in range(2)])
        gu_banks = bank_ring(0, 4)
        o_banks = bank_ring(4, 4)
        xn_ready = []
        for b in range(B):
            r, rm = rstd_of(hT[:, b, :, :], nb, gu_banks, h_ready[b])
            ms = []
            for t in range(DT):
                s = tmp.take()
                m = scaled(s.view[:, :], hT[:, b, t, :], 3, t, r, rm, s.freed)
                s.freed = split(s.view[:, :], xn[0][:, b * DT + t, :], xn[1][:, b * DT + t, :], m)
                ms += [m, s.freed]
            r.freed = [m]
            xn_ready.append(ms)

        def load_tile(i):
            n = min(P, I - i * P)
            u, d = up_w.take(), down_w.take()
            ums, dms = [], []
            for j, name in enumerate(("v_gate", "v_up", "l_gate", "l_up")):
                s = up_stage.take()
                m = sp.dma(s.port, s.view[:, :, 0:n],
                           ins[name].rearrange("(t p) i -> p t i", p=P)[:, :, i * P:i * P + n], s.freed)
                s.freed = split(s.view[:, :, 0:n], u.view[0][:, j * DT:(j + 1) * DT, 0:n],
                                u.view[1][:, j * DT:(j + 1) * DT, 0:n], m, u.freed)
                ums += [s.freed]
            for x, name in enumerate(("v_down", "l_down")):
                s = down_stage.take()
                m = sp.dma(s.port, s.view[0:n, :], ins[name][i * P:i * P + n, :], s.freed)
                s.freed = split(s.view[0:n, :], d.view[0][0:n, x, :], d.view[1][0:n, x, :], m, d.freed)
                dms += [s.freed]
            return n, u, d, ums, dms

        def hidden(b, tile):
            n, u, d, ums, dms = tile
            hd = hid.take()
            ready = []
            for x in (VEXP, LEXP):
                kg, ku = gu_banks.take(), gu_banks.take()
                done = []
                for j, k in ((2 * x, kg), (2 * x + 1, ku)):
                    done.append(pe.do(gemm(k.view[0:n, :], products(
                        [(T_(u.view, all_cols, j * DT + t, slice(0, n)), T_(xn, all_cols, b * DT + t, all_cols))
                         for t in range(DT)])), xn_ready[b], ums, k.freed))
                a = act_buf.take()
                m = act.do(lambda e, a=a, kg=kg: e.activation(a.view[0:n, :], kg.view[0:n, :], ACT.Silu),
                           done[0], a.freed)
                kg.freed = [m]
                m = dve.do(lambda e, a=a, ku=ku: e.tensor_tensor(a.view[0:n, :], ku.view[0:n, :], a.view[0:n, :],
                                                                 ALU.mult), m, done[1])
                ku.freed = [m]
                m = dve.do(lambda e, a=a, x=x: e.tensor_tensor(a.view[0:n, :], a.view[0:n, :], picked[0:n, x, b, :],
                                                               ALU.mult), m)
                a.freed = split(a.view[0:n, :], hd.view[x][0][0:n, :], hd.view[x][1][0:n, :], m, hd.freed)
                ready += [a.freed]
            u.freed = done
            return hd, ready

        def down(b, tile, hd, ready):
            n, u, d, ums, dms = tile
            for f in range(DT):
                k = o_banks.take()
                m = pe.do(gemm(k.view, products(
                    [((d.view[0][0:n, x, f * P:(f + 1) * P], d.view[1][0:n, x, f * P:(f + 1) * P]),
                      (hd.view[x][0][0:n, :], hd.view[x][1][0:n, :])) for x in (VEXP, LEXP)])),
                    ready, dms, k.freed)
                h_ready[b] = dve.do(lambda e, f=f, k=k, b=b: e.tensor_tensor(hT[:, b, f, :], hT[:, b, f, :], k.view,
                                                                             ALU.add), m, h_ready[b])
                k.freed = [h_ready[b]]
            hd.freed = [m]
            d.freed = [m]

        o_rows = ring(ph, "o_rows", 2, [P, D], dma=True)

        def write_out(b):
            for t in range(TT):
                k = o_banks.take()

                def emit(e, k=k, t=t):
                    for f in range(DT):
                        last = e.transpose(k.view[:, f * P:(f + 1) * P], hT[:, b, f, t * P:(t + 1) * P], ident[:, :])
                    return last
                m = pe.do(emit, h_ready[b], k.freed)
                s = o_rows.take()
                k.freed = [act.do(lambda e, k=k, s=s: e.activation(s.view[:, :], k.view, ACT.Copy), m, s.freed)]
                s.freed = [sp.dma(s.port, out[b, t * P:(t + 1) * P, :], s.view[:, :], k.freed)]
                stores.append(s.freed)

        pend = None
        tile = load_tile(0)
        for i in range(IT):
            for b in range(B):
                now = (b, tile, *hidden(b, tile))
                if pend:
                    down(*pend)
                    if i == IT - 1 and b > 0:
                        write_out(pend[0])
                pend = now
                if b == 1 and i + 1 < IT:
                    following = load_tile(i + 1)
            tile = following
        down(*pend)
        write_out(B - 1)
        sp.wait(stores)

    top.close()


_NAMES = {"x": "x", "ctx": "ctx_1024", "pos": "pos_1xS", "mask": "mask_BxS_ik0"}
_NAMES.update({n: "L0_xattn_" + n for n in ("W_mem", "W_gate", "b_gate", "norm_w")})
_NAMES.update({n: "L1_xattn_" + n for n in (
    "ln_in_w", "ln_post_attn_w", "ln_post_cross_w", "v_qkv", "l_qkv", "v_dense", "l_dense", "cq_w", "ckv_w",
    "cdense_w", "v_gate", "v_up", "v_down", "l_gate", "l_up", "l_down")})


def constants(T, D, NH):
    import numpy as np

    HD = D // NH
    inv = (1.0 / 10000.0 ** (np.arange(0, HD, 2, dtype=np.float32) / np.float32(HD))).astype(np.float32)
    angle = np.outer(np.arange(T, dtype=np.float32), inv).astype(np.float32)
    angle = np.tile(angle, (1, 2 * P // HD))
    rope = np.stack([np.cos(angle), np.sin(angle)]).astype(np.float32)
    turn = np.zeros((P, P), np.float32)
    for j in range(P):
        half = j % HD < HD // 2
        turn[j + HD // 2 if half else j - HD // 2, j] = -1.0 if half else 1.0
    at = np.arange(P)
    low = np.where(at[None, :] > at[:, None], -1e38, 0.0)
    return {
        "ident": np.eye(P, dtype=np.float32), "mean_w": np.full((P, P), 1.0 / D, np.float32),
        "causal": np.stack([low, low.T], axis=1).astype(np.float32),
        "rope": rope, "turn": turn,
        "row_no": (np.arange(T // P)[None, :] * P + at[:, None]).astype(np.float32),
    }


def kernel(**inputs):
    import numpy as np
    import concourse.bacc as bacc
    from concourse.bass_utils import run_bass_kernel_spmd

    nc = bacc.Bacc("TRN2", target_bir_lowering=False, num_devices=1)
    arrays, ins, const = {}, {}, {}
    for name, full in _NAMES.items():
        a = np.asarray(inputs[full])
        if a.ndim == 1:
            a = a.reshape(-1, P).T
        arrays[name + "_dram"] = np.ascontiguousarray(a)
    B, T, D = arrays["x_dram"].shape
    M, E = arrays["ctx_dram"].shape[1:]
    dims = dict(B=B, T=T, D=D, E=E, M=M, NH=16, I=arrays["v_gate_dram"].shape[1])
    for name in _NAMES:
        a = arrays[name + "_dram"]
        ins[name] = nc.dram_tensor(name + "_dram", a.shape, mybir.dt.from_np(a.dtype), kind="ExternalInput").ap()
    for name, a in constants(T, D, dims["NH"]).items():
        arrays[name + "_const"] = a
        const[name] = nc.dram_tensor(name + "_const", a.shape, mybir.dt.from_np(a.dtype), kind="ExternalInput").ap()
    out = nc.dram_tensor("out_dram", (B, T, D), F32, kind="ExternalOutput").ap()
    xattn_block(nc, dims, ins, const, out)
    r = run_bass_kernel_spmd(nc, [arrays], core_ids=[0])
    return r.results[0]["out_dram"]
```

```python
from contextlib import ExitStack

import concourse.bass as bass
from concourse import mybir

F32 = mybir.dt.float32
F32R = mybir.dt.float32r
BF16 = mybir.dt.bfloat16
I32 = mybir.dt.int32
ALU = mybir.AluOpType
ACT = mybir.ActivationFunctionType
AX = mybir.AxisListType

P = 128
BANK = 512
EPS = 1e-6


class Lane:

    def __init__(self, engine, sem):
        self.engine, self.sem, self.count, self.passed = engine, sem, 0, {}

    def wait(self, *after):
        for sem, value in marks(after):
            if self.passed.get(id(sem), 0) < value:
                self.passed[id(sem)] = value
                self.engine.wait_ge(sem, value)

    def do(self, emit, *after):
        self.wait(*after)
        self.count += 1
        emit(self.engine).then_inc(self.sem, 1)
        return (self.sem, self.count)

    def dma(self, port, out, in_, *after):
        self.wait(*after)
        port.count += 16
        self.engine.dma_start(out, in_).then_inc(port.sem, 16)
        return (port.sem, port.count)


class Port:

    def __init__(self, sem):
        self.sem, self.count = sem, 0


def marks(after):
    for a in after:
        if a is None:
            continue
        if isinstance(a, tuple) and len(a) == 2 and isinstance(a[1], int):
            yield a
        else:
            yield from marks(a)


class Slot:

    def __init__(self, view, port=None):
        self.view, self.port, self.freed = view, port, []


class Ring:
    def __init__(self, slots):
        self.slots, self.next = slots, 0

    def take(self):
        slot = self.slots[self.next % len(self.slots)]
        self.next += 1
        return slot

    def skip_to_multiple(self, n):
        self.next = -(-self.next // n) * n


def f32(ap):
    return ap.bitcast(F32)


def products(pairs):
    out = []
    for (ah, al), (bh, bl) in pairs:
        out += [(al, bh), (ah, bl), (ah, bh)]
    return out


def gemm(out, passes):
    def emit(e):
        for i, (lhsT, rhs) in enumerate(passes):
            last = e.matmul(out, lhsT, rhs, start=(i == 0), stop=(i == len(passes) - 1))
        return last
    return emit


def xattn_block(nc, dims, ins, const, out):
    B, T, D, E, M, NH, I = (dims[k] for k in ("B", "T", "D", "E", "M", "NH", "I"))
    HD, CC = D // NH, E
    CHD = CC // NH
    DT, TT, ET, MT = D // P, T // P, E // P, M // P
    assert T == BANK and D == BANK and M == 2 * BANK and HD == 32 and CHD == 16
    GH = P // HD
    L0_SCALE, SELF_SCALE, CROSS_SCALE = D ** -0.5, HD ** -0.5, CHD ** -0.5

    top = ExitStack()

    def sem(name):
        return top.enter_context(nc.semaphore(name))

    pe = Lane(nc.tensor, sem("pe_done"))
    act = Lane(nc.scalar, sem("act_done"))
    dve = Lane(nc.vector, sem("dve_done"))
    pool = Lane(nc.gpsimd, sem("pool_done"))
    sp = Lane(nc.sync, sem("sp_done"))

    all_ports = []

    def on_pool(emit, *after):
        return pool.do(emit, *after, (pool.sem, pool.count) if pool.count else None)

    def port(name):
        all_ports.append(Port(sem(name)))
        return all_ports[-1]

    def alloc(ctx, name, shape, dt=F32):
        return ctx.enter_context(nc.sbuf_tensor(name, shape, dt))

    def ring(ctx, name, n, shape, dt=F32, dma=False):
        return Ring([Slot(alloc(ctx, f"{name}{i}", shape, dt), port(f"{name}{i}_dma") if dma else None)
                     for i in range(n)])

    def pair(ctx, name, shape):
        return alloc(ctx, name + "_hi", shape, F32R), alloc(ctx, name + "_lo", shape, F32R)

    lanes = (pe, act, dve, pool, sp)
    stores = []

    def barrier():
        ends = [(x.sem, x.count) for x in lanes if x.count]
        ports = [(p.sem, p.count) for p in all_ports if p.count]
        for x in lanes:
            x.wait(ends, ports)

    psum = top.enter_context(nc.psum_tensor("psum", [P, 8, BANK], F32))

    def split(src, hi, lo, *after, copier=None):
        if copier is None:
            m_hi = act.do(lambda e: e.activation(hi, src, ACT.Copy), *after)
        else:
            m_hi = copier(hi, src, *after)
        m_lo = dve.do(lambda e: e.tensor_tensor(lo, src, f32(hi), ALU.subtract), *after, m_hi)
        return [m_hi, m_lo]

    hT = alloc(top, "hT", [P, B, DT, T])
    h_ready = [None] * B
    ident = alloc(top, "ident", [P, P])
    ident16 = alloc(top, "ident16", [P, P], BF16)
    mean_w = alloc(top, "mean_w", [P, P])
    eps_col = alloc(top, "eps_col", [P, 1])
    causal = alloc(top, "causal", [P, 2, P], BF16)
    norm_ws = alloc(top, "norm_ws", [P, 4, DT])
    gate_b = alloc(top, "gate_b", [P, DT])
    picked = alloc(top, "picked", [P, 2, B, T], BF16)
    VEXP, LEXP = 0, 1

    c_port = port("const_dma")
    for dst, src in ((ident[:, :], const["ident"]), (mean_w[:, :], const["mean_w"]),
                     (gate_b[:, :], ins["b_gate"]),
                     (norm_ws[:, 0, :], ins["norm_w"]),
                     (norm_ws[:, 1, :], ins["ln_in_w"]),
                     (norm_ws[:, 2, :], ins["ln_post_cross_w"]),
                     (norm_ws[:, 3, :], ins["ln_post_attn_w"])):
        consts = sp.dma(c_port, dst, src)
    eps_set = dve.do(lambda e: e.memset(eps_col[:, :], EPS))

    self_qk = nc.dram_tensor("self_qk", [B, 2, DT, 2, P, T], F32, kind="Internal").ap()
    self_v = nc.dram_tensor("self_v", [B, TT, P, D], F32, kind="Internal").ap()
    cross_k = nc.dram_tensor("cross_k", [B, ET, 2, P, M], F32, kind="Internal").ap()
    cross_v = nc.dram_tensor("cross_v", [B, MT, P, CC], F32, kind="Internal").ap()
    cross_q = nc.dram_tensor("cross_q", [B, ET, 2, P, T], F32, kind="Internal").ap()

    def norm_buffers(ctx, name, n=1, squares=2):
        return {"sq": ring(ctx, name + "_sq", squares, [P, T]), "rstd": ring(ctx, name + "_rstd", n, [P, T])}

    def square_sum(src, buf, *after):
        total = buf["rstd"].take()
        for t in range(DT):
            dst = buf["sq"].take() if t else total
            m = act.do(lambda e: e.activation(dst.view[:, :], src[:, t, :], ACT.Square), *after, dst.freed)
            if t == 0:
                added = m
            else:
                added = dve.do(lambda e: e.tensor_tensor(total.view[:, :], total.view[:, :], dst.view[:, :],
                                                         ALU.add), m, added)
                dst.freed = [added]
        return total, added

    def norm_rstd(total, ready, banks):
        bank = banks.take()
        m = pe.do(gemm(bank.view, [(mean_w[:, :], total.view[:, :])]), ready, bank.freed, consts)
        m = act.do(lambda e: e.activation(total.view[:, :], bank.view, ACT.Sqrt, bias=eps_col[:, 0:1]), m, eps_set)
        bank.freed = [m]
        return total, dve.do(lambda e: e.reciprocal(total.view[:, :], total.view[:, :]), m)

    def scaled(dst, src, norm, t, r, *after):
        return dve.do(lambda e: e.scalar_tensor_tensor(out=dst, in0=src, scalar=norm_ws[:, norm, t:t + 1],
                                                       in1=r.view[:, :], op0=ALU.mult, op1=ALU.mult),
                      *after, consts)

    def load_split(w, n, source, staging, width):
        out = []
        for i in range(n):
            s = staging.take()
            rows, src = source(i)
            m = sp.dma(s.port, s.view[0:rows, 0:width], src, s.freed)
            raw = s.view[0:rows, 0:width]
            ms = split(raw, w[0][0:rows, i, 0:width], w[1][0:rows, i, 0:width], m)
            s.freed = ms
            out.append(ms)
        return out

    def pick(dst, mask, kl, ml, kv, mv, *after):
        m = act.do(lambda e: e.activation(dst, kl.view, ACT.Copy), ml, *after)
        kl.freed = [m]
        m = dve.do(lambda e: e.copy_predicated(dst, mask.bitcast(mybir.dt.uint16), kv.view), m, mv)
        kv.freed = [m]
        return m

    def bank_ring(first, n, width=1):
        return Ring([Slot(psum[:, first + i * width:first + (i + 1) * width, :] if width > 1 else psum[:, first + i, :])
                     for i in range(n)])

    def T_(ap_pair, *idx):
        return ap_pair[0][idx], ap_pair[1][idx]

    every = slice(None)
    until_b = top.enter_context(ExitStack())
    cos = alloc(until_b, "cos", [P, T])
    sin = alloc(until_b, "sin", [P, T])
    turn_r = alloc(until_b, "turn_r", [P, P], F32R)
    is_v_row = alloc(until_b, "is_v_row", [P, B * TT, 1], BF16)
    with ExitStack() as ph:
        wm = pair(ph, "wm", [P, DT, E])
        wmT = pair(ph, "wmT", [P, ET, D])
        wgT = pair(ph, "wgT", [P, DT, D])
        wc = pair(ph, "wc", [P, ET, D])
        ckv = pair(ph, "ckv", [P, ET, 2 * CC])
        banks = bank_ring(0, 8)
        def load_x(b):
            h_ready[b] = sp.dma(port(f"x{b}_dma"), hT[:, b, :, :], ins["xT"][b].rearrange("(t p) n -> p t n", p=P))

        load_x(0)

        with ExitStack() as setup:
            staging = ring(setup, "wstage", 4, [P, D], dma=True)
            wg2T = pair(setup, "wg2T", [P, DT, D])

            def weight(name, dst, n, width, row=0):
                return load_split(dst, n, lambda i: (P, ins[name][(row + i) * P:(row + i + 1) * P, :]), staging, width)

            wm_ready = weight("W_mem", wm, DT, E)
            wg2T_ready = weight("W_gateT", wg2T, DT, D, DT)
            wc_ready = []
            for i in range(ET):
                bank = banks.take()
                m = pe.do(gemm(bank.view, products([(T_(wm, every, t, slice(i * P, i * P + P)),
                                                     T_(wg2T, every, t, every)) for t in range(DT)])),
                          wm_ready, wg2T_ready, bank.freed)
                bank.freed = split(bank.view, wc[0][:, i, :], wc[1][:, i, :], m)
                wc_ready.append(bank.freed)
            wgT_ready = weight("W_gateT", wgT, DT, D)
            ckv_ready = weight("ckv_w", ckv, ET, 2 * CC)
            wmT_ready = weight("W_memT", wmT, ET, D)
            causal_in = alloc(setup, "causal_in", [P, 2, P])
            m = sp.dma(port("causal_dma"), causal_in[:, :, :], const["causal"])
            dve.do(lambda e: e.tensor_copy(causal[:, :, :], causal_in[:, :, :]), m)
            dve.do(lambda e: e.tensor_copy(ident16[:, :], ident[:, :]), consts)
            types = alloc(setup, "types", [P, B, T], I32)
            types_f = alloc(setup, "types_f", [P, B, T])
            m = sp.dma(port("types_dma"), types[:, :, :].rearrange("p b t -> p (b t)"),
                       ins["mask"].rearrange("b t -> (b t)").partition_broadcast(P))
            m = dve.do(lambda e: e.tensor_scalar(types_f[:, :, :], types[:, :, :], 1.0, None, ALU.is_equal), m)
            m1 = dve.do(lambda e: e.memset(picked[:, VEXP, :, T - 1:T], 0.0))
            m2 = dve.do(lambda e: e.tensor_tensor(picked[:, VEXP, :, 0:T - 1], types_f[:, :, 0:T - 1],
                                                  types_f[:, :, 1:T], ALU.mult), m)
            picked_ready = dve.do(lambda e: e.tensor_scalar(picked[:, LEXP, :, :], picked[:, VEXP, :, :], -1.0, 1.0,
                                                            ALU.mult, ALU.add), m1, m2)
            this = alloc(setup, "this", [P, B, TT], I32)
            following = alloc(setup, "following", [P, B, TT], I32)
            f1, f2 = alloc(setup, "this_f", [P, B, TT]), alloc(setup, "following_f", [P, B, TT])
            cols = ins["mask_cols"].rearrange("p (b t) -> p b t", b=B)
            ma = sp.dma(port("this_dma"), this[:, :, :], cols)
            z = dve.do(lambda e: e.memset(following[:, :, :], 0))
            mb = sp.dma(port("next_dma"), following[0:P - 1, :, :], cols[1:P, :, :], z)
            mc = sp.dma(port("next_tile_dma"), following[P - 1:P, :, 0:TT - 1], cols[0:1, :, 1:TT], z)
            m1 = dve.do(lambda e: e.tensor_scalar(f1[:, :, :], this[:, :, :], 1.0, None, ALU.is_equal), ma)
            m2 = dve.do(lambda e: e.tensor_scalar(f2[:, :, :], following[:, :, :], 1.0, None, ALU.is_equal), mb, mc)
            rows_ready = dve.do(lambda e: e.tensor_tensor(is_v_row[:, :, 0].rearrange("p (b t) -> p b t", b=B),
                                                          f1[:, :, :], f2[:, :, :], ALU.mult), m1, m2)
            turn_raw = alloc(setup, "turn_raw", [P, P])
            table = alloc(setup, "table", [P, 2, TT, P])
            pos_i = alloc(setup, "pos_i", [P, T], I32)
            pos_f = alloc(setup, "pos_f", [P, T])
            onehot = alloc(setup, "onehot", [P, TT, T])
            row_no = alloc(setup, "row_no", [P, TT])
            m = sp.dma(port("turn_dma"), turn_raw[:, :], const["turn"])
            turn_ready = dve.do(lambda e: e.tensor_copy(turn_r[:, :], turn_raw[:, :]), m)
            tab_in = sp.dma(port("table_dma"), table[:, :, :, :], const["rope"].rearrange("a (t p) d -> p a t d", p=P))
            row_in = sp.dma(port("row_dma"), row_no[:, :], const["row_no"])
            m = sp.dma(port("pos_dma"), pos_i[:, :], ins["pos"].rearrange("a t -> (a t)").partition_broadcast(P))
            m = dve.do(lambda e: e.tensor_scalar(pos_f[:, :], pos_i[:, :], 0.0, float(T - 1), ALU.max, ALU.min), m)
            for t in range(TT):
                hot = dve.do(lambda e: e.tensor_scalar(onehot[:, t, :], pos_f[:, :], row_no[:, t:t + 1], None,
                                                       ALU.is_equal), m, row_in)
            for a, dst in enumerate((cos, sin)):
                k = banks.take()
                m = pe.do(gemm(k.view, [(table[:, a, t, :], onehot[:, t, :]) for t in range(TT)]), hot, tab_in,
                          k.freed)
                rope_ready = act.do(lambda e: e.activation(dst[:, :], k.view, ACT.Copy), m)
                k.freed = [rope_ready]
        barrier()

        mem_in = ring(ph, "mem_in", 2, [P, T], dma=True)
        xT = pair(ph, "xT", [P, DT, T])
        mem = pair(ph, "mem", [P, MT, E])
        memT = pair(ph, "memT", [P, ET, M])
        k_out = Ring([Slot(pair(ph, "k_out", [P, BANK]), port("k_dma"))])
        v_out = ring(ph, "v_out", 1, [P, CC], dma=True)
        qT = pair(ph, "qT", [P, ET, T])
        zx = alloc(ph, "zx", [P, DT, T])
        probs = ring(ph, "probs", 1, [P, M])
        probsT = pair(ph, "probsT", [P, MT, T])
        gates = ring(ph, "gate", 1, [P, T])
        stat = ring(ph, "stat", 2, [P, 4])
        nb = {"sq": gates, "rstd": ring(ph, "n0_rstd", 1, [P, T])}
        free = {"xT": [], "mem": [], "memT": [], "probsT": [], "qT": [], "zx": []}
        for b in range(1, B):
            load_x(b)
        ready = {}

        def take_x(b):
            ready["x"] = [split(hT[:, b, t, :], xT[0][:, t, :], xT[1][:, t, :], h_ready[b], free["xT"])
                          for t in range(DT)]

        def take_memT(b):
            ready["memT"] = []
            for f in range(ET):
                for half in range(2):
                    s = mem_in.take()
                    cols = slice(half * T, (half + 1) * T)
                    m = sp.dma(s.port, s.view[:, :], ins["ctxT"][b, f * P:(f + 1) * P, cols], s.freed)
                    s.freed = split(s.view[:, :], memT[0][:, f, cols], memT[1][:, f, cols], m, free["memT"])
                    ready["memT"] += [s.freed]

        def take_mem(b):
            ready["mem"] = []
            for quarter in range(4):
                s = mem_in.take()
                tiles = slice(quarter * MT // 4, (quarter + 1) * MT // 4)
                src = ins["ctx"][b].rearrange("(t p) e -> p t e", p=P)[:, tiles, :]
                view = s.view[:, :].rearrange("p (t e) -> p t e", e=E)
                m = sp.dma(s.port, view, src, s.freed)
                s.freed = split(view, mem[0][:, tiles, :], mem[1][:, tiles, :], m, free["mem"], copier=pool_copy)
                ready["mem"] += [s.freed]

        def gate_share(f):
            k = banks.take()
            m = pe.do(gemm(k.view, products([(T_(wgT, every, t, slice(f * P, f * P + P)), T_(xT, every, t, every))
                                             for t in range(DT)])), ready["x"], k.freed)
            k.freed = [act.do(lambda e: e.activation(zx[:, f, :], k.view, ACT.Copy), m, free["zx"])]
            ready["zx"] = k.freed
            free["xT"] = [m]

        def cross_keys(b, i, half):
            cols = slice(half * BANK, (half + 1) * BANK)
            k = banks.take()
            m = pe.do(gemm(k.view, products([(T_(ckv, every, t, slice(i * P, i * P + P)), T_(memT, every, t, cols))
                                             for t in range(ET)])), ready["memT"], k.freed)
            s = k_out.take()
            k.freed = split(k.view, s.view[0][:, :], s.view[1][:, :], m, s.freed)
            sp.dma(s.port, cross_k[b, i, 0, :, cols], f32(s.view[0][:, :]), k.freed)
            s.freed = [sp.dma(s.port, cross_k[b, i, 1, :, cols], f32(s.view[1][:, :]))]

        def cross_values(b, mt):
            k = banks.take()
            m = pe.do(gemm(k.view[:, 0:CC], products([(T_(memT, every, t, slice(mt * P, mt * P + P)),
                                                       T_(ckv, every, t, slice(CC, 2 * CC))) for t in range(ET)])),
                      ready["memT"], k.freed)
            s = v_out.take()
            k.freed = [act.do(lambda e: e.activation(s.view[:, :], k.view[:, 0:CC], ACT.Copy), m, s.freed)]
            s.freed = [sp.dma(s.port, cross_v[b, mt, :, :], s.view[:, :], k.freed)]

        def scores(qt):
            banks.skip_to_multiple(2)
            at = banks.next % 8
            both = psum[:, at:at + 2, :]
            two = [banks.take(), banks.take()]
            for half, k in enumerate(two):
                scored = pe.do(gemm(k.view, products([(T_(qT, every, t, slice(qt * P, (qt + 1) * P)),
                                                       T_(memT, every, t, slice(half * BANK, (half + 1) * BANK)))
                                                      for t in range(ET)])), ready["q"], ready["memT"], k.freed)
            st, p = stat.take(), probs.take()
            c = st.view
            m = dve.do(lambda e: e.tensor_reduce(c[:, 0:1], both, AX.XY, ALU.max), scored, st.freed)
            m = dve.do(lambda e: e.tensor_scalar(c[:, 1:2], c[:, 0:1], -L0_SCALE, None, ALU.mult), m)
            m = act.do(lambda e: e.activation(p.view[:, :].rearrange("p (a n) -> p a n", a=2), both, ACT.Exp,
                                              bias=c[:, 1:2], scale=L0_SCALE, accum_out=c[:, 2:3]), m, p.freed)
            for k in two:
                k.freed = [m]
            m = dve.do(lambda e: e.reciprocal(c[:, 3:4], c[:, 2:3]), m)
            m = dve.do(lambda e: e.tensor_scalar(p.view[:, :], p.view[:, :], c[:, 3:4], None, ALU.mult), m)
            st.freed = [m]
            return p, m, scored

        def turn_probs(qt, p, ready_p):
            out = []
            for half in range(2):
                k = banks.take()

                def emit(e):
                    for j in range(4):
                        at = (4 * half + j) * P
                        last = e.transpose(k.view[:, j * P:(j + 1) * P], p.view[:, at:at + P], ident[:, :])
                    return last
                turned = pe.do(emit, ready_p, k.freed)
                dst = slice(4 * half, 4 * half + 4), slice(qt * P, (qt + 1) * P)
                k.freed = split(k.view.rearrange("p (j n) -> p j n", j=4), probsT[0][:, dst[0], dst[1]],
                                probsT[1][:, dst[0], dst[1]], turned, free["probsT"])
                out.append(k.freed)
            p.freed = [turned]
            return out

        def pool_copy(hi, src, *after):
            return on_pool(lambda e: e.tensor_copy(hi, src), *after)

        take_x(0)
        take_memT(0)
        rms = None
        for b in range(B):
            ready["q"] = []
            for i in range(ET):
                k = banks.take()
                m = pe.do(gemm(k.view, products([(T_(wm, every, t, slice(i * P, i * P + P)), T_(xT, every, t, every))
                                                 for t in range(DT)])), ready["x"], k.freed)
                k.freed = split(k.view, qT[0][:, i, :], qT[1][:, i, :], m, free["qT"])
                ready["q"] += [k.freed]
            if rms:
                finish_norm(*rms)
            take_mem(b)
            free["probsT_in"] = []
            for qt in range(TT):
                p, m, scored = scores(qt)
                gate_share(qt)
                cross_keys(b, qt // 2, qt % 2)
                for mt in (2 * qt, 2 * qt + 1):
                    cross_values(b, mt)
                free["probsT_in"] += turn_probs(qt, p, m)
            free["memT"] = [(pe.sem, pe.count)]
            if b + 1 < B:
                take_x(b + 1)
                take_memT(b + 1)
            a_ready = []
            for i in range(ET):
                k = banks.take()
                m = pe.do(gemm(k.view, products([(T_(mem, every, t, slice(i * P, i * P + P)),
                                                  T_(probsT, every, t, every)) for t in range(MT)])),
                          ready["mem"], free["probsT_in"], k.freed)
                k.freed = split(k.view, qT[0][:, i, :], qT[1][:, i, :], m, scored)
                a_ready += [k.freed]
            free["probsT"] = free["mem"] = [m]
            for f in range(DT):
                fcols = slice(f * P, (f + 1) * P)
                kz, kc = banks.take(), banks.take()
                mz = pe.do(gemm(kz.view, products([(T_(wc, every, t, fcols), T_(qT, every, t, every))
                                                   for t in range(ET)])), a_ready, kz.freed)
                mc = pe.do(gemm(kc.view, products([(T_(wmT, every, t, fcols), T_(qT, every, t, every))
                                                   for t in range(ET)])), a_ready, kc.freed)
                g = gates.take()
                m = dve.do(lambda e: e.tensor_tensor(g.view[:, :], kz.view, zx[:, f, :], ALU.add),
                           mz, ready["zx"], g.freed)
                kz.freed = [m]
                free["zx"] = [m]
                m = act.do(lambda e: e.activation(g.view[:, :], g.view[:, :], ACT.Sigmoid, bias=gate_b[:, f:f + 1]),
                           m)
                m = dve.do(lambda e: e.tensor_tensor(g.view[:, :], kc.view, g.view[:, :], ALU.mult), m, mc)
                kc.freed = [m]
                h_ready[b] = dve.do(lambda e: e.tensor_tensor(hT[:, b, f, :], hT[:, b, f, :], g.view[:, :],
                                                              ALU.add), m, h_ready[b])
                g.freed = [h_ready[b]]
            free["qT"] = [mc]

            def finish_norm(b, total, m):
                r, m = norm_rstd(total, m, banks)
                for f in range(DT):
                    h_ready[b] = scaled(hT[:, b, f, :], hT[:, b, f, :], 0, f, r, m)
                r.freed = [h_ready[b]]
            rms = (b, *square_sum(hT[:, b, :, :], nb, h_ready[b]))
        finish_norm(*rms)
        barrier()

    with ExitStack() as ph:
        W3 = 3 * D
        wv = pair(ph, "wv_qkv", [P, DT, W3])
        wl = pair(ph, "wl_qkv", [P, DT, W3])
        staging = ring(ph, "qkv_stage", 2, [P, D], dma=True)
        banks = bank_ring(0, 8)
        xs = Ring([Slot(pair(ph, f"xn{i}", [P, DT, T])) for i in range(2)])
        tmp = ring(ph, "xn_tmp", 1, [P, T])
        nb = norm_buffers(ph, "n1", squares=1)
        raw = ring(ph, "raw", 2, [P, T])
        raw_hl = Ring([Slot(pair(ph, "raw_hl", [P, T]))])
        prod = ring(ph, "prod", 1, [P, T])
        qk_out = Ring([Slot(pair(ph, f"qk{i}", [P, T]), port(f"qk{i}_dma")) for i in range(2)])
        v_out = ring(ph, "sv_out", 1, [P, D], dma=True)

        w_ready = {}

        def load_part(part):
            cols = slice(part * D, (part + 1) * D)
            for x, w, name in ((LEXP, wl, "l_qkv"), (VEXP, wv, "v_qkv")):
                w_ready[x, part] = []
                for t in range(DT):
                    s = staging.take()
                    m = sp.dma(s.port, s.view[:, :], ins[name][t * P:(t + 1) * P, cols], s.freed)
                    s.freed = split(s.view[:, :], w[0][:, t, cols], w[1][:, t, cols], m)
                    w_ready[x, part] += [s.freed]

        def normed(b):
            r, rm = norm_rstd(*square_sum(hT[:, b, :, :], nb, h_ready[b]), banks)
            x = xs.take()
            x.ready = []
            for t in range(DT):
                s = tmp.take()
                m = scaled(s.view[:, :], hT[:, b, t, :], 1, t, r, rm, s.freed)
                s.freed = split(s.view[:, :], x.view[0][:, t, :], x.view[1][:, t, :], m, x.freed)
                x.ready += [s.freed]
            r.freed = [m]
            return x

        def expert_banks(x, wcols, xcols, part, rows):
            out = []
            for expert, w in ((LEXP, wl), (VEXP, wv)):
                k = banks.take()
                pairs = [(T_(w, every, t, wcols), T_(x.view, every, t, xcols)) for t in range(DT)]
                m = pe.do(gemm(k.view, products([(c, a) for a, c in pairs] if rows else pairs)),
                          x.ready, w_ready[expert, part], k.freed)
                out.append((k, m))
            return out

        def rotate(b, part, f, s, hl, ms):
            kr = banks.take()
            mr = pe.do(gemm(kr.view, [(turn_r[:, :], hl.view[1][:, :]), (turn_r[:, :], hl.view[0][:, :])]),
                       ms, kr.freed)
            hl.freed = [mr]
            p = prod.take()
            m1 = dve.do(lambda e: e.tensor_tensor(s.view[:, :], s.view[:, :], cos[:, :], ALU.mult), ms)
            m2 = dve.do(lambda e: e.tensor_tensor(p.view[:, :], kr.view, sin[:, :], ALU.mult), mr, p.freed)
            kr.freed = [m2]
            m = on_pool(lambda e: e.tensor_tensor(s.view[:, :], s.view[:, :], p.view[:, :], ALU.add), m1, m2)
            p.freed = [m]
            o = qk_out.take()
            s.freed = split(s.view[:, :], o.view[0][:, :], o.view[1][:, :], m, o.freed)
            sp.dma(o.port, self_qk[b, part, f, 0, :, :], f32(o.view[0][:, :]), s.freed)
            o.freed = [sp.dma(o.port, self_qk[b, part, f, 1, :, :], f32(o.view[1][:, :]))]

        x = normed(0)
        load_part(0)
        turning = None
        for b in range(B):
            for i in range(2 * DT):
                part, f = divmod(i, DT)
                (kl, ml), (kv, mv) = expert_banks(x, slice(part * D + f * P, part * D + (f + 1) * P), every, part,
                                                  False)
                if turning:
                    rotate(*turning)
                s = raw.take()
                m = pick(s.view[:, :], picked[:, VEXP, b, :], kl, ml, kv, mv, s.freed)
                hl = raw_hl.take()
                turning = (b, part, f, s, hl, split(s.view[:, :], hl.view[0][:, :], hl.view[1][:, :], m, hl.freed))
                if b == 0 and i in (1, 4):
                    load_part(1 + i // 4)
                if b + 1 < B and i == 4:
                    following_x = normed(b + 1)
            for t in range(TT):
                (kl, ml), (kv, mv) = expert_banks(x, slice(2 * D, W3), slice(t * P, (t + 1) * P), 2, True)
                if t == 0:
                    rotate(*turning)
                    turning = None
                s = v_out.take()
                mask = is_v_row[:, b * TT + t, :].to_broadcast([P, D])
                m = pick(s.view[:, :], mask, kl, ml, kv, mv, s.freed)
                s.freed = [sp.dma(s.port, self_v[b, t, :, :], s.view[:, :], m)]
            x.freed = [mv]
            x = following_x
        barrier()
    until_b.close()

    def attention(groups, G, score_sets, accs, misc, bufs, load_group, row_blocks, col_blocks, scale,
                  set_views, neg_rows, pv_blocks, heads_per_out, finish, side, lag, group_slots, rows_by):
        stage = {}
        closing = []

        chunks = len(col_blocks)
        units = G * chunks

        def rows_of(g, unit):
            st = stage[g]
            h, c = divmod(unit, chunks)
            s = score_sets.take()
            m = pe.do(set_views["row"](s, st, h, row_blocks[c]), st["loaded"], s.freed)
            s.freed = [dve.do(lambda e: e.tensor_reduce(
                st["max"].view[:, h * TT + col:h * TT + col + 1], view, AX.X, ALU.max), m, st["max"].freed)
                for col, view in set_views["maxima"](s, row_blocks[c])]
            st["maxed"] += s.freed

        def maxima_to_rows(g):
            st = stage[g]
            k = misc.take()
            n = G * TT
            m = pe.do(lambda e: e.transpose(k.view[0:n, 0:P], st["max"].view[:, 0:n], ident[:, :]),
                      st["maxed"], k.freed)
            st["max"].freed = [m]
            neg = bufs["neg"].take()
            m1 = dve.do(lambda e: e.tensor_scalar(neg.view[0][0:n, :], k.view[0:n, 0:P], -1.0, None, ALU.mult),
                        m, neg.freed)
            m2 = dve.do(lambda e: e.scalar_tensor_tensor(out=neg.view[1][0:n, :], in0=k.view[0:n, 0:P], scalar=-1.0,
                                                         in1=f32(neg.view[0][0:n, :]), op0=ALU.mult,
                                                         op1=ALU.subtract), m1)
            k.freed = [m1, m2]
            for part in range(2):
                row = f32(st["q"].view[neg_rows + part:neg_rows + part + 1, :, :]).rearrange(
                    "o h (t n) -> o (h t) n", n=P)
                st["neg_in"] = sp.dma(neg.port, row, f32(neg.view[part][0:n, :]), m1, m2)
            neg.freed = [st["neg_in"]]

        def exps(g, unit):
            st = stage[g]
            h, c = divmod(unit, chunks)
            s = score_sets.take()
            m = pe.do(set_views["col"](s, st, h, col_blocks[c]), st["neg_in"], s.freed)
            p = bufs["probs"].take()
            s.freed = [act.do(lambda e: e.activation(p.view[:, :], set_views["used"](s), ACT.Exp, scale=scale),
                              m, p.freed)]
            if unit == units - 1:
                st["q"].freed = st["k"].freed = [m]
            return p, s.freed

        def values(g, unit, p, ready):
            st = stage[g]
            h, c = divmod(unit, chunks)
            first = h % heads_per_out == 0 and c == 0
            last = h % heads_per_out == heads_per_out - 1 and c == chunks - 1
            if first:
                st["acc"] = accs.take()
            acc = st["acc"]
            parts = list(pv_blocks(col_blocks[c]))

            def emit(e):
                for n, (block, cols, pcols) in enumerate(parts):
                    x = e.matmul(acc.view[:, cols], st["v_lhs"](h, block), p.view[:, pcols],
                                 start=first and n == 0, stop=last and n == len(parts) - 1, skip_group_check=True)
                return x
            m = pe.do(emit, ready, st["v_ready"], acc.freed if first else None)
            p.freed = [m]
            if last:
                n = (g * G + h) // heads_per_out
                rows = slice(32 * (n % 4), 32 * (n % 4) + 32)
                if n % 4 == 0:
                    stage["o"] = bufs["ctx"].take(), bufs["sums"].take(), []
                ctx, sums, ms = stage["o"]
                m1 = act.do(lambda e: e.activation(ctx.view[rows, :], acc.view[0:32, :], ACT.Copy), m, ctx.freed)
                m2 = dve.do(lambda e: e.tensor_copy(sums.view[rows, :], acc.view[32:64, :]), m, sums.freed)
                acc.freed = [m1, m2]
                ms += [m1, m2]
                if n % 4 == 3:
                    closing.append(close(n // 4, ctx, sums, ms))
            return m

        def close(n, ctx, sums, ms):
            for half in range(2):
                cols = slice(half * T // 2, (half + 1) * T // 2)
                ms = [dve.do(lambda e: e.reciprocal(sums.view[:, cols], sums.view[:, cols]), ms)]
                yield
            m = dve.do(lambda e: e.tensor_tensor(ctx.view[:, :], ctx.view[:, :], sums.view[:, :], ALU.mult), ms)
            sums.freed = [m]
            yield from finish(n, ctx, m)

        def start(g):
            stage[g] = load_group(g)
            stage[g]["max"] = bufs["max"].take()
            stage[g]["maxed"] = []

        for g in range(min(groups, group_slots)):
            start(g)
        rows_done, due, waiting = 0, [], []
        for n in range(groups * units):
            g, unit = divmod(n, units)
            turning, due = due, []
            while rows_done < min(groups * units, rows_by(n)):
                rows_of(*divmod(rows_done, units))
                rows_done += 1
                if rows_done % units == 0:
                    (due if rows_done > n + units else turning).append(rows_done // units - 1)
            for ready_group in turning:
                maxima_to_rows(ready_group)
            waiting.append((g, unit, *exps(g, unit)))
            if unit == units - 1 and g + group_slots < groups:
                start(g + group_slots)
            while len(waiting) > lag or (waiting and n == groups * units - 1):
                done, at, *operands = waiting.pop(0)
                m = values(done, at, *operands)
                if at == units - 1:
                    stage[done]["v_done"](m)
                for tasks in (side, closing):
                    for task in tasks[:1]:
                        if next(task, "over") == "over":
                            tasks.remove(task)
        drain(closing)
        drain(side)

    def drain(tasks):
        while tasks:
            for _ in tasks.pop(0):
                pass

    def stack(ctx, name, width, n_rows):
        return alloc(ctx, name, [n_rows, 4, width], F32R)

    with ExitStack() as ph:
        NEG = 3 * HD
        wdv, wdl = pair(ph, "wdv", [P, DT, D]), pair(ph, "wdl", [P, DT, D])
        q_ring = Ring([Slot(stack(ph, f"sq{i}", T, P)) for i in range(3)])
        k_ring = Ring([Slot(stack(ph, f"sk{i}", T, P)) for i in range(3)])
        for r_, n_ in ((q_ring, "sq"), (k_ring, "sk")):
            for i, s in enumerate(r_.slots):
                s.ports = [port(f"{n_}{i}_{j}_dma") for j in range(3)]
        VW = 2 * HD
        VEND = TT * NH * VW
        v_ring = ring(ph, "sv", 2, [P, VEND + VW])
        v_rows = ring(ph, "sv_rows", 1, [P, D], dma=True)
        bufs = {"max": ring(ph, "smax", 3, [P, 4 * TT]),
                "neg": Ring([Slot(pair(ph, f"sneg{i}", [4 * TT, P]), port(f"sneg{i}_dma")) for i in range(2)]),
                "probs": ring(ph, "sprobs", 3, [P, 1280]),
                "sums": ring(ph, "ssums", 2, [P, T]), "ctx": ring(ph, "sctx", 2, [P, T])}
        xs = pair(ph, "cx", [P, DT, T])
        xe = ring(ph, "cxe", 2, [P, T], dma=True)
        for s in k_ring.slots:
            s.freed = [on_pool(lambda e, s=s: e.memset(f32(s.view[NEG:P, :, :]), 1.0))]
        for s in q_ring.slots:
            s.freed = [on_pool(lambda e, s=s: e.memset(f32(s.view[NEG:P, :, :]), 0.0))]
        for vs in v_ring.slots:
            vs.freed = [on_pool(lambda e: e.memset(vs.view[:, :], 1.0))]
        wdv_ready = load_split(wdv, DT, lambda i: (P, ins["v_dense"][i * P:(i + 1) * P, :]), xe, D)
        wdl_ready = load_split(wdl, DT, lambda i: (P, ins["l_dense"][i * P:(i + 1) * P, :]), xe, D)
        sets = Ring([Slot(psum[:, 0:3, :]), Slot(psum[:, 3:6, :])])
        outs = bank_ring(6, 2)
        at_of = {512: 0, 384: 512, 128: 896, 256: 1024}
        state = {}

        def load_group(g):
            b, f = divmod(g, DT)
            q, k = q_ring.take(), k_ring.take()
            ms = []
            for s, part, order in ((q, 0, (0, 1, 0)), (k, 1, (0, 0, 1))):
                for j, hl in enumerate(order):
                    src = self_qk[b, part, f, hl, :, :].rearrange("(h r) t -> r h t", h=GH)
                    ms.append(sp.dma(s.ports[j], f32(s.view[j * HD:(j + 1) * HD, :, :]), src, s.freed))
            def v_lhs(h, t):
                head = f * GH + h
                at = (t * NH + head) * VW
                return vs.view[:, at:at + P]

            def v_done(m):
                if f == DT - 1:
                    vs.freed = [m]
            vs, v_ready = values_of(b, f)
            return {"q": q, "k": k, "loaded": ms, "v_lhs": v_lhs, "v_ready": v_ready, "v_done": v_done}

        def values_of(b, f):
            if f == 0:
                vs = v_ring.take()
                vms = []
                for t in range(TT):
                    r_ = v_rows.take()
                    m = sp.dma(r_.port, r_.view[:, :], self_v[b, t, :, :], r_.freed)
                    dst = vs.view[:, t * NH * VW:(t + 1) * NH * VW].rearrange("p (h w) -> p h w", w=VW)[:, :, 0:HD]
                    src = r_.view[:, :].rearrange("p (h w) -> p h w", w=HD)
                    vms.append(on_pool(lambda e, dst=dst, src=src: e.tensor_copy(dst, src), m, vs.freed))
                    r_.freed = vms[-1:]
                state["v"] = vs, vms
            return state["v"]

        def flat(s):
            return s.view.rearrange("p a n -> p (a n)")

        def row_scores(s, st, h, blocks):
            def emit(e):
                for i in blocks:
                    n = P * (i + 1)
                    at = at_of[n]
                    o = flat(s)
                    e.matmul(o[:, at:at + n], st["q"].view[0:NEG, h, i * P:(i + 1) * P], st["k"].view[0:NEG, h, 0:n],
                             start=True, stop=False, skip_group_check=True)
                    last = e.matmul(o[:, at + n - P:at + n], ident16[:, :], causal[:, 0, :], start=False, stop=True,
                                    skip_group_check=True)
                return last
            return emit

        def col_scores(s, st, h, blocks):
            def emit(e):
                for j in blocks:
                    n = T - P * j
                    at = at_of[n]
                    o = flat(s)
                    e.matmul(o[:, at:at + n], st["k"].view[0:NEG + 2, h, j * P:(j + 1) * P],
                             st["q"].view[0:NEG + 2, h, j * P:T], start=True, stop=False, skip_group_check=True)
                    last = e.matmul(o[:, at:at + P], ident16[:, :], causal[:, 1, :], start=False, stop=True,
                                    skip_group_check=True)
                return last
            return emit

        views = {"row": row_scores, "col": col_scores,
                 "maxima": lambda s, blocks: [(i, flat(s)[:, at_of[P * (i + 1)]:at_of[P * (i + 1)] + P * (i + 1)])
                                              for i in blocks],
                 "used": lambda s: flat(s)[:, 0:1280]}

        def pv_blocks(blocks):
            return [(j, slice(j * P, T), slice(at_of[T - j * P], at_of[T - j * P] + T - j * P)) for j in blocks]

        xs_free, xs_ready, side = [], {}, []

        def finish(n, ctx, m):
            b, f = divmod(n, DT)
            yield
            if f == 0:
                drain(side)
            ctx.freed = split(ctx.view[:, :], xs[0][:, f, :], xs[1][:, f, :], m, xs_free)
            xs_ready.setdefault(b, []).append(ctx.freed)
            if f == DT - 1:
                side.append(dense(b))

        def dense(b):
            for f in range(DT):
                yield
                both = []
                for w, w_ready in ((wdl, wdl_ready), (wdv, wdv_ready)):
                    k = outs.take()
                    pairs = [(T_(w, every, t, slice(f * P, (f + 1) * P)), T_(xs, every, t, every)) for t in range(DT)]
                    both.append((k, pe.do(gemm(k.view, products(pairs)), xs_ready[b], w_ready, k.freed)))
                (kl, ml), (kv, mv) = both
                s = xe.take()
                m = pick(s.view[:, :], picked[:, VEXP, b, :], kl, ml, kv, mv, s.freed)
                h_ready[b] = dve.do(lambda e: e.tensor_tensor(hT[:, b, f, :], hT[:, b, f, :], s.view[:, :], ALU.add),
                                    m, h_ready[b])
                s.freed = [h_ready[b]]
            xs_free[:] = [mv]

        attention(B * DT, GH, sets, outs, outs, bufs, load_group, [range(TT)], [range(TT)],
                  SELF_SCALE, views, NEG, pv_blocks, 1, finish, side, lag=2, group_slots=3,
                  rows_by=lambda n: n + GH + 3)
        barrier()

    with ExitStack() as ph:
        wcq = pair(ph, "wcq", [P, DT, CC])
        staging = ring(ph, "cq_stage", 4, [P, CC], dma=True)
        nb = norm_buffers(ph, "n2", n=B)
        tmp = ring(ph, "cn_tmp", 2, [P, T])
        cns = Ring([Slot(pair(ph, f"cn{i}", [P, DT, T])) for i in range(2)])
        q_out = Ring([Slot(pair(ph, f"cq{i}", [P, T]), port(f"cq{i}_dma")) for i in range(2)])
        banks = bank_ring(0, 8)
        wcq_ready = load_split(wcq, DT, lambda i: (P, ins["cq_w"][i * P:(i + 1) * P, :]), staging, CC)
        sums = [square_sum(hT[:, b, :, :], nb, h_ready[b]) for b in range(B)]
        for b in range(B):
            r, rm = norm_rstd(*sums[b], banks)
            cn = cns.take()
            ms = []
            for t in range(DT):
                s = tmp.take()
                m = scaled(s.view[:, :], hT[:, b, t, :], 2, t, r, rm, s.freed)
                s.freed = split(s.view[:, :], cn.view[0][:, t, :], cn.view[1][:, t, :], m, cn.freed)
                ms += [s.freed]
            for i in range(ET):
                k = banks.take()
                m = pe.do(gemm(k.view, products([(T_(wcq, every, t, slice(i * P, i * P + P)),
                                                  T_(cn.view, every, t, every)) for t in range(DT)])),
                          ms, wcq_ready, k.freed)
                s = q_out.take()
                k.freed = split(k.view, s.view[0][:, :], s.view[1][:, :], m, s.freed)
                sp.dma(s.port, cross_q[b, i, 0, :, :], f32(s.view[0][:, :]), k.freed)
                s.freed = [sp.dma(s.port, cross_q[b, i, 1, :, :], f32(s.view[1][:, :]))]
            cn.freed = [m]
        barrier()

    with ExitStack() as ph:
        NEG = 4 * CHD + 32
        wcd = pair(ph, "wcd", [P, ET, D])
        q_ring = Ring([Slot(stack(ph, f"xq{i}", T, P)) for i in range(2)])
        k_ring = Ring([Slot(stack(ph, f"xk{i}", M, P)) for i in range(2)])
        for r_, n_ in ((q_ring, "xq"), (k_ring, "xk")):
            for i, s in enumerate(r_.slots):
                s.ports = [port(f"{n_}{i}_{j}_dma") for j in range(4)]
        VW = 4 * CHD
        VEND = MT * NH * VW
        v_ring = ring(ph, "xv", 2, [P, VEND + VW])
        v_rows = ring(ph, "xv_rows", 2, [P, CC], dma=True)
        bufs = {"max": ring(ph, "xmax", 2, [P, 4 * TT]),
                "neg": Ring([Slot(pair(ph, f"xneg{i}", [4 * TT, P]), port(f"xneg{i}_dma")) for i in range(2)]),
                "probs": ring(ph, "xprobs", 5, [P, 1024]),
                "sums": ring(ph, "xsums", 1, [P, T]), "ctx": ring(ph, "xctx", 2, [P, T])}
        cs = pair(ph, "cctx", [P, ET, T])
        staging = ring(ph, "cd_stage", 2, [P, D], dma=True)
        for s in k_ring.slots:
            z = on_pool(lambda e, s=s: e.memset(f32(s.view[64:96, :, :]), 0.0))
            s.freed = [z, on_pool(lambda e, s=s: e.memset(f32(s.view[96:P, :, :]), 1.0))]
        for s in q_ring.slots:
            s.freed = [on_pool(lambda e, s=s: e.memset(f32(s.view[64:P, :, :]), 0.0))]
        for vs in v_ring.slots:
            z = on_pool(lambda e: e.memset(vs.view[:, :], 0.0))
            pairs = vs.view[:, 0:VEND].rearrange("p (h o w) -> p h o w", o=2, w=VW)
            vs.freed = [on_pool(lambda e: e.memset(pairs[:, :, o, (2 + o) * CHD:(3 + o) * CHD], 1.0), z)
                        for o in range(2)]
        wcd_ready = load_split(wcd, ET, lambda i: (P, ins["cdense_w"][i * P:(i + 1) * P, :]), staging, D)
        sets = bank_ring(0, 3, 2)
        accs, outs = bank_ring(6, 1), bank_ring(7, 1)
        GPT = P // (4 * CHD)
        state = {}

        def load_group(g):
            b, i = divmod(g, NH // 4)
            f, part0 = i // GPT, (i % GPT) * 4 * CHD
            q, k = q_ring.take(), k_ring.take()
            ms = []
            for s, dram, order in ((q, cross_q, (0, 1, 0, 1)), (k, cross_k, (0, 0, 1, 1))):
                for j, hl in enumerate(order):
                    src = dram[b, f, hl, part0:part0 + 4 * CHD, :].rearrange("(h r) t -> r h t", h=4)
                    ms.append(sp.dma(s.ports[j], f32(s.view[j * CHD:(j + 1) * CHD, :, :]), src, s.freed))
            def v_lhs(h, t):
                at = (t * NH + i * 4 + h) * VW
                return vs.view[:, at:at + P]

            def v_done(m):
                if i == NH // 4 - 1:
                    vs.freed = [m]
            vs, v_ready = values_of(b, i)
            return {"q": q, "k": k, "loaded": ms, "v_lhs": v_lhs, "v_ready": v_ready, "v_done": v_done}

        def values_of(b, i):
            if i == 0:
                vs = v_ring.take()
                vms = []
                for t in range(MT):
                    r_ = v_rows.take()
                    m = sp.dma(r_.port, r_.view[:, :], cross_v[b, t, :, :], r_.freed)
                    for o in range(2):
                        dst = vs.view[:, t * NH * VW:(t + 1) * NH * VW].rearrange("p (h o w) -> p h o w", o=2, w=VW)[
                            :, :, o, o * CHD:(o + 1) * CHD]
                        src = r_.view[:, :].rearrange("p (h o w) -> p h o w", o=2, w=CHD)[:, :, o, :]
                        vms.append(on_pool(lambda e, dst=dst, src=src: e.tensor_copy(dst, src), m, vs.freed))
                    r_.freed = vms[-2:]
                state["v"] = vs, vms
            return state["v"]

        def row_scores(s, st, h, blocks):
            (i,) = blocks

            def emit(e):
                for half in range(2):
                    last = e.matmul(s.view[:, half, :], st["q"].view[0:NEG, h, i * P:(i + 1) * P],
                                    st["k"].view[0:NEG, h, half * BANK:(half + 1) * BANK], start=True, stop=True)
                return last
            return emit

        def col_scores(s, st, h, blocks):
            def emit(e):
                for n, j in enumerate(blocks):
                    last = e.matmul(s.view[:, n, :], st["k"].view[0:NEG + 2, h, j * P:(j + 1) * P],
                                    st["q"].view[0:NEG + 2, h, :], start=True, stop=True)
                return last
            return emit

        views = {"row": row_scores, "col": col_scores,
                 "maxima": lambda s, blocks: [(blocks[0], s.view.rearrange("p a n -> p (a n)"))],
                 "used": lambda s: s.view.rearrange("p a n -> p (a n)")}

        def pv_blocks(blocks):
            return [(j, slice(0, T), slice(n * BANK, (n + 1) * BANK)) for n, j in enumerate(blocks)]

        side, cs_free, cs_ready = [], [], {}

        def finish(n, ctx, m):
            b, f = divmod(n, ET)
            yield
            if f == 0:
                drain(side)
            ctx.freed = split(ctx.view[:, :], cs[0][:, f, :], cs[1][:, f, :], m, cs_free)
            cs_ready.setdefault(b, []).append(ctx.freed)
            if f == ET - 1:
                side.append(dense(b))

        def dense(b):
            for f in range(DT):
                yield
                k = outs.take()
                m = pe.do(gemm(k.view, products([(T_(wcd, every, t, slice(f * P, f * P + P)), T_(cs, every, t, every))
                                                 for t in range(ET)])), cs_ready[b], wcd_ready, k.freed)
                h_ready[b] = dve.do(lambda e: e.tensor_tensor(hT[:, b, f, :], hT[:, b, f, :], k.view, ALU.add),
                                    m, h_ready[b])
                k.freed = [h_ready[b]]
            cs_free[:] = [m]

        def rows_by(n):
            g, unit = divmod(n, 4 * TT)
            return 4 * TT * (g + 1) + min(4 * TT, -(-(unit + 1) * 4 * TT // (4 * TT - 2)))

        attention(B * NH // 4, 4, sets, accs, outs, bufs, load_group, [(i,) for i in range(TT)],
                  [(2 * j, 2 * j + 1) for j in range(MT // 2)], CROSS_SCALE, views,
                  NEG, pv_blocks, 2, finish, side, lag=3, group_slots=2, rows_by=rows_by)
        barrier()

    with ExitStack() as ph:
        IT = -(-I // P)
        xn = pair(ph, "mn", [P, B * DT, T])
        tmp = ring(ph, "mtmp", 2, [P, T])
        nb = norm_buffers(ph, "n3", 1)
        up_w = Ring([Slot(pair(ph, f"up_w{i}", [P, 4 * DT, P])) for i in range(2)])
        down_w = Ring([Slot(pair(ph, f"down_w{i}", [P, 2, D])) for i in range(2)])
        up_stage = ring(ph, "up_stage", 2, [P, DT, P], dma=True)
        down_stage = ring(ph, "down_stage", 1, [P, D], dma=True)
        act_buf = ring(ph, "silu", 2, [P, T])
        hid = Ring([Slot([pair(ph, f"hid{i}_{x}", [P, T]) for x in "vl"]) for i in range(2)])
        gu_banks = bank_ring(0, 4)
        o_banks = bank_ring(4, 4)
        xn_ready = []
        for b in range(B):
            r, rm = norm_rstd(*square_sum(hT[:, b, :, :], nb, h_ready[b]), gu_banks)
            ms = []
            for t in range(DT):
                s = tmp.take()
                m = scaled(s.view[:, :], hT[:, b, t, :], 3, t, r, rm, s.freed)
                s.freed = split(s.view[:, :], xn[0][:, b * DT + t, :], xn[1][:, b * DT + t, :], m)
                ms += [m, s.freed]
            r.freed = [m]
            xn_ready.append(ms)

        def load_tile(i):
            n = min(P, I - i * P)
            u, d = up_w.take(), down_w.take()
            ums, dms = [], []
            for j, name in enumerate(("v_gate", "v_up", "l_gate", "l_up")):
                s = up_stage.take()
                m = sp.dma(s.port, s.view[:, :, 0:n],
                           ins[name].rearrange("(t p) i -> p t i", p=P)[:, :, i * P:i * P + n], s.freed)
                s.freed = split(s.view[:, :, 0:n], u.view[0][:, j * DT:(j + 1) * DT, 0:n],
                                u.view[1][:, j * DT:(j + 1) * DT, 0:n], m, u.freed)
                ums += [s.freed]
            for x, name in enumerate(("v_down", "l_down")):
                s = down_stage.take()
                m = sp.dma(s.port, s.view[0:n, :], ins[name][i * P:i * P + n, :], s.freed)
                s.freed = split(s.view[0:n, :], d.view[0][0:n, x, :], d.view[1][0:n, x, :], m, d.freed)
                dms += [s.freed]
            return n, u, d, ums, dms

        def hidden(b, tile):
            n, u, d, ums, dms = tile
            hd = hid.take()
            ready = []
            for x in (VEXP, LEXP):
                kg, ku = gu_banks.take(), gu_banks.take()
                done = []
                for j, k in ((2 * x, kg), (2 * x + 1, ku)):
                    done.append(pe.do(gemm(k.view[0:n, :], products(
                        [(T_(u.view, every, j * DT + t, slice(0, n)), T_(xn, every, b * DT + t, every))
                         for t in range(DT)])), xn_ready[b], ums, k.freed))
                a = act_buf.take()
                m = act.do(lambda e, a=a, kg=kg: e.activation(a.view[0:n, :], kg.view[0:n, :], ACT.Silu),
                           done[0], a.freed)
                kg.freed = [m]
                m = dve.do(lambda e, a=a, ku=ku: e.tensor_tensor(a.view[0:n, :], ku.view[0:n, :], a.view[0:n, :],
                                                                 ALU.mult), m, done[1])
                ku.freed = [m]
                m = dve.do(lambda e, a=a, x=x: e.tensor_tensor(a.view[0:n, :], a.view[0:n, :], picked[0:n, x, b, :],
                                                               ALU.mult), m)
                a.freed = split(a.view[0:n, :], hd.view[x][0][0:n, :], hd.view[x][1][0:n, :], m, hd.freed)
                ready += [a.freed]
            u.freed = done
            return hd, ready

        def down(b, tile, hd, ready):
            n, u, d, ums, dms = tile
            for f in range(DT):
                k = o_banks.take()
                m = pe.do(gemm(k.view, products(
                    [((d.view[0][0:n, x, f * P:(f + 1) * P], d.view[1][0:n, x, f * P:(f + 1) * P]),
                      (hd.view[x][0][0:n, :], hd.view[x][1][0:n, :])) for x in (VEXP, LEXP)])),
                    ready, dms, k.freed)
                h_ready[b] = dve.do(lambda e, f=f, k=k, b=b: e.tensor_tensor(hT[:, b, f, :], hT[:, b, f, :], k.view,
                                                                             ALU.add), m, h_ready[b])
                k.freed = [h_ready[b]]
            hd.freed = [m]
            d.freed = [m]

        def write_out(b):
            stores.append(sp.dma(port(f"out{b}_dma"), out[b].rearrange("(t p) n -> p t n", p=P), hT[:, b, :, :],
                                 h_ready[b]))

        pend = None
        tile = load_tile(0)
        for i in range(IT):
            for b in range(B):
                now = (b, tile, *hidden(b, tile))
                if pend:
                    down(*pend)
                    if i == IT - 1 and b > 0:
                        write_out(pend[0])
                pend = now
                if b == 1 and i + 1 < IT:
                    following = load_tile(i + 1)
            tile = following
        down(*pend)
        write_out(B - 1)
        sp.wait(stores)

    top.close()


_NAMES = {"ctx": "ctx_1024", "pos": "pos_1xS", "mask": "mask_BxS_ik0"}
_NAMES.update({n: "L0_xattn_" + n for n in ("W_mem", "W_gate", "b_gate", "norm_w")})
_NAMES.update({n: "L1_xattn_" + n for n in (
    "ln_in_w", "ln_post_attn_w", "ln_post_cross_w", "v_qkv", "l_qkv", "v_dense", "l_dense", "cq_w", "ckv_w",
    "cdense_w", "v_gate", "v_up", "v_down", "l_gate", "l_up", "l_down")})
_TURNED = {"xT": "x", "ctxT": "ctx_1024", "W_memT": "L0_xattn_W_mem", "W_gateT": "L0_xattn_W_gate"}


def constants(T, D, NH):
    import numpy as np

    HD = D // NH
    inv = (1.0 / 10000.0 ** (np.arange(0, HD, 2, dtype=np.float32) / np.float32(HD))).astype(np.float32)
    angle = np.outer(np.arange(T, dtype=np.float32), inv).astype(np.float32)
    angle = np.tile(angle, (1, 2 * P // HD))
    rope = np.stack([np.cos(angle), np.sin(angle)]).astype(np.float32)
    turn = np.zeros((P, P), np.float32)
    for j in range(P):
        half = j % HD < HD // 2
        turn[j + HD // 2 if half else j - HD // 2, j] = -1.0 if half else 1.0
    at = np.arange(P)
    low = np.where(at[None, :] > at[:, None], -1e38, 0.0)
    return {
        "ident": np.eye(P, dtype=np.float32), "mean_w": np.full((P, P), 1.0 / D, np.float32),
        "causal": np.stack([low, low.T], axis=1).astype(np.float32),
        "rope": rope, "turn": turn,
        "row_no": (np.arange(T // P)[None, :] * P + at[:, None]).astype(np.float32),
    }


def kernel(**inputs):
    import numpy as np
    import concourse.bacc as bacc
    from concourse.bass_utils import run_bass_kernel_spmd

    nc = bacc.Bacc("TRN2", target_bir_lowering=False, num_devices=1)
    arrays, ins, const = {}, {}, {}
    for name, full in _NAMES.items():
        a = np.asarray(inputs[full])
        if a.ndim == 1:
            a = a.reshape(-1, P).T
        arrays[name] = np.ascontiguousarray(a)
    for name, full in _TURNED.items():
        arrays[name] = np.ascontiguousarray(np.swapaxes(np.asarray(inputs[full]), -1, -2))
    arrays["mask_cols"] = np.ascontiguousarray(arrays["mask"].reshape(-1, P).T)
    B, D, T = arrays["xT"].shape
    M, E = arrays["ctx"].shape[1:]
    dims = dict(B=B, T=T, D=D, E=E, M=M, NH=16, I=arrays["v_gate"].shape[1])
    for views, of, suffix in ((ins, dict(arrays), "_dram"), (const, constants(T, D, dims["NH"]), "_const")):
        for name, a in of.items():
            arrays.pop(name, None)
            arrays[name + suffix] = a
            views[name] = nc.dram_tensor(name + suffix, a.shape, mybir.dt.from_np(a.dtype),
                                         kind="ExternalInput").ap()
    out = nc.dram_tensor("out_dram", (B, D, T), F32, kind="ExternalOutput").ap()
    xattn_block(nc, dims, ins, const, out)
    r = run_bass_kernel_spmd(nc, [arrays], core_ids=[0])
    return np.ascontiguousarray(np.swapaxes(r.results[0]["out_dram"], -1, -2))
```

```python
from contextlib import ExitStack

import concourse.bass as bass
from concourse import mybir

F32 = mybir.dt.float32
F32R = mybir.dt.float32r
BF16 = mybir.dt.bfloat16
I32 = mybir.dt.int32
ALU = mybir.AluOpType
ACT = mybir.ActivationFunctionType
AX = mybir.AxisListType

P = 128
BANK = 512
EPS = 1e-6


class Lane:

    def __init__(self, engine, sem):
        self.engine, self.sem, self.count, self.passed = engine, sem, 0, {}

    def wait(self, *after):
        for sem, value in marks(after):
            if self.passed.get(id(sem), 0) < value:
                self.passed[id(sem)] = value
                self.engine.wait_ge(sem, value)

    def do(self, emit, *after):
        self.wait(*after)
        self.count += 1
        emit(self.engine).then_inc(self.sem, 1)
        return (self.sem, self.count)

    def dma(self, port, out, in_, *after):
        self.wait(*after)
        port.count += 16
        self.engine.dma_start(out, in_).then_inc(port.sem, 16)
        return (port.sem, port.count)


class Port:

    def __init__(self, sem):
        self.sem, self.count = sem, 0


def marks(after):
    for a in after:
        if a is None:
            continue
        if isinstance(a, tuple) and len(a) == 2 and isinstance(a[1], int):
            yield a
        else:
            yield from marks(a)


class Slot:

    def __init__(self, view, port=None):
        self.view, self.port, self.freed = view, port, []


class Ring:
    def __init__(self, slots):
        self.slots, self.next = slots, 0

    def take(self):
        slot = self.slots[self.next % len(self.slots)]
        self.next += 1
        return slot

    def skip_to_multiple(self, n):
        self.next = -(-self.next // n) * n


def f32(ap):
    return ap.bitcast(F32)


def products(pairs):
    out = []
    for (ah, al), (bh, bl) in pairs:
        out += [(al, bh), (ah, bl), (ah, bh)]
    return out


def gemm(out, passes):
    def emit(e):
        for i, (lhsT, rhs) in enumerate(passes):
            last = e.matmul(out, lhsT, rhs, start=(i == 0), stop=(i == len(passes) - 1))
        return last
    return emit


def xattn_block(nc, dims, ins, const, out):
    B, T, D, E, M, NH, I = (dims[k] for k in ("B", "T", "D", "E", "M", "NH", "I"))
    HD, CC = D // NH, E
    CHD = CC // NH
    DT, TT, ET, MT = D // P, T // P, E // P, M // P
    assert T == BANK and D == BANK and M == 2 * BANK and HD == 32 and CHD == 16
    GH = P // HD
    L0_SCALE, SELF_SCALE, CROSS_SCALE = D ** -0.5, HD ** -0.5, CHD ** -0.5

    top = ExitStack()

    def sem(name):
        return top.enter_context(nc.semaphore(name))

    pe = Lane(nc.tensor, sem("pe_done"))
    act = Lane(nc.scalar, sem("act_done"))
    dve = Lane(nc.vector, sem("dve_done"))
    pool = Lane(nc.gpsimd, sem("pool_done"))
    sp = Lane(nc.sync, sem("sp_done"))

    all_ports = []

    def on_pool(emit, *after):
        return pool.do(emit, *after, (pool.sem, pool.count) if pool.count else None)

    def port(name):
        all_ports.append(Port(sem(name)))
        return all_ports[-1]

    def alloc(ctx, name, shape, dt=F32):
        return ctx.enter_context(nc.sbuf_tensor(name, shape, dt))

    def ring(ctx, name, n, shape, dt=F32, dma=False):
        return Ring([Slot(alloc(ctx, f"{name}{i}", shape, dt), port(f"{name}{i}_dma") if dma else None)
                     for i in range(n)])

    def pair(ctx, name, shape):
        return alloc(ctx, name + "_hi", shape, F32R), alloc(ctx, name + "_lo", shape, F32R)

    lanes = (pe, act, dve, pool, sp)
    stores = []

    def barrier():
        ends = [(x.sem, x.count) for x in lanes if x.count]
        ports = [(p.sem, p.count) for p in all_ports if p.count]
        for x in lanes:
            x.wait(ends, ports)

    psum = top.enter_context(nc.psum_tensor("psum", [P, 8, BANK], F32))

    def split(src, hi, lo, *after, copier=None):
        if copier is None:
            m_hi = act.do(lambda e: e.activation(hi, src, ACT.Copy), *after)
        else:
            m_hi = copier(hi, src, *after)
        m_lo = dve.do(lambda e: e.tensor_tensor(lo, src, f32(hi), ALU.subtract), *after, m_hi)
        return [m_hi, m_lo]

    hT = alloc(top, "hT", [P, B, DT, T])
    h_ready = [None] * B
    ident = alloc(top, "ident", [P, P])
    ident16 = alloc(top, "ident16", [P, P], BF16)
    mean_w = alloc(top, "mean_w", [P, P])
    eps_col = alloc(top, "eps_col", [P, 1])
    causal = alloc(top, "causal", [P, 2, P], BF16)
    norm_ws = alloc(top, "norm_ws", [P, 4, DT])
    gate_b = alloc(top, "gate_b", [P, DT])
    picked = alloc(top, "picked", [P, 2, B, T], BF16)
    VEXP, LEXP = 0, 1
    has_v = alloc(top, "has_v", [1, TT], I32)

    c_port = port("const_dma")
    for dst, src in ((ident[:, :], const["ident"]), (mean_w[:, :], const["mean_w"]),
                     (gate_b[:, :], ins["b_gate"]),
                     (norm_ws[:, 0, :], ins["norm_w"]),
                     (norm_ws[:, 1, :], ins["ln_in_w"]),
                     (norm_ws[:, 2, :], ins["ln_post_cross_w"]),
                     (norm_ws[:, 3, :], ins["ln_post_attn_w"])):
        consts = sp.dma(c_port, dst, src)
    eps_set = dve.do(lambda e: e.memset(eps_col[:, :], EPS))

    self_qk = nc.dram_tensor("self_qk", [B, 2, DT, 2, P, T], F32, kind="Internal").ap()
    self_v = nc.dram_tensor("self_v", [B, TT, P, D], F32, kind="Internal").ap()
    cross_k = nc.dram_tensor("cross_k", [B, ET, 2, P, M], F32, kind="Internal").ap()
    cross_v = nc.dram_tensor("cross_v", [B, MT, P, CC], F32, kind="Internal").ap()
    cross_q = nc.dram_tensor("cross_q", [B, ET, 2, P, T], F32, kind="Internal").ap()

    def norm_buffers(ctx, name, n=1, squares=2):
        return {"sq": ring(ctx, name + "_sq", squares, [P, T]), "rstd": ring(ctx, name + "_rstd", n, [P, T])}

    def square_sum(src, buf, *after):
        total = buf["rstd"].take()
        for t in range(DT):
            dst = buf["sq"].take() if t else total
            m = act.do(lambda e: e.activation(dst.view[:, :], src[:, t, :], ACT.Square), *after, dst.freed)
            if t == 0:
                added = m
            else:
                added = dve.do(lambda e: e.tensor_tensor(total.view[:, :], total.view[:, :], dst.view[:, :],
                                                         ALU.add), m, added)
                dst.freed = [added]
        return total, added

    def norm_rstd(total, ready, banks):
        bank = banks.take()
        m = pe.do(gemm(bank.view, [(mean_w[:, :], total.view[:, :])]), ready, bank.freed, consts)
        m = act.do(lambda e: e.activation(total.view[:, :], bank.view, ACT.Sqrt, bias=eps_col[:, 0:1]), m, eps_set)
        bank.freed = [m]
        return total, dve.do(lambda e: e.reciprocal(total.view[:, :], total.view[:, :]), m)

    def scaled(dst, src, norm, t, r, *after):
        return dve.do(lambda e: e.scalar_tensor_tensor(out=dst, in0=src, scalar=norm_ws[:, norm, t:t + 1],
                                                       in1=r.view[:, :], op0=ALU.mult, op1=ALU.mult),
                      *after, consts)

    def drain(tasks):
        while tasks:
            for _ in tasks.pop(0):
                pass

    def normalised(jobs, tmp, r, rm):
        out = []
        drain([normalising(jobs, tmp, r, rm, out)])
        return out

    def normalising(jobs, tmp, r, rm, out):
        pending = []

        def low(s, lo, hi, m, m_hi):
            s.freed = [dve.do(lambda e: e.tensor_tensor(lo, s.view[:, :], f32(hi), ALU.subtract), m, m_hi)]
            out.append([m_hi, s.freed])

        for src, norm, t, hi, lo, after in jobs:
            s = tmp.take()
            m = scaled(s.view[:, :], src, norm, t, r, rm, s.freed)
            m_hi = act.do(lambda e: e.activation(hi, s.view[:, :], ACT.Copy), m, after)
            pending.append((s, lo, hi, [m, after], m_hi))
            r.freed = [m]
            if len(pending) > 1:
                low(*pending.pop(0))
            yield
        low(*pending.pop(0))

    def finish_norm(b, total, m, banks):
        r, m = norm_rstd(total, m, banks)
        for f in range(DT):
            h_ready[b] = scaled(hT[:, b, f, :], hT[:, b, f, :], 0, f, r, m)
        r.freed = [h_ready[b]]

    def load_split(w, n, source, staging, width):
        out = []
        for i in range(n):
            s = staging.take()
            rows, src = source(i)
            m = sp.dma(s.port, s.view[0:rows, 0:width], src, s.freed)
            raw = s.view[0:rows, 0:width]
            ms = split(raw, w[0][0:rows, i, 0:width], w[1][0:rows, i, 0:width], m)
            s.freed = ms
            out.append(ms)
        return out

    def pick(dst, mask, kl, ml, kv, mv, *after):
        m = act.do(lambda e: e.activation(dst, kl.view, ACT.Copy), ml, *after)
        kl.freed = [m]
        m = dve.do(lambda e: e.copy_predicated(dst, mask.bitcast(mybir.dt.uint16), kv.view), m, mv)
        kv.freed = [m]
        return m

    def bank_ring(first, n, width=1):
        return Ring([Slot(psum[:, first + i * width:first + (i + 1) * width, :] if width > 1 else psum[:, first + i, :])
                     for i in range(n)])

    def T_(ap_pair, *idx):
        return ap_pair[0][idx], ap_pair[1][idx]

    every = slice(None)
    until_b = top.enter_context(ExitStack())
    cos = alloc(until_b, "cos", [P, T])
    sin = alloc(until_b, "sin", [P, T])
    turn_r = alloc(until_b, "turn_r", [P, P], F32R)
    is_v_row = alloc(until_b, "is_v_row", [P, B * TT, 1], BF16)
    with ExitStack() as ph:
        wm = pair(ph, "wm", [P, DT, E])
        wmT = pair(ph, "wmT", [P, ET, D])
        wgT = pair(ph, "wgT", [P, DT, D])
        wc = pair(ph, "wc", [P, ET, D])
        ckv = pair(ph, "ckv", [P, ET, 2 * CC])
        banks = bank_ring(0, 8)
        def load_x(b):
            h_ready[b] = sp.dma(port(f"x{b}_dma"), hT[:, b, :, :], ins["xT"][b].rearrange("(t p) n -> p t n", p=P))

        load_x(0)

        with ExitStack() as setup:
            staging = ring(setup, "wstage", 4, [P, D], dma=True)
            wg2T = pair(setup, "wg2T", [P, DT, D])

            def weight(name, dst, n, width, row=0):
                return load_split(dst, n, lambda i: (P, ins[name][(row + i) * P:(row + i + 1) * P, :]), staging, width)

            wm_ready = weight("W_mem", wm, DT, E)
            wg2T_ready = weight("W_gateT", wg2T, DT, D, DT)
            wc_ready = []
            for i in range(ET):
                bank = banks.take()
                m = pe.do(gemm(bank.view, products([(T_(wm, every, t, slice(i * P, i * P + P)),
                                                     T_(wg2T, every, t, every)) for t in range(DT)])),
                          wm_ready, wg2T_ready, bank.freed)
                bank.freed = split(bank.view, wc[0][:, i, :], wc[1][:, i, :], m)
                wc_ready.append(bank.freed)
            wgT_ready = weight("W_gateT", wgT, DT, D)
            ckv_ready = weight("ckv_w", ckv, ET, 2 * CC)
            wmT_ready = weight("W_memT", wmT, ET, D)
            causal_in = alloc(setup, "causal_in", [P, 2, P])
            m = sp.dma(port("causal_dma"), causal_in[:, :, :], const["causal"])
            dve.do(lambda e: e.tensor_copy(causal[:, :, :], causal_in[:, :, :]), m)
            dve.do(lambda e: e.tensor_copy(ident16[:, :], ident[:, :]), consts)
            types = alloc(setup, "types", [P, B, T], I32)
            types_f = alloc(setup, "types_f", [P, B, T])
            m = sp.dma(port("types_dma"), types[:, :, :].rearrange("p b t -> p (b t)"),
                       ins["mask"].rearrange("b t -> (b t)").partition_broadcast(P))
            m = dve.do(lambda e: e.tensor_scalar(types_f[:, :, :], types[:, :, :], 1.0, None, ALU.is_equal), m)
            m1 = dve.do(lambda e: e.memset(picked[:, VEXP, :, T - 1:T], 0.0))
            m2 = dve.do(lambda e: e.tensor_tensor(picked[:, VEXP, :, 0:T - 1], types_f[:, :, 0:T - 1],
                                                  types_f[:, :, 1:T], ALU.mult), m)
            picked_ready = dve.do(lambda e: e.tensor_scalar(picked[:, LEXP, :, :], picked[:, VEXP, :, :], -1.0, 1.0,
                                                            ALU.mult, ALU.add), m1, m2)
            has_v_f = alloc(setup, "has_v_f", [1, TT])
            m = dve.do(lambda e: e.tensor_reduce(has_v_f[0:1, :], picked[0:1, VEXP, :, :].rearrange(
                "p b (t n) -> p t b n", n=P), AX.XY, ALU.max), m2, m1)
            dve.do(lambda e: e.tensor_copy(has_v[0:1, :], has_v_f[0:1, :]), m)
            this = alloc(setup, "this", [P, B, TT], I32)
            following = alloc(setup, "following", [P, B, TT], I32)
            f1, f2 = alloc(setup, "this_f", [P, B, TT]), alloc(setup, "following_f", [P, B, TT])
            cols = ins["mask_cols"].rearrange("p (b t) -> p b t", b=B)
            ma = sp.dma(port("this_dma"), this[:, :, :], cols)
            z = dve.do(lambda e: e.memset(following[:, :, :], 0))
            mb = sp.dma(port("next_dma"), following[0:P - 1, :, :], cols[1:P, :, :], z)
            mc = sp.dma(port("next_tile_dma"), following[P - 1:P, :, 0:TT - 1], cols[0:1, :, 1:TT], z)
            m1 = dve.do(lambda e: e.tensor_scalar(f1[:, :, :], this[:, :, :], 1.0, None, ALU.is_equal), ma)
            m2 = dve.do(lambda e: e.tensor_scalar(f2[:, :, :], following[:, :, :], 1.0, None, ALU.is_equal), mb, mc)
            rows_ready = dve.do(lambda e: e.tensor_tensor(is_v_row[:, :, 0].rearrange("p (b t) -> p b t", b=B),
                                                          f1[:, :, :], f2[:, :, :], ALU.mult), m1, m2)
            turn_raw = alloc(setup, "turn_raw", [P, P])
            table = alloc(setup, "table", [P, 2, TT, P])
            pos_i = alloc(setup, "pos_i", [P, T], I32)
            pos_f = alloc(setup, "pos_f", [P, T])
            onehot = alloc(setup, "onehot", [P, TT, T])
            row_no = alloc(setup, "row_no", [P, TT])
            m = sp.dma(port("turn_dma"), turn_raw[:, :], const["turn"])
            turn_ready = dve.do(lambda e: e.tensor_copy(turn_r[:, :], turn_raw[:, :]), m)
            tab_in = sp.dma(port("table_dma"), table[:, :, :, :], const["rope"].rearrange("a (t p) d -> p a t d", p=P))
            row_in = sp.dma(port("row_dma"), row_no[:, :], const["row_no"])
            m = sp.dma(port("pos_dma"), pos_i[:, :], ins["pos"].rearrange("a t -> (a t)").partition_broadcast(P))
            m = dve.do(lambda e: e.tensor_scalar(pos_f[:, :], pos_i[:, :], 0.0, float(T - 1), ALU.max, ALU.min), m)
            for t in range(TT):
                hot = dve.do(lambda e: e.tensor_scalar(onehot[:, t, :], pos_f[:, :], row_no[:, t:t + 1], None,
                                                       ALU.is_equal), m, row_in)
            for a, dst in enumerate((cos, sin)):
                k = banks.take()
                m = pe.do(gemm(k.view, [(table[:, a, t, :], onehot[:, t, :]) for t in range(TT)]), hot, tab_in,
                          k.freed)
                rope_ready = act.do(lambda e: e.activation(dst[:, :], k.view, ACT.Copy), m)
                k.freed = [rope_ready]
        barrier()

        mem_in = ring(ph, "mem_in", 2, [P, T], dma=True)
        xT = pair(ph, "xT", [P, DT, T])
        mem = pair(ph, "mem", [P, MT, E])
        memT = pair(ph, "memT", [P, ET, M])
        k_out = Ring([Slot(pair(ph, "k_out", [P, BANK]), port("k_dma"))])
        v_out = ring(ph, "v_out", 1, [P, 2, CC], dma=True)
        qT = pair(ph, "qT", [P, ET, T])
        zx = alloc(ph, "zx", [P, DT, T])
        probs = ring(ph, "probs", 1, [P, M])
        probsT = pair(ph, "probsT", [P, MT, T])
        inverse = ring(ph, "inverse", 1, [P, P])
        stat = ring(ph, "stat", 2, [P, 4])
        nb = {"sq": mem_in, "rstd": ring(ph, "n0_rstd", 1, [P, T])}
        free = {"xT": [], "mem": [], "memT": [], "probsT": [], "qT": [], "zx": []}
        for b in range(1, B):
            load_x(b)
        ready = {}

        def take_x(b):
            ready["x"] = [split(hT[:, b, t, :], xT[0][:, t, :], xT[1][:, t, :], h_ready[b], free["xT"])
                          for t in range(DT)]

        def take_memT(b):
            ready["memT"] = []
            for f in range(ET):
                for half in range(2):
                    s = mem_in.take()
                    cols = slice(half * T, (half + 1) * T)
                    m = sp.dma(s.port, s.view[:, :], ins["ctxT"][b, f * P:(f + 1) * P, cols], s.freed)
                    s.freed = split(s.view[:, :], memT[0][:, f, cols], memT[1][:, f, cols], m, free["memT"])
                    ready["memT"] += [s.freed]

        def take_mem(b):
            ready["mem"] = []
            for quarter in range(4):
                s = mem_in.take()
                tiles = slice(quarter * MT // 4, (quarter + 1) * MT // 4)
                src = ins["ctx"][b].rearrange("(t p) e -> p t e", p=P)[:, tiles, :]
                view = s.view[:, :].rearrange("p (t e) -> p t e", e=E)
                m = sp.dma(s.port, view, src, s.freed)
                s.freed = split(view, mem[0][:, tiles, :], mem[1][:, tiles, :], m, free["mem"], copier=pool_copy)
                ready["mem"] += [s.freed]

        def gate_share(f):
            k = banks.take()
            m = pe.do(gemm(k.view, products([(T_(wgT, every, t, slice(f * P, f * P + P)), T_(xT, every, t, every))
                                             for t in range(DT)])), ready["x"], k.freed)
            k.freed = [act.do(lambda e: e.activation(zx[:, f, :], k.view, ACT.Copy), m, free["zx"])]
            ready["zx"] = k.freed
            free["xT"] = [m]

        def cross_keys(b, i, half):
            cols = slice(half * BANK, (half + 1) * BANK)
            k = banks.take()
            m = pe.do(gemm(k.view, products([(T_(ckv, every, t, slice(i * P, i * P + P)), T_(memT, every, t, cols))
                                             for t in range(ET)])), ready["memT"], k.freed)
            s = k_out.take()
            k.freed = split(k.view, s.view[0][:, :], s.view[1][:, :], m, s.freed)
            sp.dma(s.port, cross_k[b, i, 0, :, cols], f32(s.view[0][:, :]), k.freed)
            s.freed = [sp.dma(s.port, cross_k[b, i, 1, :, cols], f32(s.view[1][:, :]))]

        def cross_values(b, pair_at):
            k = banks.take()
            both = k.view.rearrange("p (a c) -> p a c", a=2)
            for j in range(2):
                rows = slice((2 * pair_at + j) * P, (2 * pair_at + j + 1) * P)
                m = pe.do(gemm(both[:, j, :], products([(T_(memT, every, t, rows),
                                                         T_(ckv, every, t, slice(CC, 2 * CC))) for t in range(ET)])),
                          ready["memT"], k.freed)
            s = v_out.take()
            k.freed = [act.do(lambda e: e.activation(s.view[:, :, :], both, ACT.Copy), m, s.freed)]
            s.freed = [sp.dma(s.port, cross_v[b, 2 * pair_at:2 * pair_at + 2, :, :].rearrange("t p c -> p t c"),
                              s.view[:, :, :], k.freed)]

        def scores(qt):
            banks.skip_to_multiple(2)
            at = banks.next % 8
            both = psum[:, at:at + 2, :]
            two = [banks.take(), banks.take()]
            for half, k in enumerate(two):
                scored = pe.do(gemm(k.view, products([(T_(qT, every, t, slice(qt * P, (qt + 1) * P)),
                                                       T_(memT, every, t, slice(half * BANK, (half + 1) * BANK)))
                                                      for t in range(ET)])), ready["q"], ready["memT"], k.freed)
            st, p = stat.take(), probs.take()
            c = st.view
            m = dve.do(lambda e: e.tensor_reduce(c[:, 0:1], both, AX.XY, ALU.max), scored, st.freed)
            m = dve.do(lambda e: e.tensor_scalar(c[:, 1:2], c[:, 0:1], -L0_SCALE, None, ALU.mult), m)
            m = act.do(lambda e: e.activation(p.view[:, :].rearrange("p (a n) -> p a n", a=2), both, ACT.Exp,
                                              bias=c[:, 1:2], scale=L0_SCALE, accum_out=c[:, 2:3]), m, p.freed)
            for k in two:
                k.freed = [m]
            d = inverse.take()
            m1 = dve.do(lambda e: e.reciprocal(c[:, 3:4], c[:, 2:3]), m)
            m1 = dve.do(lambda e: e.tensor_scalar(d.view[:, :], ident[:, :], c[:, 3:4], None, ALU.mult), m1, d.freed)
            st.freed = [m1]
            return p, d, [m, m1], scored

        def turn_probs(qt, p, d, ready_p):
            out = []
            for half in range(2):
                k = banks.take()

                def emit(e):
                    for j in range(4):
                        at = (4 * half + j) * P
                        last = e.matmul(k.view[:, j * P:(j + 1) * P], p.view[:, at:at + P], d.view[:, :], start=True,
                                        stop=True)
                    return last
                turned = pe.do(emit, ready_p, k.freed)
                dst = slice(4 * half, 4 * half + 4), slice(qt * P, (qt + 1) * P)
                k.freed = split(k.view.rearrange("p (j n) -> p j n", j=4), probsT[0][:, dst[0], dst[1]],
                                probsT[1][:, dst[0], dst[1]], turned, free["probsT"])
                out.append(k.freed)
            p.freed = d.freed = [turned]
            return out

        def pool_copy(hi, src, *after):
            return on_pool(lambda e: e.tensor_copy(hi, src), *after)

        def queries(b):
            out = []
            for i in range(ET):
                k = banks.take()
                m = pe.do(gemm(k.view, products([(T_(wm, every, t, slice(i * P, i * P + P)), T_(xT, every, t, every))
                                                 for t in range(DT)])), ready["x"], k.freed)
                k.freed = split(k.view, qT[0][:, i, :], qT[1][:, i, :], m, free["qT"])
                out += [k.freed]
            ready["q"] = out

        def sum_squares(b):
            return b, *square_sum(hT[:, b, :, :], nb, h_ready[b])

        take_x(0)
        take_memT(0)
        for b in range(B):
            queries(b)
            probsT_in = []
            for qt in range(TT):
                if qt == 0:
                    gate_share(qt)
                p, d, m, scored = scores(qt)
                if qt == 0:
                    take_mem(b)
                if b and qt == 1:
                    rms = sum_squares(b - 1)
                if b and qt == 2:
                    finish_norm(*rms, banks)
                if qt:
                    gate_share(qt)
                cross_keys(b, qt // 2, qt % 2)
                cross_values(b, qt)
                if qt == TT - 1:
                    free["memT"] = [(pe.sem, pe.count)]
                    if b + 1 < B:
                        take_x(b + 1)
                probsT_in += turn_probs(qt, p, d, m)
            if b + 1 < B:
                take_memT(b + 1)
            a_ready = []
            for i in range(ET):
                k = banks.take()
                m = pe.do(gemm(k.view, products([(T_(mem, every, t, slice(i * P, i * P + P)),
                                                  T_(probsT, every, t, every)) for t in range(MT)])),
                          ready["mem"], probsT_in, k.freed)
                k.freed = split(k.view, qT[0][:, i, :], qT[1][:, i, :], m, scored)
                a_ready += [k.freed]
            free["probsT"] = free["mem"] = [m]
            pending = []

            def fuse(f, kc, mc, m):
                m = dve.do(lambda e: e.tensor_tensor(zx[:, f, :], kc.view, zx[:, f, :], ALU.mult), m, mc)
                kc.freed = [m]
                h_ready[b] = dve.do(lambda e: e.tensor_tensor(hT[:, b, f, :], hT[:, b, f, :], zx[:, f, :], ALU.add),
                                    m, h_ready[b])
                free["zx"] = [h_ready[b]]

            for f in range(DT):
                fcols = slice(f * P, (f + 1) * P)
                kz, kc = banks.take(), banks.take()
                mz = pe.do(gemm(kz.view, products([(T_(wc, every, t, fcols), T_(qT, every, t, every))
                                                   for t in range(ET)])), a_ready, kz.freed)
                mc = pe.do(gemm(kc.view, products([(T_(wmT, every, t, fcols), T_(qT, every, t, every))
                                                   for t in range(ET)])), a_ready, kc.freed)
                m = dve.do(lambda e: e.tensor_tensor(zx[:, f, :], kz.view, zx[:, f, :], ALU.add), mz, ready["zx"])
                kz.freed = [m]
                m = act.do(lambda e: e.activation(zx[:, f, :], zx[:, f, :], ACT.Sigmoid, bias=gate_b[:, f:f + 1]), m)
                pending.append((f, kc, mc, m))
                if f:
                    fuse(*pending.pop(0))
            fuse(*pending.pop(0))
            free["qT"] = [mc]
        barrier()

    with ExitStack() as ph:
        W3 = 3 * D
        wv = pair(ph, "wv_qkv", [P, DT, W3])
        wl = pair(ph, "wl_qkv", [P, DT, W3])
        staging = ring(ph, "qkv_stage", 2, [P, D], dma=True)
        banks = bank_ring(0, 8)
        xs = Ring([Slot(pair(ph, f"xn{i}", [P, DT, T])) for i in range(2)])
        tmp = ring(ph, "xn_tmp", 2, [P, T])
        nb = norm_buffers(ph, "n1", squares=1)
        raw = ring(ph, "raw", 2, [P, T])
        raw_hl = Ring([Slot(pair(ph, "raw_hl", [P, T]))])
        prod = ring(ph, "prod", 1, [P, T])
        qk_out = Ring([Slot(pair(ph, f"qk{i}", [P, T]), port(f"qk{i}_dma")) for i in range(2)])
        v_out = ring(ph, "sv_out", 1, [P, D], dma=True)

        w_ready = {}

        def weights(parts, experts=(LEXP, VEXP)):
            loaded = []
            for part in parts:
                cols = slice(part * D, (part + 1) * D)
                for x in experts:
                    w, name = ((wv, "v_qkv"), (wl, "l_qkv"))[x]
                    w_ready[x, part] = []
                    for t in range(DT):
                        s = staging.take()
                        m = sp.dma(s.port, s.view[:, :], ins[name][t * P:(t + 1) * P, cols], s.freed)
                        loaded.append((s, w, t, cols, w_ready[x, part], m))
                        if len(loaded) == len(staging.slots):
                            yield
                            for s, w_, t_, cols_, done, m in loaded:
                                s.freed = split(s.view[:, :], w_[0][:, t_, cols_], w_[1][:, t_, cols_], m)
                                done.append(s.freed)
                            loaded = []

        def norms(b):
            if b == 0:
                total = square_sum(hT[:, B - 1, :, :], nb, h_ready[B - 1])
                yield
                finish_norm(B - 1, *total, banks)
                yield
            if b + 1 < B:
                total = square_sum(hT[:, b + 1, :, :], nb, h_ready[b + 1])
                yield
                following_x.append(xs.take())
                yield from normed(b + 1, total, following_x[0])

        def normed(b, total, x):
            r, rm = norm_rstd(*total, banks)
            yield
            x.ready = []
            yield from normalising([(hT[:, b, t, :], 1, t, x.view[0][:, t, :], x.view[1][:, t, :], x.freed)
                                    for t in range(DT)], tmp, r, rm, x.ready)

        def expert_banks(x, wcols, xcols, part, rows):
            out = []
            for expert, w in ((LEXP, wl), (VEXP, wv)):
                k = banks.take()
                pairs = [(T_(w, every, t, wcols), T_(x.view, every, t, xcols)) for t in range(DT)]
                m = pe.do(gemm(k.view, products([(c, a) for a, c in pairs] if rows else pairs)),
                          x.ready, w_ready[expert, part], k.freed)
                out.append((k, m))
            return out

        def rotate(b, part, f, s, hl, ms):
            kr = banks.take()
            mr = pe.do(gemm(kr.view, [(turn_r[:, :], hl.view[1][:, :]), (turn_r[:, :], hl.view[0][:, :])]),
                       ms, kr.freed)
            hl.freed = [mr]
            p = prod.take()
            m1 = dve.do(lambda e: e.tensor_tensor(s.view[:, :], s.view[:, :], cos[:, :], ALU.mult), ms)
            m2 = dve.do(lambda e: e.tensor_tensor(p.view[:, :], kr.view, sin[:, :], ALU.mult), mr, p.freed)
            kr.freed = [m2]

            def finish():
                m = on_pool(lambda e: e.tensor_tensor(s.view[:, :], s.view[:, :], p.view[:, :], ALU.add), m1, m2)
                p.freed = [m]
                o = qk_out.take()
                s.freed = split(s.view[:, :], o.view[0][:, :], o.view[1][:, :], m, o.freed)
                sp.dma(o.port, self_qk[b, part, f, 0, :, :], f32(o.view[0][:, :]), s.freed)
                o.freed = [sp.dma(o.port, self_qk[b, part, f, 1, :, :], f32(o.view[1][:, :]))]
            return finish

        total = square_sum(hT[:, 0, :, :], nb, h_ready[0])
        drain([weights((0,), (LEXP,))])
        x = xs.take()
        drain([normed(0, total, x), weights((0,), (VEXP,))])
        later_weights = weights((1, 2))
        next(later_weights)
        turning = None
        for b in range(B):
            following_x = []
            norm_steps = norms(b)
            for i in range(2 * DT):
                part, f = divmod(i, DT)
                (kl, ml), (kv, mv) = expert_banks(x, slice(part * D + f * P, part * D + (f + 1) * P), every, part,
                                                  False)
                rotated = rotate(*turning) if turning else None
                s = raw.take()
                m = pick(s.view[:, :], picked[:, VEXP, b, :], kl, ml, kv, mv, s.freed)
                hl = raw_hl.take()
                turning = (b, part, f, s, hl, split(s.view[:, :], hl.view[0][:, :], hl.view[1][:, :], m, hl.freed))
                if rotated:
                    rotated()
                for steps in (later_weights, norm_steps):
                    next(steps, None)
            drain([norm_steps])
            for t in range(TT):
                (kl, ml), (kv, mv) = expert_banks(x, slice(2 * D, W3), slice(t * P, (t + 1) * P), 2, True)
                if t == 0:
                    rotated = rotate(*turning)
                    turning = None
                s = v_out.take()
                mask = is_v_row[:, b * TT + t, :].to_broadcast([P, D])
                m = pick(s.view[:, :], mask, kl, ml, kv, mv, s.freed)
                s.freed = [sp.dma(s.port, self_v[b, t, :, :], s.view[:, :], m)]
                if t == 0:
                    rotated()
            x.freed = [mv]
            x = following_x[0] if following_x else None
        barrier()
    until_b.close()

    def attention(groups, G, score_sets, accs, misc, bufs, load_group, row_blocks, col_blocks, scale,
                  set_views, neg_rows, pv_blocks, heads_per_out, finish, side, lag, group_slots, rows_by,
                  split_probs=None):
        stage = {}
        closing = []

        unsplit = []
        chunks = len(col_blocks)
        units = G * chunks

        def rows_of(g, unit):
            st = stage[g]
            h, c = divmod(unit, chunks)
            s = score_sets.take()
            m = pe.do(set_views["row"](s, st, h, row_blocks[c]), st["loaded"], s.freed)
            s.freed = [dve.do(lambda e: e.tensor_reduce(
                st["max"].view[:, h * TT + col:h * TT + col + 1], view, AX.X, ALU.max), m, st["max"].freed)
                for col, view in set_views["maxima"](s, row_blocks[c])]
            st["maxed"] += s.freed

        def maxima_to_rows(g):
            st = stage[g]
            k = misc.take()
            n = G * TT
            m = pe.do(lambda e: e.transpose(k.view[0:n, 0:P], st["max"].view[:, 0:n], ident[:, :]),
                      st["maxed"], k.freed)
            st["max"].freed = [m]
            neg = bufs["neg"].take()
            m1 = dve.do(lambda e: e.tensor_scalar(neg.view[0][0:n, :], k.view[0:n, 0:P], -1.0, None, ALU.mult),
                        m, neg.freed)
            m2 = dve.do(lambda e: e.scalar_tensor_tensor(out=neg.view[1][0:n, :], in0=k.view[0:n, 0:P], scalar=-1.0,
                                                         in1=f32(neg.view[0][0:n, :]), op0=ALU.mult,
                                                         op1=ALU.subtract), m1)
            k.freed = [m1, m2]
            for part in range(2):
                row = f32(st["q"].view[neg_rows + part:neg_rows + part + 1, :, :]).rearrange(
                    "o h (t n) -> o (h t) n", n=P)
                st["neg_in"] = sp.dma(neg.port, row, f32(neg.view[part][0:n, :]), m1, m2)
            neg.freed = [st["neg_in"]]

        def exps(g, unit):
            st = stage[g]
            h, c = divmod(unit, chunks)
            s = score_sets.take()
            m = pe.do(set_views["col"](s, st, h, col_blocks[c]), st["neg_in"], s.freed)
            p = bufs["probs"].take()
            ready = []
            if split_probs:
                hl = bufs["probs_hl"].take()
                ready = [act.do(lambda e: e.activation(hl.view[0][:, :], set_views["used"](s), ACT.Exp, scale=scale),
                                m, hl.freed)]
            s.freed = [act.do(lambda e: e.activation(p.view[:, :], set_views["used"](s), ACT.Exp, scale=scale),
                              m, p.freed)]
            if unit == units - 1:
                st["q"].freed = st["k"].freed = [m]
            if split_probs:
                unsplit.append((p, hl, ready, s.freed))
                return hl, ready
            return p, s.freed

        def low_probs(p, hl, ready, exped):
            parts = []
            for cols, put in ((slice(0, split_probs), dve.do), (slice(split_probs, None), on_pool)):
                parts.append(put(lambda e: e.tensor_tensor(hl.view[1][:, cols], p.view[:, cols],
                                                           f32(hl.view[0][:, cols]), ALU.subtract), ready, exped))
            p.freed = parts
            ready.extend(parts)

        def values(g, unit, p, ready):
            st = stage[g]
            h, c = divmod(unit, chunks)
            first = h % heads_per_out == 0 and c == 0
            last = h % heads_per_out == heads_per_out - 1 and c == chunks - 1
            if first:
                st["acc"] = accs.take()
            acc = st["acc"]
            parts = list(pv_blocks(col_blocks[c]))

            def emit(e):
                whole = p.view[::-1] if split_probs else [p.view]
                for n, (block, cols, pcols) in enumerate(parts):
                    for part, probs in enumerate(whole):
                        x = e.matmul(acc.view[:, cols], st["v_lhs"](h, block), probs[:, pcols],
                                     start=first and n == part == 0,
                                     stop=last and n == len(parts) - 1 and part == len(whole) - 1,
                                     skip_group_check=True)
                return x
            m = pe.do(emit, ready, st["v_ready"], acc.freed if first else None)
            p.freed = [m]
            if last:
                at = 64 if split_probs else 32
                n = (g * G + h) // heads_per_out
                rows = slice(32 * (n % 4), 32 * (n % 4) + 32)
                if n % 4 == 0:
                    low = bufs["low"].take() if split_probs else None
                    stage["o"] = bufs["ctx"].take(), bufs["sums"].take(), low, []
                ctx, sums, low, ms = stage["o"]
                m1 = act.do(lambda e: e.activation(ctx.view[rows, :], acc.view[0:32, :], ACT.Copy), m, ctx.freed)
                m2 = dve.do(lambda e: e.tensor_copy(sums.view[rows, :], acc.view[at:at + 32, :]), m, sums.freed)
                acc.freed = [m1, m2]
                if low:
                    acc.freed += [act.do(lambda e: e.activation(low.view[rows, :], acc.view[32:64, :], ACT.Copy),
                                         m, low.freed)]
                ms += acc.freed
                if n % 4 == 3:
                    closing.append(close(n // 4, ctx, sums, low, ms))
            return m

        def close(n, ctx, sums, low, ms):
            if low:
                yield
                ms = [dve.do(lambda e: e.tensor_tensor(ctx.view[:, :], ctx.view[:, :], low.view[:, :], ALU.add), ms)]
                low.freed = ms
            for half in range(2):
                cols = slice(half * T // 2, (half + 1) * T // 2)
                ms = [dve.do(lambda e: e.reciprocal(sums.view[:, cols], sums.view[:, cols]), ms)]
                yield
            m = dve.do(lambda e: e.tensor_tensor(ctx.view[:, :], ctx.view[:, :], sums.view[:, :], ALU.mult), ms)
            sums.freed = [m]
            yield from finish(n, ctx, m)

        def start(g):
            stage[g] = load_group(g)
            stage[g]["max"] = bufs["max"].take()
            stage[g]["maxed"] = []
            if "spread" in stage[g]:
                closing.append(stage[g]["spread"])

        for g in range(min(groups, group_slots)):
            start(g)
        drain(closing)
        rows_done, due, waiting = 0, [], []
        for n in range(groups * units):
            g, unit = divmod(n, units)
            turning, due = due, []
            while rows_done < min(groups * units, rows_by(n)):
                rows_of(*divmod(rows_done, units))
                rows_done += 1
                if rows_done % units == 0:
                    (due if rows_done > n + units else turning).append(rows_done // units - 1)
            for ready_group in turning:
                maxima_to_rows(ready_group)
            waiting.append((g, unit, *exps(g, unit)))
            while len(unsplit) > (n < groups * units - 1):
                low_probs(*unsplit.pop(0))
            if unit == units - 1 and g + group_slots < groups:
                start(g + group_slots)
            while len(waiting) > lag or (waiting and n == groups * units - 1):
                done, at, *operands = waiting.pop(0)
                m = values(done, at, *operands)
                if at == units - 1:
                    stage[done]["v_done"](m)
                for tasks, taken in ((side, side[:1]), (closing, list(closing))):
                    for task in taken:
                        if next(task, "over") == "over":
                            tasks.remove(task)
        drain(closing)
        drain(side)

    def stack(ctx, name, width, n_rows):
        return alloc(ctx, name, [n_rows, 4, width], F32R)

    with ExitStack() as ph:
        NEG = 3 * HD
        wdv, wdl = pair(ph, "wdv", [P, DT, D]), pair(ph, "wdl", [P, DT, D])
        q_ring = Ring([Slot(stack(ph, f"sq{i}", T, P)) for i in range(3)])
        k_ring = Ring([Slot(stack(ph, f"sk{i}", T, P)) for i in range(3)])
        for r_, n_ in ((q_ring, "sq"), (k_ring, "sk")):
            for i, s in enumerate(r_.slots):
                s.ports = [port(f"{n_}{i}_{j}_dma") for j in range(3)]
        VW = 2 * HD
        VEND = TT * NH * VW
        v_ring = ring(ph, "sv", 2, [P, VEND + VW])
        v_rows = ring(ph, "sv_rows", 1, [P, D], dma=True)
        bufs = {"max": ring(ph, "smax", 3, [P, 4 * TT]),
                "neg": Ring([Slot(pair(ph, f"sneg{i}", [4 * TT, P]), port(f"sneg{i}_dma")) for i in range(2)]),
                "probs": ring(ph, "sprobs", 3, [P, 1280]),
                "sums": ring(ph, "ssums", 2, [P, T]), "ctx": ring(ph, "sctx", 2, [P, T])}
        xs = pair(ph, "cx", [P, DT, T])
        xe = ring(ph, "cxe", 2, [P, T], dma=True)
        for n, (k, q) in enumerate(zip(k_ring.slots, q_ring.slots)):
            put = on_pool if n else dve.do
            k.pads = [put(lambda e: e.memset(f32(k.view[NEG:P, :, :]), 1.0))]
            q.pads = [put(lambda e: e.memset(f32(q.view[NEG:P, :, :]), 0.0))]
        for vs in v_ring.slots:
            vs.freed = [on_pool(lambda e: e.memset(vs.view[:, 0:VEND].rearrange("p (h w) -> p h w", w=VW)[:, :, HD:VW],
                                                   1.0)),
                        on_pool(lambda e: e.memset(vs.view[:, VEND:VEND + VW], 1.0))]
        wd_ready = {VEXP: [], LEXP: []}

        def dense_weights():
            for t in range(DT):
                loaded = []
                for x, w, name in ((VEXP, wdv, "v_dense"), (LEXP, wdl, "l_dense")):
                    s = xe.take()
                    loaded.append((s, x, w, sp.dma(s.port, s.view[:, :], ins[name][t * P:(t + 1) * P, :], s.freed)))
                yield
                for s, x, w, m in loaded:
                    s.freed = split(s.view[:, :], w[0][:, t, :], w[1][:, t, :], m)
                    wd_ready[x].append(s.freed)

        sets = Ring([Slot(psum[:, 0:3, :]), Slot(psum[:, 3:6, :])])
        outs = bank_ring(6, 2)
        at_of = {512: 0, 384: 512, 128: 896, 256: 1024}
        state = {}

        def load_group(g):
            b, f = divmod(g, DT)
            q, k = q_ring.take(), k_ring.take()
            ms = []
            for s, part, order in ((q, 0, (0, 1, 0)), (k, 1, (0, 0, 1))):
                for j, hl in enumerate(order):
                    src = self_qk[b, part, f, hl, :, :].rearrange("(h r) t -> r h t", h=GH)
                    ms.append(sp.dma(s.ports[j], f32(s.view[j * HD:(j + 1) * HD, :, :]), src, s.freed))
            def v_lhs(h, t):
                head = f * GH + h
                at = (t * NH + head) * VW
                return vs.view[:, at:at + P]

            def v_done(m):
                if f == DT - 1:
                    vs.freed = [m]
            if f == 0:
                state["v"] = v_ring.take(), []
            vs, v_ready = state["v"]
            st = {"q": q, "k": k, "loaded": ms + q.pads + k.pads, "v_lhs": v_lhs, "v_ready": v_ready, "v_done": v_done}
            if f == 0:
                st["spread"] = spread(b, vs, v_ready)
            return st

        def spread(b, vs, v_ready):
            for t in range(TT):
                r_ = v_rows.take()
                m = sp.dma(r_.port, r_.view[:, :], self_v[b, t, :, :], r_.freed)
                dst = vs.view[:, t * NH * VW:(t + 1) * NH * VW].rearrange("p (h w) -> p h w", w=VW)[:, :, 0:HD]
                src = r_.view[:, :].rearrange("p (h w) -> p h w", w=HD)
                v_ready.append(on_pool(lambda e: e.tensor_copy(dst, src), m, vs.freed))
                r_.freed = v_ready[-1:]
                yield

        def flat(s):
            return s.view.rearrange("p a n -> p (a n)")

        def row_scores(s, st, h, blocks):
            def emit(e):
                for i in blocks:
                    n = P * (i + 1)
                    at = at_of[n]
                    o = flat(s)
                    e.matmul(o[:, at:at + n], st["q"].view[0:NEG, h, i * P:(i + 1) * P], st["k"].view[0:NEG, h, 0:n],
                             start=True, stop=False, skip_group_check=True)
                    last = e.matmul(o[:, at + n - P:at + n], ident16[:, :], causal[:, 0, :], start=False, stop=True,
                                    skip_group_check=True)
                return last
            return emit

        def col_scores(s, st, h, blocks):
            def emit(e):
                for j in blocks:
                    n = T - P * j
                    at = at_of[n]
                    o = flat(s)
                    e.matmul(o[:, at:at + n], st["k"].view[0:NEG + 2, h, j * P:(j + 1) * P],
                             st["q"].view[0:NEG + 2, h, j * P:T], start=True, stop=False, skip_group_check=True)
                    last = e.matmul(o[:, at:at + P], ident16[:, :], causal[:, 1, :], start=False, stop=True,
                                    skip_group_check=True)
                return last
            return emit

        views = {"row": row_scores, "col": col_scores,
                 "maxima": lambda s, blocks: [(i, flat(s)[:, at_of[P * (i + 1)]:at_of[P * (i + 1)] + P * (i + 1)])
                                              for i in blocks],
                 "used": lambda s: flat(s)[:, 0:1280]}

        def pv_blocks(blocks):
            return [(j, slice(j * P, T), slice(at_of[T - j * P], at_of[T - j * P] + T - j * P)) for j in blocks]

        xs_free, xs_ready, side = [], {}, [dense_weights()]

        def finish(n, ctx, m):
            b, f = divmod(n, DT)
            yield
            if f == 0:
                drain(side)
            ctx.freed = split(ctx.view[:, :], xs[0][:, f, :], xs[1][:, f, :], m, xs_free)
            xs_ready.setdefault(b, []).append(ctx.freed)
            if f == DT - 1:
                side.append(dense(b))

        def dense(b):
            for f in range(DT):
                yield
                both = []
                for w, w_ready in ((wdl, wd_ready[LEXP]), (wdv, wd_ready[VEXP])):
                    k = outs.take()
                    pairs = [(T_(w, every, t, slice(f * P, (f + 1) * P)), T_(xs, every, t, every)) for t in range(DT)]
                    both.append((k, pe.do(gemm(k.view, products(pairs)), xs_ready[b], w_ready, k.freed)))
                (kl, ml), (kv, mv) = both
                s = xe.take()
                m = pick(s.view[:, :], picked[:, VEXP, b, :], kl, ml, kv, mv, s.freed)
                h_ready[b] = dve.do(lambda e: e.tensor_tensor(hT[:, b, f, :], hT[:, b, f, :], s.view[:, :], ALU.add),
                                    m, h_ready[b])
                s.freed = [h_ready[b]]
            xs_free[:] = [mv]

        attention(B * DT, GH, sets, outs, outs, bufs, load_group, [range(TT)], [range(TT)],
                  SELF_SCALE, views, NEG, pv_blocks, 1, finish, side, lag=2, group_slots=3,
                  rows_by=lambda n: n + GH + 3)
        barrier()

    with ExitStack() as ph:
        NEG = 4 * CHD + 32
        q_ring = Ring([Slot(stack(ph, f"xq{i}", T, P)) for i in range(2)])
        k_ring = Ring([Slot(stack(ph, f"xk{i}", M, P)) for i in range(2)])
        for r_, n_ in ((q_ring, "xq"), (k_ring, "xk")):
            for i, s in enumerate(r_.slots):
                s.ports = [port(f"{n_}{i}_{j}_dma") for j in range(4)]
        VW = 6 * CHD
        VEND = MT * 4 * VW
        v_ring = Ring([Slot(alloc(ph, f"xv{i}", [P, VEND + 2 * CHD], F32R)) for i in range(3)])
        v_rows = ring(ph, "xv_rows", 2, [P, MT, 4 * CHD], dma=True)
        for k, q in zip(k_ring.slots, q_ring.slots):
            k.pads = [on_pool(lambda e: e.memset(f32(k.view[64:96, :, :]), 0.0)),
                      on_pool(lambda e: e.memset(f32(k.view[96:P, :, :]), 1.0))]
            q.pads = [on_pool(lambda e: e.memset(f32(q.view[64:P, :, :]), 0.0))]
        for vs in v_ring.slots:
            z = on_pool(lambda e: e.memset(f32(vs.view[:, :]), 0.0))
            vs.freed = [on_pool(lambda e: e.memset(f32(vs.view[:, 0:VEND]).rearrange(
                "p (n w) -> p n w", w=2 * VW)[:, :, o * VW + (4 + o) * CHD:o * VW + (5 + o) * CHD], 1.0), z)
                for o in range(2)]

        with ExitStack() as mid:
            wcq = pair(mid, "wcq", [P, DT, CC])
            staging = ring(mid, "cq_stage", 4, [P, CC], dma=True)
            nb = norm_buffers(mid, "n2", n=B)
            tmp = ring(mid, "cn_tmp", 4, [P, T])
            cns = Ring([Slot(pair(mid, f"cn{i}", [P, DT, T])) for i in range(2)])
            q_out = Ring([Slot(pair(mid, f"cq{i}", [P, T]), port(f"cq{i}_dma")) for i in range(2)])
            banks = bank_ring(0, 8)
            sums = [square_sum(hT[:, b, :, :], nb, h_ready[b]) for b in range(B)]
            wcq_ready = load_split(wcq, DT, lambda i: (P, ins["cq_w"][i * P:(i + 1) * P, :]), staging, CC)
            rstds = [norm_rstd(*sums[b], banks) for b in range(B)]

            def take_norm(b):
                cn = cns.take()
                ms = normalised([(hT[:, b, t, :], 2, t, cn.view[0][:, t, :], cn.view[1][:, t, :], cn.freed)
                                 for t in range(DT)], tmp, *rstds[b])
                return cn, ms

            following = take_norm(0)
            for b in range(B):
                cn, ms = following
                projected = []
                for i in range(ET):
                    k = banks.take()
                    m = pe.do(gemm(k.view, products([(T_(wcq, every, t, slice(i * P, i * P + P)),
                                                      T_(cn.view, every, t, every)) for t in range(DT)])),
                              ms, wcq_ready, k.freed)
                    projected.append((k, m))
                cn.freed = [m]
                if b + 1 < B:
                    following = take_norm(b + 1)
                for i, (k, m) in enumerate(projected):
                    s = q_out.take()
                    k.freed = split(k.view, s.view[0][:, :], s.view[1][:, :], m, s.freed)
                    sp.dma(s.port, cross_q[b, i, 0, :, :], f32(s.view[0][:, :]), k.freed)
                    s.freed = [sp.dma(s.port, cross_q[b, i, 1, :, :], f32(s.view[1][:, :]))]
            barrier()

        wcd = pair(ph, "wcd", [P, ET, D])
        bufs = {"max": ring(ph, "xmax", 2, [P, 4 * TT]),
                "neg": Ring([Slot(pair(ph, f"xneg{i}", [4 * TT, P]), port(f"xneg{i}_dma")) for i in range(2)]),
                "probs": ring(ph, "xprobs", 3, [P, 1024]),
                "probs_hl": Ring([Slot(pair(ph, f"xprobs_hl{i}", [P, 1024])) for i in range(4)]),
                "sums": ring(ph, "xsums", 1, [P, T]), "low": ring(ph, "xlow", 1, [P, T]),
                "ctx": ring(ph, "xctx", 2, [P, T])}
        cs = pair(ph, "cctx", [P, ET, T])
        staging = ring(ph, "cd_stage", 2, [P, D], dma=True)
        wcd_ready = load_split(wcd, ET, lambda i: (P, ins["cdense_w"][i * P:(i + 1) * P, :]), staging, D)
        sets = bank_ring(0, 3, 2)
        accs, outs = bank_ring(6, 1), bank_ring(7, 1)
        GPT = P // (4 * CHD)
        state = {}

        def load_group(g):
            b, i = divmod(g, NH // 4)
            f, part0 = i // GPT, (i % GPT) * 4 * CHD
            q, k = q_ring.take(), k_ring.take()
            ms = []
            for s, dram, order in ((q, cross_q, (0, 1, 0, 1)), (k, cross_k, (0, 0, 1, 1))):
                for j, hl in enumerate(order):
                    src = dram[b, f, hl, part0:part0 + 4 * CHD, :].rearrange("(h r) t -> r h t", h=4)
                    ms.append(sp.dma(s.ports[j], f32(s.view[j * CHD:(j + 1) * CHD, :, :]), src, s.freed))
            vs, v_ready = v_ring.take(), []
            r_ = v_rows.take()
            m_in = sp.dma(r_.port, r_.view[:, :, :], cross_v[b, :, :, i * 4 * CHD:(i + 1) * 4 * CHD].rearrange(
                "t p w -> p t w"), r_.freed)

            def spread():
                for a in range(4):
                    yield
                    at = a * VW + a % 2 * CHD
                    hi, lo = (vs.view[:, 0:VEND].rearrange("p (t n) -> p t n", t=MT)[
                        :, :, at + k * 2 * CHD:at + k * 2 * CHD + CHD] for k in range(2))
                    raw = r_.view[:, :, a * CHD:(a + 1) * CHD]
                    m = on_pool(lambda e: e.tensor_copy(hi, raw), m_in, vs.freed)
                    v_ready.append(on_pool(lambda e: e.tensor_tensor(lo, raw, f32(hi), ALU.subtract), m))
                r_.freed = v_ready[-1:]

            def v_lhs(h, t):
                at = (t * 4 + h) * VW
                return vs.view[:, at:at + P]

            def v_done(m):
                vs.freed = [m]
            return {"q": q, "k": k, "loaded": ms + q.pads + k.pads, "v_lhs": v_lhs, "v_ready": v_ready,
                    "v_done": v_done, "spread": spread()}

        def row_scores(s, st, h, blocks):
            (i,) = blocks

            def emit(e):
                for half in range(2):
                    last = e.matmul(s.view[:, half, :], st["q"].view[0:NEG, h, i * P:(i + 1) * P],
                                    st["k"].view[0:NEG, h, half * BANK:(half + 1) * BANK], start=True, stop=True)
                return last
            return emit

        def col_scores(s, st, h, blocks):
            def emit(e):
                for n, j in enumerate(blocks):
                    last = e.matmul(s.view[:, n, :], st["k"].view[0:NEG + 2, h, j * P:(j + 1) * P],
                                    st["q"].view[0:NEG + 2, h, :], start=True, stop=True)
                return last
            return emit

        views = {"row": row_scores, "col": col_scores,
                 "maxima": lambda s, blocks: [(blocks[0], s.view.rearrange("p a n -> p (a n)"))],
                 "used": lambda s: s.view.rearrange("p a n -> p (a n)")}

        def pv_blocks(blocks):
            return [(j, slice(0, T), slice(n * BANK, (n + 1) * BANK)) for n, j in enumerate(blocks)]

        side, cs_free, cs_ready = [], [], {}

        def finish(n, ctx, m):
            b, f = divmod(n, ET)
            yield
            if f == 0:
                drain(side)
            ctx.freed = split(ctx.view[:, :], cs[0][:, f, :], cs[1][:, f, :], m, cs_free)
            cs_ready.setdefault(b, []).append(ctx.freed)
            if f == ET - 1:
                side.append(dense(b))

        def dense(b):
            for f in range(DT):
                yield
                k = outs.take()
                m = pe.do(gemm(k.view, products([(T_(wcd, every, t, slice(f * P, f * P + P)), T_(cs, every, t, every))
                                                 for t in range(ET)])), cs_ready[b], wcd_ready, k.freed)
                h_ready[b] = dve.do(lambda e: e.tensor_tensor(hT[:, b, f, :], hT[:, b, f, :], k.view, ALU.add),
                                    m, h_ready[b])
                k.freed = [h_ready[b]]
            cs_free[:] = [m]

        def rows_by(n):
            g, unit = divmod(n, 4 * TT)
            return 4 * TT * (g + 1) + max(0, min(4 * TT, -(-(unit + 1 - 2) * 4 * TT // (4 * TT - 6))))

        attention(B * NH // 4, 4, sets, accs, outs, bufs, load_group, [(i,) for i in range(TT)],
                  [(2 * j, 2 * j + 1) for j in range(MT // 2)], CROSS_SCALE, views,
                  NEG, pv_blocks, 2, finish, side, lag=3, group_slots=2, rows_by=rows_by,
                  split_probs=384)
        barrier()

    with ExitStack() as ph:
        IT = -(-I // P)
        xn = pair(ph, "mn", [P, B * DT, T])
        tmp = ring(ph, "mtmp", 2, [P, T])
        nb = norm_buffers(ph, "n3", 1)
        up_w = [pair(ph, f"up_w{i}", [P, 2 * DT, P]) for i in range(3)]
        down_w = [pair(ph, f"down_w{i}", [P, D]) for i in range(3)]
        up_stage = [alloc(ph, f"up_stage{i}", [P, DT, P]) for i in range(4)]
        down_stage = [alloc(ph, f"down_stage{i}", [P, D]) for i in range(2)]
        silu = [alloc(ph, f"silu{i}", [P, T]) for i in range(2)]
        hid = [pair(ph, f"hid{i}", [P, T]) for i in range(2)]

        def slots(views, name=None):
            return Ring([Slot(v, port(f"{name}{i}_dma") if name else None) for i, v in enumerate(views)])

        def mlp(name, gate, up, down, units, before):
            ups, downs, acts, hids = slots(up_w), slots(down_w), slots(silu), slots(hid)
            up_in, down_in = slots(up_stage, f"{name}_up"), slots(down_stage, f"{name}_down")
            gu_banks, o_banks = bank_ring(0, 4), bank_ring(4, 4)
            h_mark = [None] * len(units)

            def fetch(i):
                n = min(P, I - i * P)
                got = []
                for w in (gate, up):
                    s = up_in.take()
                    src = ins[w].rearrange("(t p) i -> p t i", p=P)[:, :, i * P:i * P + n]
                    got.append((s, sp.dma(s.port, s.view[:, :, 0:n], src, s.freed)))
                s = down_in.take()
                got.append((s, sp.dma(s.port, s.view[0:n, :], ins[down][i * P:i * P + n, :], s.freed)))
                return n, got

            def prepare(n, got):
                u, d = ups.take(), downs.take()
                for j, (s, m) in enumerate(got[:2]):
                    s.freed = split(s.view[:, :, 0:n], u.view[0][:, j * DT:(j + 1) * DT, 0:n],
                                    u.view[1][:, j * DT:(j + 1) * DT, 0:n], m, u.freed)
                s, m = got[2]
                s.freed = split(s.view[0:n, :], d.view[0][0:n, :], d.view[1][0:n, :], m, d.freed)
                return n, u, d, [got[0][0].freed, got[1][0].freed], s.freed

            def hidden(j, tile):
                n, u, d, u_ready, d_ready = tile
                x, h, mask, ready = units[j]
                done = []
                for part in range(2):
                    k = gu_banks.take()
                    m = pe.do(gemm(k.view[0:n, :], products([(T_(u.view, every, part * DT + t, slice(0, n)), x(t))
                                                             for t in range(DT)])), ready(), u_ready, k.freed)
                    done.append((k, m))
                u.freed = [m]
                (kg, mg), (ku, mu) = done
                a, hd = acts.take(), hids.take()
                m = act.do(lambda e: e.activation(a.view[0:n, :], kg.view[0:n, :], ACT.Silu), mg, a.freed)
                kg.freed = [m]
                m = dve.do(lambda e: e.tensor_tensor(a.view[0:n, :], ku.view[0:n, :], a.view[0:n, :], ALU.mult), m, mu)
                ku.freed = [m]
                masked = shaped(a.view, mask(n))
                m = dve.do(lambda e: e.tensor_tensor(masked, masked, mask(n), ALU.mult), m)
                a.freed = split(a.view[0:n, :], hd.view[0][0:n, :], hd.view[1][0:n, :], m, hd.freed)
                return hd, a.freed

            def shaped(view, like):
                rows = view[0:like.shape[0], :]
                return rows.rearrange("p (b n) -> p b n", b=like.shape[1]) if len(like.shape) == 3 else rows

            def down_product(j, tile, hd, ready):
                n, u, d, u_ready, d_ready = tile
                h = units[j][1]
                for f in range(DT):
                    k = o_banks.take()
                    fcols = slice(f * P, (f + 1) * P)
                    m = pe.do(gemm(k.view, products([((d.view[0][0:n, fcols], d.view[1][0:n, fcols]),
                                                      (hd.view[0][0:n, :], hd.view[1][0:n, :]))])),
                              ready, d_ready, k.freed)
                    h_mark[j] = dve.do(lambda e: e.tensor_tensor(h(f), h(f), shaped(k.view, h(f)), ALU.add), m, h_mark[j])
                    k.freed = [h_mark[j]]
                hd.freed = d.freed = [m]

            pend, split_tiles, fetched = None, [], []

            def advance(i):
                while len(split_tiles) < min(IT, i + 1):
                    split_tiles.append(prepare(*fetched.pop(0)))
                    if len(split_tiles) + len(fetched) < IT:
                        fetched.append(fetch(len(split_tiles) + len(fetched)))

            fetched += [fetch(i) for i in range(2)]
            before(0, -1, gu_banks)
            advance(0)
            for i in range(IT):
                for j in range(len(units)):
                    before(i, j, gu_banks)
                    now = (j, split_tiles[i], *hidden(j, split_tiles[i]))
                    if pend:
                        down_product(*pend)
                    pend = now
                    if j == min(1, len(units) - 1):
                        advance(i + 2)
            down_product(*pend)

        xn_ready = {}

        def norm_ahead(i, j, banks):
            b = j + 2 if j >= 0 else 0
            if i == 0 and b < B and b not in xn_ready:
                for b in ((0, 1) if b == 0 else (b,)):
                    r, rm = norm_rstd(*square_sum(hT[:, b, :, :], nb, h_ready[b]), banks)
                    xn_ready[b] = normalised([(hT[:, b, t, :], 3, t, xn[0][:, b * DT + t, :],
                                               xn[1][:, b * DT + t, :], None) for t in range(DT)], tmp, r, rm)

        mlp("l", "l_gate", "l_up", "l_down",
            [(lambda t, b=b: T_(xn, every, b * DT + t, every), lambda f, b=b: hT[:, b, f, :],
              lambda n, b=b: picked[0:n, LEXP, b, :], lambda b=b: xn_ready[b]) for b in range(B)],
            norm_ahead)
        barrier()
        for s in range(TT):
            tokens = slice(s * P, (s + 1) * P)
            flag = nc.values_load(has_v[0:1, s:s + 1], min_val=0, max_val=1)
            with nc.If(flag == 1):
                outside = pe, act, dve, sp, all_ports
                pe, act, dve, sp = (Lane(x.engine, sem(f"v{s}_{n}_done"))
                                    for x, n in ((pe, "pe"), (act, "act"), (dve, "dve"), (sp, "sp")))
                all_ports = []
                by_batch = [part.rearrange("p (b t) n -> p b t n", t=DT) for part in (xn[0][:, :, :], xn[1][:, :, :])]
                mlp(f"v{s}", "v_gate", "v_up", "v_down",
                    [(lambda t: tuple(part[:, :, t, tokens] for part in by_batch), lambda f: hT[:, :, f, tokens],
                      lambda n: picked[0:n, VEXP, :, tokens], lambda: None)],
                    lambda i, j, banks: None)
                ends = [(x.sem, x.count) for x in (pe, act, dve, sp) if x.count] + [(p.sem, p.count) for p in all_ports]
                for x in (pe, act, dve, sp):
                    x.wait(ends)
                pe, act, dve, sp, all_ports = outside
            for b in range(B):
                stores.append(sp.dma(port(f"out{s}_{b}_dma"), out[b].rearrange("(t p) n -> p t n", p=P)[:, :, tokens],
                                     hT[:, b, :, tokens]))
        sp.wait(stores)

    top.close()


_NAMES = {"ctx": "ctx_1024", "pos": "pos_1xS", "mask": "mask_BxS_ik0"}
_NAMES.update({n: "L0_xattn_" + n for n in ("W_mem", "W_gate", "b_gate", "norm_w")})
_NAMES.update({n: "L1_xattn_" + n for n in (
    "ln_in_w", "ln_post_attn_w", "ln_post_cross_w", "v_qkv", "l_qkv", "v_dense", "l_dense", "cq_w", "ckv_w",
    "cdense_w", "v_gate", "v_up", "v_down", "l_gate", "l_up", "l_down")})
_TURNED = {"xT": "x", "ctxT": "ctx_1024", "W_memT": "L0_xattn_W_mem", "W_gateT": "L0_xattn_W_gate"}


def constants(T, D, NH):
    import numpy as np

    HD = D // NH
    inv = (1.0 / 10000.0 ** (np.arange(0, HD, 2, dtype=np.float32) / np.float32(HD))).astype(np.float32)
    angle = np.outer(np.arange(T, dtype=np.float32), inv).astype(np.float32)
    angle = np.tile(angle, (1, 2 * P // HD))
    rope = np.stack([np.cos(angle), np.sin(angle)]).astype(np.float32)
    turn = np.zeros((P, P), np.float32)
    for j in range(P):
        half = j % HD < HD // 2
        turn[j + HD // 2 if half else j - HD // 2, j] = -1.0 if half else 1.0
    at = np.arange(P)
    low = np.where(at[None, :] > at[:, None], -1e38, 0.0)
    return {
        "ident": np.eye(P, dtype=np.float32), "mean_w": np.full((P, P), 1.0 / D, np.float32),
        "causal": np.stack([low, low.T], axis=1).astype(np.float32),
        "rope": rope, "turn": turn,
        "row_no": (np.arange(T // P)[None, :] * P + at[:, None]).astype(np.float32),
    }


def kernel(**inputs):
    import numpy as np
    import concourse.bacc as bacc
    from concourse.bass_utils import run_bass_kernel_spmd

    nc = bacc.Bacc("TRN2", target_bir_lowering=False, num_devices=1)
    arrays, ins, const = {}, {}, {}
    for name, full in _NAMES.items():
        a = np.asarray(inputs[full])
        if a.ndim == 1:
            a = a.reshape(-1, P).T
        arrays[name] = np.ascontiguousarray(a)
    for name, full in _TURNED.items():
        arrays[name] = np.ascontiguousarray(np.swapaxes(np.asarray(inputs[full]), -1, -2))
    arrays["mask_cols"] = np.ascontiguousarray(arrays["mask"].reshape(-1, P).T)
    B, D, T = arrays["xT"].shape
    M, E = arrays["ctx"].shape[1:]
    dims = dict(B=B, T=T, D=D, E=E, M=M, NH=16, I=arrays["v_gate"].shape[1])
    for views, of, suffix in ((ins, dict(arrays), "_dram"), (const, constants(T, D, dims["NH"]), "_const")):
        for name, a in of.items():
            arrays.pop(name, None)
            arrays[name + suffix] = a
            views[name] = nc.dram_tensor(name + suffix, a.shape, mybir.dt.from_np(a.dtype),
                                         kind="ExternalInput").ap()
    out = nc.dram_tensor("out_dram", (B, D, T), F32, kind="ExternalOutput").ap()
    xattn_block(nc, dims, ins, const, out)
    r = run_bass_kernel_spmd(nc, [arrays], core_ids=[0])
    return np.ascontiguousarray(np.swapaxes(r.results[0]["out_dram"], -1, -2))
```
